# Optimizing a Trainium2 kernel written in Bass

```python
import numpy as np
import jax
import jax.numpy as jnp

def _softmax(x, axis=-1):
    return jax.nn.softmax(x, axis=axis)

def _gelu(x):
    return jax.nn.gelu(x, approximate=True)

def _silu(x):
    return jax.nn.silu(x)

def _sigmoid(x):
    return jax.nn.sigmoid(x)

def _layernorm(x, axis=-1, eps=1e-05):
    m = jnp.mean(x, axis=axis, keepdims=True)
    v = jnp.var(x, axis=axis, keepdims=True)
    return (x - m) / jnp.sqrt(v + eps)

def _scatter_add(tgt, idx, src, axis=0):
    return tgt.at[idx].add(src)

def _segment_sum(src, seg, n):
    return jax.ops.segment_sum(src, seg, n)
kernel_name = 'mk_perceiver_d2_seqx_r4_b5380e'

def setup_inputs(seed: int=0):
    np.random.seed(seed)
    _w = jnp.asarray

    def _rec_inputs():
        import jax
        import jax.numpy as jnp
        _rk = jax.random.key(seed)
        x = -0.0003929 + 0.9999 * jax.random.normal(jax.random.fold_in(_rk, 1), (8, 64, 256), jnp.float32)
        _lenS = 64 - jax.random.randint(jax.random.fold_in(_rk, 7), (8,), 0, max(1, 64 // 4) + 1, jnp.int32)
        _lenS2 = 1601 - jax.random.randint(jax.random.fold_in(_rk, 8), (8,), 0, max(1, 1601 // 4) + 1, jnp.int32)
        _ctx_1024P = jax.random.normal(jax.random.fold_in(_rk, 11), (8, 16, 256), jnp.float32)
        _ctx_1024c = jax.random.dirichlet(jax.random.fold_in(_rk, 511), 0.3 * jnp.ones((16,), jnp.float32), (8, 1601))
        _ctx_1024t = jnp.einsum('bsk,bkd->bsd', _ctx_1024c, _ctx_1024P)
        _ctx_1024t = _ctx_1024t * jax.lax.rsqrt(jnp.mean(jnp.square(_ctx_1024t)) + 1e-12) * 0.953939
        ctx_1024 = 2.81802e-05 + 1.00001 * (_ctx_1024t + 0.3 * jax.random.normal(jax.random.fold_in(_rk, 611), (8, 1601, 256), jnp.float32))
        fside_1xSxS2_0 = 0.000675642 + 1.00031 * jax.random.normal(jax.random.fold_in(_rk, 12), (1, 64, 1601), jnp.float32)
        return (x, ctx_1024, fside_1xSxS2_0)
    x, ctx_1024, fside_1xSxS2_0 = _rec_inputs()

    def _L0_xattn_setup():
        import jax, jax.numpy as jnp
        import numpy as np
        import math
        D = 256
        B, S = (8, 512)

        def _proj(x, W1, b1, W2, b2):
            h = jnp.einsum('bsd,od->bso', x, W1) + b1
            return jnp.einsum('bsd,od->bso', h, W2) + b2
        key = jax.random.key(seed)
        ks = jax.random.split(key, 8)
        q = jax.random.normal(ks[0], (B, S, D), dtype=jnp.float32)
        k = jax.random.normal(ks[1], (B, S, D), dtype=jnp.float32)
        v1 = jax.random.normal(ks[2], (B, S, D), dtype=jnp.float32)
        mask = jax.random.normal(ks[3], (1, S, S), dtype=jnp.float32)
        lim = 1.0 / math.sqrt(D)
        W1 = jax.random.uniform(ks[4], (D, D), jnp.float32, -lim, lim)
        b1 = jax.random.uniform(ks[5], (D,), jnp.float32, -lim, lim)
        W2 = jax.random.uniform(ks[6], (D, D), jnp.float32, -lim, lim)
        b2 = jax.random.uniform(ks[7], (D,), jnp.float32, -lim, lim)
        return {'q': q, 'k': k, 'v1': v1, 'mask': mask, 'W1': W1, 'b1': b1, 'W2': W2, 'b2': b2}
    _L0_xattn_all = _L0_xattn_setup()
    _L0_xattn_in = {k: v for k, v in _L0_xattn_all.items() if k in ('W1', 'b1', 'W2', 'b2')}
    del _L0_xattn_all

    def _L0_attn_setup():
        import jax, jax.numpy as jnp
        import numpy as np
        HIDDEN = 256
        NHEADS = 16
        HEAD_DIM = HIDDEN // NHEADS
        CONV_K = 4
        EPS = 1e-06

        def _short_conv(x, w):
            K = w.shape[-1]
            L = x.shape[1]
            xp = jnp.pad(x, ((0, 0), (K - 1, 0), (0, 0)))
            y = jnp.zeros_like(x)
            for k in range(K):
                y = y + xp[:, k:k + L, :] * w[:, k]
            return y

        def _l2norm(x):
            n = jnp.sqrt(jnp.sum(x * x, axis=-1, keepdims=True))
            return x / jnp.maximum(n, EPS)

        def _delta_rule(q, k, v, beta):
            b, h, l, dk = q.shape
            dv = v.shape[-1]
            q = q * dk ** (-0.5)
            S0 = jnp.zeros((b, h, dk, dv), dtype=v.dtype)

            def step(S, inp):
                q_t, k_t, v_t, b_t = inp
                v_new = (v_t - jnp.einsum('bhd,bhdm->bhm', k_t, S)) * b_t[..., None]
                S = S + jnp.einsum('bhd,bhm->bhdm', k_t, v_new)
                o_t = jnp.einsum('bhd,bhdm->bhm', q_t, S)
                return (S, o_t)
            ql, kl, vl = (t.transpose(2, 0, 1, 3) for t in (q, k, v))
            bl = beta.transpose(2, 0, 1)
            S, o = jax.lax.scan(step, S0, (ql, kl, vl, bl))
            return (o.transpose(1, 2, 0, 3), S)

        def _reference_tuple_inner(x, Wq, Wk, Wv, Wb, Wo, conv_q, conv_k, conv_v, o_norm_w):
            b, l, _ = x.shape
            q = x @ Wq.T
            k = x @ Wk.T
            v = x @ Wv.T
            beta = jax.nn.sigmoid(x @ Wb.T)
            q = jax.nn.silu(_short_conv(q, conv_q))
            k = jax.nn.silu(_short_conv(k, conv_k))
            v = jax.nn.silu(_short_conv(v, conv_v))

            def to_heads(t):
                return t.reshape(b, l, NHEADS, HEAD_DIM).transpose(0, 2, 1, 3)
            q, k, v = (to_heads(q), to_heads(k), to_heads(v))
            beta = beta.transpose(0, 2, 1)
            q = _l2norm(q)
            k = _l2norm(k)
            o, S = _delta_rule(q, k, v, beta)
            o = o * jax.lax.rsqrt(jnp.mean(o * o, axis=-1, keepdims=True) + EPS) * o_norm_w
            out = o.transpose(0, 2, 1, 3).reshape(b, l, HIDDEN) @ Wo.T
            return (out, S)
        key = jax.random.key(seed)
        ks = jax.random.split(key, 10)
        b, l = (4, 256)
        init = 0.02
        return {'x': jax.random.normal(ks[0], (b, l, HIDDEN), dtype=jnp.float32), 'Wq': jax.random.normal(ks[1], (HIDDEN, HIDDEN), dtype=jnp.float32) * init, 'Wk': jax.random.normal(ks[2], (HIDDEN, HIDDEN), dtype=jnp.float32) * init, 'Wv': jax.random.normal(ks[3], (HIDDEN, HIDDEN), dtype=jnp.float32) * init, 'Wb': jax.random.normal(ks[4], (NHEADS, HIDDEN), dtype=jnp.float32) * init, 'Wo': jax.random.normal(ks[5], (HIDDEN, HIDDEN), dtype=jnp.float32) * init, 'conv_q': jax.random.normal(ks[6], (HIDDEN, CONV_K), dtype=jnp.float32) * 0.3, 'conv_k': jax.random.normal(ks[7], (HIDDEN, CONV_K), dtype=jnp.float32) * 0.3, 'conv_v': jax.random.normal(ks[8], (HIDDEN, CONV_K), dtype=jnp.float32) * 0.3, 'o_norm_w': jnp.ones((HEAD_DIM,), dtype=jnp.float32)}
    _L0_attn_all = _L0_attn_setup()
    _L0_attn_in = {k: v for k, v in _L0_attn_all.items() if k in ('Wq', 'Wk', 'Wv', 'Wb', 'Wo', 'conv_q', 'conv_k', 'conv_v', 'o_norm_w')}
    del _L0_attn_all

    def _L0_ffn_setup():
        import jax, jax.numpy as jnp
        import numpy as np
        B, S, D = (2, 128, 256)
        E, K, I = (16, 8, 256)
        I_SH = 256
        ROUTE_SCALE = 2.826
        key = jax.random.key(seed)
        ks = jax.random.split(key, 8)
        s = 0.02
        return {'x': jax.random.normal(ks[0], (B, S, D), dtype=jnp.float32), 'gate_w': jax.random.normal(ks[1], (E, D), dtype=jnp.float32) * s, 'expert_bias': jnp.zeros((E,), dtype=jnp.float32), 'w_gate': jax.random.normal(ks[2], (E, I, D), dtype=jnp.float32) * s, 'w_up': jax.random.normal(ks[3], (E, I, D), dtype=jnp.float32) * s, 'w_down': jax.random.normal(ks[4], (E, D, I), dtype=jnp.float32) * s, 'shared_gate_w': jax.random.normal(ks[5], (I_SH, D), dtype=jnp.float32) * s, 'shared_up_w': jax.random.normal(ks[6], (I_SH, D), dtype=jnp.float32) * s, 'shared_down_w': jax.random.normal(ks[7], (D, I_SH), dtype=jnp.float32) * s}
    _L0_ffn_all = _L0_ffn_setup()
    _L0_ffn_in = {k: v for k, v in _L0_ffn_all.items() if k in ('gate_w', 'expert_bias', 'w_gate', 'w_up', 'w_down', 'shared_gate_w', 'shared_up_w', 'shared_down_w')}
    del _L0_ffn_all

    def _L1_xattn_setup():
        import jax, jax.numpy as jnp
        import numpy as np
        B, L_ENC, L_DEC, D = (16, 128, 128, 256)
        key = jax.random.key(seed)
        k1, k2, k3, k4, k5, k6 = jax.random.split(key, 6)
        encoder_hc = jax.random.normal(k1, (B, L_ENC, D), dtype=jnp.float32)
        decoder_hq = jax.random.normal(k2, (B, L_DEC, D), dtype=jnp.float32)
        w_sim = jax.random.normal(k3, (3 * D,), dtype=jnp.float32) * 0.02
        b_sim = jax.random.normal(k4, (1,), dtype=jnp.float32) * 0.02
        W_qv = jax.random.normal(k5, (4 * D, D), dtype=jnp.float32) * 0.02
        b_qv = jax.random.normal(k6, (D,), dtype=jnp.float32) * 0.02
        return {'encoder_hc': encoder_hc, 'decoder_hq': decoder_hq, 'w_sim': w_sim, 'b_sim': b_sim, 'W_qv': W_qv, 'b_qv': b_qv}
    _L1_xattn_all = _L1_xattn_setup()
    _L1_xattn_in = {k: v for k, v in _L1_xattn_all.items() if k in ('w_sim', 'b_sim', 'W_qv', 'b_qv')}
    del _L1_xattn_all

    def _L1_attn_setup():
        import jax, jax.numpy as jnp
        import numpy as np
        INDIM = 256
        NHEADS = 16
        DK = INDIM // NHEADS
        DV = INDIM // NHEADS
        B, S = (4, 512)
        key = jax.random.key(seed)
        ks = jax.random.split(key, 5)
        x = jax.random.normal(ks[0], (B, S, INDIM), dtype=jnp.float32)
        std_qk = np.sqrt(2.0 / (INDIM + DK)).astype(np.float32)
        std_v = np.sqrt(2.0 / (INDIM + DV)).astype(np.float32)
        Wq = jax.random.normal(ks[1], (NHEADS * DK, INDIM), dtype=jnp.float32) * std_qk
        Wk = jax.random.normal(ks[2], (NHEADS * DK, INDIM), dtype=jnp.float32) * std_qk
        Wv = jax.random.normal(ks[3], (NHEADS * DV, INDIM), dtype=jnp.float32) * std_v
        std_o = np.sqrt(2.0 / (NHEADS * DV + INDIM)).astype(np.float32)
        Wo = jax.random.normal(ks[4], (INDIM, NHEADS * DV), dtype=jnp.float32) * std_o
        bq = jnp.zeros((NHEADS * DK,), jnp.float32)
        bk = jnp.zeros((NHEADS * DK,), jnp.float32)
        bv = jnp.zeros((NHEADS * DV,), jnp.float32)
        bo = jnp.zeros((INDIM,), jnp.float32)
        return {'x': x, 'Wq': Wq, 'bq': bq, 'Wk': Wk, 'bk': bk, 'Wv': Wv, 'bv': bv, 'Wo': Wo, 'bo': bo}
    _L1_attn_all = _L1_attn_setup()
    _L1_attn_in = {k: v for k, v in _L1_attn_all.items() if k in ('Wq', 'bq', 'Wk', 'bk', 'Wv', 'bv', 'Wo', 'bo')}
    del _L1_attn_all

    def _L1_ffn_setup():
        import jax, jax.numpy as jnp
        import numpy as np
        D_MODEL, D_FF, N_EXP = (256, 1024, 8)
        key = jax.random.key(seed)
        ks = jax.random.split(key, 8)
        s = lambda fan_in: 1.0 / np.sqrt(fan_in)
        x = jax.random.normal(ks[0], (4, 512, D_MODEL), dtype=jnp.float32)
        Wr = jax.random.uniform(ks[1], (N_EXP, D_MODEL), jnp.float32, -s(D_MODEL), s(D_MODEL))
        br = jax.random.uniform(ks[2], (N_EXP,), jnp.float32, -s(D_MODEL), s(D_MODEL))
        W1 = jax.random.uniform(ks[3], (N_EXP, D_FF, D_MODEL), jnp.float32, -s(D_MODEL), s(D_MODEL))
        b1 = jax.random.uniform(ks[4], (N_EXP, D_FF), jnp.float32, -s(D_MODEL), s(D_MODEL))
        W2 = jax.random.uniform(ks[5], (N_EXP, D_MODEL, D_FF), jnp.float32, -s(D_FF), s(D_FF))
        b2 = jax.random.uniform(ks[6], (N_EXP, D_MODEL), jnp.float32, -s(D_FF), s(D_FF))
        return {'x': x, 'Wr': Wr, 'br': br, 'W1': W1, 'b1': b1, 'W2': W2, 'b2': b2}
    _L1_ffn_all = _L1_ffn_setup()
    _L1_ffn_in = {k: v for k, v in _L1_ffn_all.items() if k in ('Wr', 'br', 'W1', 'b1', 'W2', 'b2')}
    del _L1_ffn_all
    return {'x': x, 'ctx_1024': ctx_1024, 'fside_1xSxS2_0': fside_1xSxS2_0, 'L0_xattn_W1': _L0_xattn_in['W1'], 'L0_xattn_b1': _L0_xattn_in['b1'], 'L0_xattn_W2': _L0_xattn_in['W2'], 'L0_xattn_b2': _L0_xattn_in['b2'], 'L0_attn_Wq': _L0_attn_in['Wq'], 'L0_attn_Wk': _L0_attn_in['Wk'], 'L0_attn_Wv': _L0_attn_in['Wv'], 'L0_attn_Wb': _L0_attn_in['Wb'], 'L0_attn_Wo': _L0_attn_in['Wo'], 'L0_attn_conv_q': _L0_attn_in['conv_q'], 'L0_attn_conv_k': _L0_attn_in['conv_k'], 'L0_attn_conv_v': _L0_attn_in['conv_v'], 'L0_attn_o_norm_w': _L0_attn_in['o_norm_w'], 'L0_ffn_gate_w': _L0_ffn_in['gate_w'], 'L0_ffn_expert_bias': _L0_ffn_in['expert_bias'], 'L0_ffn_w_gate': _L0_ffn_in['w_gate'], 'L0_ffn_w_up': _L0_ffn_in['w_up'], 'L0_ffn_w_down': _L0_ffn_in['w_down'], 'L0_ffn_shared_gate_w': _L0_ffn_in['shared_gate_w'], 'L0_ffn_shared_up_w': _L0_ffn_in['shared_up_w'], 'L0_ffn_shared_down_w': _L0_ffn_in['shared_down_w'], 'L1_xattn_w_sim': _L1_xattn_in['w_sim'], 'L1_xattn_b_sim': _L1_xattn_in['b_sim'], 'L1_xattn_W_qv': _L1_xattn_in['W_qv'], 'L1_xattn_b_qv': _L1_xattn_in['b_qv'], 'L1_attn_Wq': _L1_attn_in['Wq'], 'L1_attn_bq': _L1_attn_in['bq'], 'L1_attn_Wk': _L1_attn_in['Wk'], 'L1_attn_bk': _L1_attn_in['bk'], 'L1_attn_Wv': _L1_attn_in['Wv'], 'L1_attn_bv': _L1_attn_in['bv'], 'L1_attn_Wo': _L1_attn_in['Wo'], 'L1_attn_bo': _L1_attn_in['bo'], 'L1_ffn_Wr': _L1_ffn_in['Wr'], 'L1_ffn_br': _L1_ffn_in['br'], 'L1_ffn_W1': _L1_ffn_in['W1'], 'L1_ffn_b1': _L1_ffn_in['b1'], 'L1_ffn_W2': _L1_ffn_in['W2'], 'L1_ffn_b2': _L1_ffn_in['b2']}

def reference(x, ctx_1024, fside_1xSxS2_0, L0_xattn_W1, L0_xattn_b1, L0_xattn_W2, L0_xattn_b2, L0_attn_Wq, L0_attn_Wk, L0_attn_Wv, L0_attn_Wb, L0_attn_Wo, L0_attn_conv_q, L0_attn_conv_k, L0_attn_conv_v, L0_attn_o_norm_w, L0_ffn_gate_w, L0_ffn_expert_bias, L0_ffn_w_gate, L0_ffn_w_up, L0_ffn_w_down, L0_ffn_shared_gate_w, L0_ffn_shared_up_w, L0_ffn_shared_down_w, L1_xattn_w_sim, L1_xattn_b_sim, L1_xattn_W_qv, L1_xattn_b_qv, L1_attn_Wq, L1_attn_bq, L1_attn_Wk, L1_attn_bk, L1_attn_Wv, L1_attn_bv, L1_attn_Wo, L1_attn_bo, L1_ffn_Wr, L1_ffn_br, L1_ffn_W1, L1_ffn_b1, L1_ffn_W2, L1_ffn_b2):
    import jax
    import jax.numpy as jnp

    def _L0_xattn_ref(q, k, v1, mask, W1, b1, W2, b2):
        import jax, jax.numpy as jnp
        import numpy as np
        import math
        D = 256
        B, S = (8, 512)

        def _proj(x, W1, b1, W2, b2):
            h = jnp.einsum('bsd,od->bso', x, W1) + b1
            return jnp.einsum('bsd,od->bso', h, W2) + b2
        qp = _proj(q, W1, b1, W2, b2)
        kp = _proj(k, W1, b1, W2, b2)
        scale = 1.0 / math.sqrt(qp.shape[-1])
        qk = jnp.einsum('bqd,bkd->bqk', qp, kp) * scale
        qk = qk + mask
        attn = jax.nn.softmax(qk, axis=-1)
        return jnp.einsum('bqk,bkd->bqd', attn, v1)

    def _L0_attn_ref(x, Wq, Wk, Wv, Wb, Wo, conv_q, conv_k, conv_v, o_norm_w):
        import jax, jax.numpy as jnp
        import numpy as np
        HIDDEN = 256
        NHEADS = 16
        HEAD_DIM = HIDDEN // NHEADS
        CONV_K = 4
        EPS = 1e-06

        def _short_conv(x, w):
            K = w.shape[-1]
            L = x.shape[1]
            xp = jnp.pad(x, ((0, 0), (K - 1, 0), (0, 0)))
            y = jnp.zeros_like(x)
            for k in range(K):
                y = y + xp[:, k:k + L, :] * w[:, k]
            return y

        def _l2norm(x):
            n = jnp.sqrt(jnp.sum(x * x, axis=-1, keepdims=True))
            return x / jnp.maximum(n, EPS)

        def _delta_rule(q, k, v, beta):
            b, h, l, dk = q.shape
            dv = v.shape[-1]
            q = q * dk ** (-0.5)
            S0 = jnp.zeros((b, h, dk, dv), dtype=v.dtype)

            def step(S, inp):
                q_t, k_t, v_t, b_t = inp
                v_new = (v_t - jnp.einsum('bhd,bhdm->bhm', k_t, S)) * b_t[..., None]
                S = S + jnp.einsum('bhd,bhm->bhdm', k_t, v_new)
                o_t = jnp.einsum('bhd,bhdm->bhm', q_t, S)
                return (S, o_t)
            ql, kl, vl = (t.transpose(2, 0, 1, 3) for t in (q, k, v))
            bl = beta.transpose(2, 0, 1)
            S, o = jax.lax.scan(step, S0, (ql, kl, vl, bl))
            return (o.transpose(1, 2, 0, 3), S)

        def _reference_tuple_inner(x, Wq, Wk, Wv, Wb, Wo, conv_q, conv_k, conv_v, o_norm_w):
            b, l, _ = x.shape
            q = x @ Wq.T
            k = x @ Wk.T
            v = x @ Wv.T
            beta = jax.nn.sigmoid(x @ Wb.T)
            q = jax.nn.silu(_short_conv(q, conv_q))
            k = jax.nn.silu(_short_conv(k, conv_k))
            v = jax.nn.silu(_short_conv(v, conv_v))

            def to_heads(t):
                return t.reshape(b, l, NHEADS, HEAD_DIM).transpose(0, 2, 1, 3)
            q, k, v = (to_heads(q), to_heads(k), to_heads(v))
            beta = beta.transpose(0, 2, 1)
            q = _l2norm(q)
            k = _l2norm(k)
            o, S = _delta_rule(q, k, v, beta)
            o = o * jax.lax.rsqrt(jnp.mean(o * o, axis=-1, keepdims=True) + EPS) * o_norm_w
            out = o.transpose(0, 2, 1, 3).reshape(b, l, HIDDEN) @ Wo.T
            return (out, S)
        return _reference_tuple_inner(x, Wq, Wk, Wv, Wb, Wo, conv_q, conv_k, conv_v, o_norm_w)[0]

    def _L0_ffn_ref(x, gate_w, expert_bias, w_gate, w_up, w_down, shared_gate_w, shared_up_w, shared_down_w):
        import jax, jax.numpy as jnp
        import numpy as np
        B, S, D = (2, 128, 256)
        E, K, I = (16, 8, 256)
        I_SH = 256
        ROUTE_SCALE = 2.826
        gates = jnp.einsum('bsd,ed->bse', x, gate_w)
        scores = jax.nn.sigmoid(gates.astype(jnp.float32))
        sel_scores = scores + expert_bias
        _, inds = jax.lax.top_k(sel_scores, K)
        selected = jnp.take_along_axis(scores, inds, axis=-1)
        selected = selected / selected.sum(axis=-1, keepdims=True)
        selected = selected * ROUTE_SCALE
        onehot = jax.nn.one_hot(inds, E, dtype=selected.dtype)
        combine = jnp.einsum('bske,bsk->bse', onehot, selected)
        hg = jnp.einsum('bsd,eid->bsei', x, w_gate)
        hu = jnp.einsum('bsd,eid->bsei', x, w_up)
        h = jax.nn.silu(hg) * hu
        ye = jnp.einsum('bsei,edi->bsed', h, w_down)
        y = jnp.einsum('bsed,bse->bsd', ye, combine).astype(x.dtype)
        g = jnp.einsum('bsd,id->bsi', x, shared_gate_w)
        u = jnp.einsum('bsd,id->bsi', x, shared_up_w)
        y = y + jnp.einsum('bsi,di->bsd', jax.nn.silu(g) * u, shared_down_w)
        return y

    def _L1_xattn_ref(encoder_hc, decoder_hq, w_sim, b_sim, W_qv, b_qv):
        import jax, jax.numpy as jnp
        import numpy as np
        B, L_ENC, L_DEC, D = (16, 128, 128, 256)
        d = encoder_hc.shape[-1]
        w1, w2, w3 = (w_sim[:d], w_sim[d:2 * d], w_sim[2 * d:])
        Sim = (encoder_hc @ w1)[:, :, None] + (decoder_hq @ w2)[:, None, :] + jnp.einsum('bid,bjd->bij', encoder_hc * w3, decoder_hq) + b_sim[0]
        A = jax.nn.softmax(Sim, axis=2)
        hq_hat = jnp.einsum('bij,bjd->bid', A, decoder_hq)
        Batt = jax.nn.softmax(jnp.max(Sim, axis=2), axis=1)
        hc_bar = jnp.einsum('bi,bid->bd', Batt, encoder_hc)[:, None, :]
        hc_hat = jnp.broadcast_to(hc_bar, encoder_hc.shape)
        feats = jnp.concatenate([encoder_hc, hq_hat, encoder_hc * hq_hat, encoder_hc * hc_hat], axis=-1)
        hcq = feats @ W_qv + b_qv
        return hcq

    def _L1_attn_ref(x, Wq, bq, Wk, bk, Wv, bv, Wo, bo):
        import jax, jax.numpy as jnp
        import numpy as np
        INDIM = 256
        NHEADS = 16
        DK = INDIM // NHEADS
        DV = INDIM // NHEADS
        B, S = (4, 512)
        b, s, _ = x.shape
        q = (x @ Wq.T + bq).reshape(b, s, NHEADS, DK)
        k = (x @ Wk.T + bk).reshape(b, s, NHEADS, DK)
        v = (x @ Wv.T + bv).reshape(b, s, NHEADS, DV)
        w = jnp.einsum('bshd,bzhd->bhsz', q, k)
        w = w / jnp.sqrt(jnp.float32(DV))
        w = jax.nn.softmax(w, axis=-1)
        vw = jnp.einsum('bhsz,bzhd->bshd', w, v)
        vw = vw.reshape(b, s, NHEADS * DV)
        out = vw @ Wo.T + bo
        return out

    def _L1_ffn_ref(x, Wr, br, W1, b1, W2, b2):
        import jax, jax.numpy as jnp
        import numpy as np
        D_MODEL, D_FF, N_EXP = (256, 1024, 8)
        B, S, D = x.shape
        xf = x.reshape(-1, D)
        logits = xf @ Wr.T + br
        expert_idx = jnp.argmax(logits, axis=-1)
        h = jax.nn.relu(jnp.einsum('td,efd->etf', xf, W1) + b1[:, None, :])
        y = jnp.einsum('etf,edf->etd', h, W2) + b2[:, None, :]
        out = y[expert_idx, jnp.arange(xf.shape[0])]
        return out.reshape(B, S, D)
    x = x + _L0_xattn_ref(_layernorm(x, axis=-1), ctx_1024, ctx_1024, fside_1xSxS2_0, L0_xattn_W1, L0_xattn_b1, L0_xattn_W2, L0_xattn_b2)
    x = x + _L0_attn_ref(_layernorm(x, axis=-1), L0_attn_Wq, L0_attn_Wk, L0_attn_Wv, L0_attn_Wb, L0_attn_Wo, L0_attn_conv_q, L0_attn_conv_k, L0_attn_conv_v, L0_attn_o_norm_w)
    x = x + _L0_ffn_ref(_layernorm(x, axis=-1), L0_ffn_gate_w, L0_ffn_expert_bias, L0_ffn_w_gate, L0_ffn_w_up, L0_ffn_w_down, L0_ffn_shared_gate_w, L0_ffn_shared_up_w, L0_ffn_shared_down_w)
    x = x + _L1_xattn_ref(_layernorm(x, axis=-1), ctx_1024, L1_xattn_w_sim, L1_xattn_b_sim, L1_xattn_W_qv, L1_xattn_b_qv)
    x = x + _L1_attn_ref(_layernorm(x, axis=-1), L1_attn_Wq, L1_attn_bq, L1_attn_Wk, L1_attn_bk, L1_attn_Wv, L1_attn_bv, L1_attn_Wo, L1_attn_bo)
    x = x + _L1_ffn_ref(_layernorm(x, axis=-1), L1_ffn_Wr, L1_ffn_br, L1_ffn_W1, L1_ffn_b1, L1_ffn_W2, L1_ffn_b2)
    return x

_drawn_inputs = setup_inputs


def setup_inputs(seed=0):
    import zlib

    import numpy as np

    out = dict(_drawn_inputs(seed))
    spreads = {'L0_attn_o_norm_w': (1.0, 0.2),
     'L0_ffn_expert_bias': (0.0, 0.1),
     'L1_attn_bq': (0.0, 0.1),
     'L1_attn_bk': (0.0, 0.8),
     'L1_attn_bv': (0.0, 0.1),
     'L1_attn_bo': (0.0, 0.1)}
    factors = {'L0_xattn_b1': 8.0,
     'L0_xattn_b2': 6.877,
     'L0_ffn_gate_w': 2.915,
     'L1_ffn_b1': 5.844,
     'L1_ffn_b2': 4.616}
    for name, (base, spread) in spreads.items():
        noise = np.random.default_rng([zlib.crc32(name.encode()), seed]).standard_normal(out[name].shape)
        drawn = base * np.exp(spread * noise) if base else spread * noise
        out[name] = jnp.asarray(drawn.astype(out[name].dtype))
    for name, factor in factors.items():
        out[name] = (out[name] * factor).astype(out[name].dtype)
    return out
```

```python
from contextlib import ExitStack

import concourse.bass as bass
from concourse import mybir

F32 = mybir.dt.float32
ALU = mybir.AluOpType
ACT = mybir.ActivationFunctionType
AX = mybir.AxisListType

P = 128
B, S, D = 8, 64, 256
T = B * S
NT = T // P
DC = D // P
KEYS = 1601
KT = -(-KEYS // P)
BANK = 512
KB4 = -(-KEYS // BANK)
H, HD = 16, 16
HC = H // DC
TAPS = 4
E0 = 16
E1, F1 = 8, 1024
FC = F1 // P
ROUTE = 2.826
SCALE = D ** -0.5
UNROLL = 8
GROUP = 4
STEPS = 6
CUT = -1.0e30

W1T, W2T, W2N, W1N, AK, AV, AQ, AO, SQ, SK, SV, SO = range(12)
C_B1, C_B2, C_CONV, C_ON, C_S1, C_S2, C_S3, C_BQ, C_BK, C_F1 = 0, 2, 4, 28, 30, 32, 34, 36, 38, 40
NCOLS = C_F1 + E1 * FC
R_QV, R_BV, R_BO, R_EB, R_BR, R_SIM = 0, 256, 512, 768, 784, 792
NROWS = 793
N_BETA, N_GATE, N_ROUTE, NNARROW = 0, 16, 32, 40


PAIR = [0, 1, 2, 3, 2, 3, 0, 1]
LOADS = [1, 1, 2, 2, 2, 2, 3, 3]


def keys_of(j, width):
    return min(KEYS, (j + 1) * width) - j * width


def perceiver(nc, x_in, ctx_n, ctx_t, mask_in, w_small, cols_in, rows_in, narrow_in, wqv_in,
              w_ffn0, w_ffn1, b2_in, out, stages):
    with ExitStack() as ctx:
        def sb(name, shape):
            return ctx.enter_context(nc.sbuf_tensor(name, shape, F32))

        def sem(name):
            return ctx.enter_context(nc.semaphore(name))

        X = sb("X", [P, NT, D])
        XN = sb("XN", [P, NT, D])
        XT = sb("XT", [P, DC, T])
        W = sb("W", [P, 12, DC, D])
        cols = sb("cols", [P, NCOLS])
        rows = sb("rows", [P, NROWS])
        narrow = sb("narrow", [P, DC, NNARROW])
        b2e = sb("b2e", [E1, D])
        ident = sb("ident", [P, P])
        eps5 = sb("eps5", [P, 1])
        eps6 = sb("eps6", [P, 1])
        headmask = sb("headmask", [P, HC])
        index = sb("index", [P, NT, E1])
        stats = sb("stats", [P, NT, 6])
        mv = sb("mv", [P, NT, 2])
        std = sb("std", [P, NT])
        big = sb("big", [P, 14336])
        CTX_T = sb("CTX_T", [P, 2, 2, DC, KEYS])
        CTX_N = sb("CTX_N", [P, 2, 2, KT, D])
        ps = ctx.enter_context(nc.psum_tensor("ps", [P, 8, BANK], F32))
        psf = ps[:].rearrange("p b n -> p (b n)")
        scratch = nc.dram_tensor("scratch", [4, B, D, S], F32, kind="Internal").ap()
        scratch_beta = nc.dram_tensor("scratch_beta", [B, H, S], F32, kind="Internal").ap()

        def cut(at, *shape):
            n = 1
            for m in shape:
                n *= m
            v = big[:, at:at + n]
            if len(shape) == 2:
                v = v.rearrange("p (a b) -> p a b", a=shape[0])
            elif len(shape) == 3:
                v = v.rearrange("p (a b c) -> p a b c", a=shape[0], b=shape[1])
            return v

        maskP = cut(0, KEYS)
        prob = [cut(1601, KEYS), cut(3202, KEYS)]
        probT = [cut(4804, KT, P), cut(6468, KT, P)]
        QT = cut(8132, DC, T)
        HA, HB = cut(9156, DC, T), cut(10180, DC, T)
        F3, F4 = cut(9156, DC, T), cut(10180, DC, T)
        HQT = cut(11204, DC, T)
        crow = cut(12228, NT)
        mx = cut(12232, NT)
        nmx = cut(12236, NT)
        den = cut(12240, NT)
        rec = cut(12244, NT)
        batt = cut(12248, P)
        bsum = cut(12376, 2)
        bmask = cut(12378, NT, 2)
        hcb = cut(12386, DC, B)
        hq = cut(12402, D)
        WQV = cut(4804, 2 * NT, D)
        battv = batt.rearrange("p (a b) -> p a b", a=2)
        Y = [[cut(1024 * z + 512 * m, B, S) for m in range(DC)] for z in range(3)]
        raw = [cut(3072 + 1024 * z, HD, S) for z in range(3)]
        KN = cut(6144, S + 1, HD)
        KB = cut(7184, S + 1, HD)
        VB = cut(8224, S + 1, HD)
        QN = cut(9264, S, HD)
        sq = cut(10288, HD, S)
        beta = cut(11312, S)
        ss = cut(11376, S)
        nk = cut(11440, S)
        nega = cut(11504, S + 1)
        qscale = cut(11570, S)
        state = [cut(11634 + 256 * r, HD, HD) for r in range(UNROLL)]
        betaT = big[0:H, 11634:11634 + T]
        kS, outer = cut(3072, HD, HD), cut(3328, HD, HD)
        rsum, wv = cut(3584, HD), cut(3600, HD)
        uu = [cut(3616, HD), cut(3632, HD)]
        O = cut(0, HD, S)
        OS = cut(1024, HD, S)
        OTr = cut(2048, DC, T)
        qS = cut(4096, GROUP * HD, HD)
        tr8, tr4, tr2 = cut(5120, GROUP * HD, 8), cut(5632, GROUP * HD, 4), cut(5888, GROUP * HD, 2)
        W0 = [cut(1536 * r, 3, DC, D) for r in range(4)]
        G = cut(6144, DC, T)
        HT = [cut(7168, DC, T), cut(8192, DC, T)]
        sg, sel, rep = cut(9216, NT, E0), cut(9280, NT, E0), cut(9344, NT, E0)
        top8 = cut(9408, NT, 8)
        csum = cut(9440, NT)
        cw = cut(9444, NT, E0 + 1)
        KM = [cut(0, HC, T), cut(4096, HC, T)]
        QTT = cut(8192, DC, T)
        PA = [cut(9216, H, S), cut(10240, H, S)]
        PAT = [cut(11264, HC, P), cut(12288, HC, P)]
        ON = cut(13312, D)
        OAT = cut(13568, DC, P)
        am, asum = cut(13824, H), cut(13840, H)
        bkm = cut(13856, HC)
        XD = cut(11264, DC, B, 2 * S)
        VM = CTX_N[:].rearrange("p a b c k -> p (a b c k)")[:, 0:B * H * HD].rearrange(
            "p (b h m) -> p b h m", b=B, h=HC)
        HF = cut(0, FC, T)
        lg, oh, eq = cut(4096, NT, E1), cut(4128, NT, E1), cut(4160, NT, E1)
        lmax, lmin = cut(4192, NT), cut(4196, NT)
        ohT = big[0:E1, 4200:4200 + T]
        ctx_tf = CTX_T[:].rearrange("p a b c k -> p (a b c k)")
        WE1 = [ctx_tf[:, 4096 * r:4096 * r + 2048].rearrange("p (c n) -> p c n", c=DC) for r in range(2)]
        WE2 = [ctx_tf[:, 4096 * r + 2048:4096 * r + 4096].rearrange("p (c n) -> p c n", c=FC) for r in range(2)]

        ld_x, ld_w, ld_mask, ld_rest = sem("ld_x"), sem("ld_w"), sem("ld_mask"), sem("ld_rest")
        ld_ct = [sem(f"ld_ct{r}") for r in range(2)]
        ld_cn = [sem(f"ld_cn{r}") for r in range(2)]
        ld_w0 = [sem(f"ld_w0{r}") for r in range(4)]
        ld_we = [sem(f"ld_we{r}") for r in range(2)]
        ld_wqv = sem("ld_wqv")
        consts = sem("consts")
        vec, sca, pol = sem("vec"), sem("sca"), sem("pol")
        ln_stat, ln_std, ln_xn, ln_tr, ln_xt = (sem(n) for n in ("ln_stat", "ln_std", "ln_xn", "ln_tr", "ln_xt"))
        pj_ready, pj_a, pj_v = sem("pj_ready"), sem("pj_a"), sem("pj_v")
        cr_ready, cr_taken = sem("cr_ready"), sem("cr_taken")
        sc_ready, sc_taken = sem("sc_ready"), sem("sc_taken")
        mx_ready, ex_ready, bt_ready = sem("mx_ready"), sem("ex_ready"), sem("bt_ready")
        pt_ready, pt_taken = sem("pt_ready"), sem("pt_taken")
        pv_ready, pv_taken, on_ready, on_taken = (sem(n) for n in ("pv_ready", "pv_taken", "on_ready", "on_taken"))
        xa_done = sem("xa_done")
        small_pe, small_v, small_a = sem("small_pe"), sem("small_v"), sem("small_a")
        ap_ready, conv_done, silu_done = sem("ap_ready"), sem("conv_done"), sem("silu_done")
        first_tap = sem("first_tap")
        y_out = [sem(f"y_out{z}") for z in range(3)]
        y_in = [sem(f"y_in{z}") for z in range(3)]
        b_ready = sem("b_ready")
        b_out, b_in = sem("b_out"), sem("b_in")
        q_sq = sem("q_sq")
        dl_v, dl_a, q_done = sem("dl_v"), sem("dl_a"), sem("q_done")
        tok, q_read, o_part = sem("tok"), sem("q_read"), sem("o_part")
        o_ready, o_out, o_in = sem("o_ready"), sem("o_out"), sem("o_in")
        gt_ready, gt_act, route_done = sem("gt_ready"), sem("gt_act"), sem("route_done")
        gu_ready, silu0, h0_done, d_ready, y0_taken = (
            sem(n) for n in ("gu_ready", "silu0", "h0_done", "d_ready", "y0_taken"))
        f_ready, relu_a, relu_v, y1_ready, y1_taken, we_used = (
            sem(n) for n in ("f_ready", "relu_a", "relu_v", "y1_ready", "y1_taken", "we_used"))
        qk_ready, q_taken, k_a, k_v = sem("qk_ready"), sem("q_taken"), sem("k_a"), sem("k_v")
        xd_ready, v_ready, v_taken = sem("xd_ready"), sem("v_ready"), sem("v_taken")
        as_ready, sub_done, pa_ready = sem("as_ready"), sem("sub_done"), sem("pa_ready")
        at_ready, at_a, at_v = sem("at_ready"), sem("at_a"), sem("at_v")
        ao_ready, aon_ready, aot_ready, aoc_ready, ay_ready, ay_taken = (
            sem(n) for n in ("ao_ready", "aon_ready", "aot_ready", "aoc_ready", "ay_ready", "ay_taken"))
        stored = sem("stored")

        block = ctx.enter_context(nc.Block())

        def w_of(n, c, m):
            return W[:, n, c, m * P:(m + 1) * P]

        def bcast(v, shape):
            return v.rearrange("p (n o) -> p n o", o=1).to_broadcast(shape)

        def bcast_mid(v, shape):
            return v.rearrange("p (o n) -> p o n", o=1).to_broadcast(shape)

        @block.sync
        def _(sp):
            sp.dma_start(X[:], x_in).then_inc(ld_x, 16)
            sp.dma_start(W[:, 0:4], w_small[:, 0:4]).then_inc(ld_w, 16)
            sp.dma_start(cols[:], cols_in).then_inc(ld_w, 16)
            for r in range(2):
                sp.dma_start(CTX_T[:, r], ctx_t[r]).then_inc(ld_ct[r], 16)
                if r == 0:
                    sp.dma_start(maskP, mask_in).then_inc(ld_mask, 16)
                    sp.dma_start(rows[:], rows_in).then_inc(ld_mask, 16)
                sp.dma_start(CTX_N[:, r], ctx_n[r]).then_inc(ld_cn[r], 16)
            def context(n):
                r = n % 2
                sp.wait_ge(sc_ready, KB4 * (n - 1))
                sp.dma_start(CTX_T[:, r], ctx_t[PAIR[n]]).then_inc(ld_ct[r], 16)
                sp.wait_ge(pv_ready, n - 1)
                sp.dma_start(CTX_N[:, r], ctx_n[PAIR[n]]).then_inc(ld_cn[r], 16)

            for n in range(2, NT):
                context(n)
            sp.dma_start(W[:, 4:12], w_small[:, 4:12]).then_inc(ld_rest, 16)
            sp.dma_start(narrow[:], narrow_in).then_inc(ld_rest, 16)
            sp.dma_start(b2e[:], b2_in).then_inc(ld_rest, 16)
            if stages > 1:
                for z in range(3):
                    if z == 1:
                        sp.wait_ge(small_a, 1)
                        sp.dma_start(scratch_beta.rearrange("b h t -> h b t"),
                                     betaT.rearrange("h (b t) -> h b t", b=B)).then_inc(b_out, 16)
                    for m in range(DC):
                        sp.wait_ge(silu_done, 2 * z + m + 1)
                        sp.dma_start(scratch[z, :, m * P:(m + 1) * P, :].rearrange("b c t -> c b t"),
                                     Y[z][m]).then_inc(y_out[z], 16)
                    sp.wait_ge(y_out[z], 32)
                    sp.dma_start(raw[z], scratch[z].rearrange("b (h d) t -> (b h) d t", d=HD)).then_inc(y_in[z], 16)
                    if z == 1:
                        sp.wait_ge(b_out, 16)
                        sp.dma_start(beta, scratch_beta.rearrange("b h t -> (b h) t")).then_inc(b_in, 16)
                sp.wait_ge(o_ready, 1)
                sp.dma_start(scratch[3].rearrange("b (h m) t -> (b h) m t", m=HD), O).then_inc(o_out, 16)
                sp.wait_ge(o_out, 16)
                for m in range(DC):
                    sp.dma_start(OTr[:, m].rearrange("p (b t) -> p b t", b=B),
                                 scratch[3, :, m * P:(m + 1) * P, :].rearrange("b c t -> c b t")).then_inc(o_in, 16)
            if stages > 2:
                sp.wait_ge(xa_done, 2)
                for r in range(4):
                    sp.dma_start(W0[r], w_ffn0[r]).then_inc(ld_w0[r], 16)
                with sp.Fori(1, E0 // 4) as g:
                    for r in range(4):
                        sp.wait_ge(d_ready, 8 * g + 2 * r - 6)
                        sp.dma_start(W0[r], w_ffn0[bass.ds(4 * g + r, 1)].rearrange(
                            "e p a b c -> p (e a) b c")).then_inc(ld_w0[r], 16)
                sp.wait_ge(d_ready, 2 * (E0 - 3))
                sp.dma_start(W0[0], w_ffn0[E0]).then_inc(ld_w0[0], 16)
            if stages > 3:
                sp.wait_ge(xa_done, 3)
                for n in range(NT + 2, 2 * NT):
                    context(n)
                sp.wait_ge(pv_ready, 2 * NT)
                sp.dma_start(WQV, wqv_in).then_inc(ld_wqv, 16)
            if stages > 5:
                for e in range(2):
                    sp.dma_start(WE1[e], w_ffn1[e][:, 0:2048].rearrange("p (c n) -> p c n", c=DC)).then_inc(ld_we[e], 16)
                    sp.dma_start(WE2[e], w_ffn1[e][:, 2048:4096].rearrange("p (c n) -> p c n", c=FC)).then_inc(ld_we[e], 16)
                with sp.Fori(1, E1 // 2) as g:
                    for r in range(2):
                        sp.wait_ge(we_used, 2 * g + r - 1)
                        src = w_ffn1[bass.ds(2 * g + r, 1)].rearrange("e p n -> p (e n)")
                        sp.dma_start(WE1[r], src[:, 0:2048].rearrange("p (c n) -> p c n", c=DC)).then_inc(ld_we[r], 16)
                        sp.dma_start(WE2[r], src[:, 2048:4096].rearrange("p (c n) -> p c n", c=FC)).then_inc(ld_we[r], 16)
            sp.wait_ge(xa_done, stages)
            sp.dma_start(out, X[:]).then_inc(stored, 16)
            sp.wait_ge(stored, 16)

        @block.gpsimd
        def _(pool):
            n = [0]

            def chain(ins):
                n[0] += 1
                ins.then_inc(pol, 1)
                pool.wait_ge(pol, n[0])

            pool.memset(eps5[:], 1e-5).then_inc(consts, 1)
            pool.memset(eps6[:], 1e-6).then_inc(consts, 1)
            chain(pool.memset(ident[:], 0.0))
            pool.affine_select(out=ident[:], in_=ident[:], compare_op=ALU.not_equal, fill=1.0, base=0,
                               pattern=[[-1, P]], channel_multiplier=1).then_inc(consts, 1)
            chain(pool.memset(headmask[:], 1.0))
            chain(pool.affine_select(out=headmask[:], in_=headmask[:], compare_op=ALU.is_ge, fill=0.0, base=0,
                                     pattern=[[-HD, HC]], channel_multiplier=1))
            pool.affine_select(out=headmask[:], in_=headmask[:], compare_op=ALU.is_ge, fill=0.0, base=HD - 1,
                               pattern=[[HD, HC]], channel_multiplier=-1).then_inc(consts, 1)
            pool.iota(index[:], pattern=[[0, NT], [1, E1]], base=-E1, channel_multiplier=0,
                      allow_small_or_imprecise_dtypes=True).then_inc(consts, 1)
            if stages > 1:
                pool.wait_ge(y_in[2], 16)
                pool.tensor_copy(QN.rearrange("p t d -> p d t"), raw[2]).then_inc(q_done, 1)
                pool.wait_ge(q_done, 1)
                pool.wait_ge(q_sq, 1)
                pool.sem_inc(q_read, 1)
                pool.sem_inc(o_part, 1)
                with pool.Fori(0, S // UNROLL) as g:
                    for half in range(UNROLL // GROUP):
                        part = g * 10 + (5 * half + 1)
                        pool.wait_ge(o_part, part)
                        for r in range(GROUP):
                            t = UNROLL * g + GROUP * half + r
                            pool.wait_ge(tok, STEPS * t + 8)
                            pool.tensor_tensor(qS[:, HD * r:HD * (r + 1)], state[GROUP * half + r],
                                               QN[:, bass.ds(t, 1)].to_broadcast([P, HD, HD]),
                                               ALU.mult).then_inc(q_read, 1)
                        pool.wait_ge(q_read, UNROLL * g + (GROUP * (half + 1) + 1))
                        pool.tensor_tensor(tr8, qS[:, :, 0:8], qS[:, :, 8:16], ALU.add).then_inc(o_part, 1)
                        pool.wait_ge(o_part, part + 1)
                        pool.tensor_tensor(tr4, tr8[:, :, 0:4], tr8[:, :, 4:8], ALU.add).then_inc(o_part, 1)
                        pool.wait_ge(o_part, part + 2)
                        pool.tensor_tensor(tr2, tr4[:, :, 0:2], tr4[:, :, 2:4], ALU.add).then_inc(o_part, 1)
                        pool.wait_ge(o_part, part + 3)
                        pair = tr2.rearrange("p (t m) d -> p t m d", t=GROUP)
                        pool.tensor_tensor(O[:, :, bass.ds(UNROLL * g + GROUP * half, GROUP)].rearrange("p m t -> p t m"),
                                           pair[:, :, :, 0], pair[:, :, :, 1], ALU.add).then_inc(o_part, 2)

            if stages > 4:
                pool.wait_ge(ln_xt, 10)
                for c in range(DC):
                    pool.tensor_copy(XD[:, c].rearrange("p b (o z) -> p b o z", o=2),
                                     XT[:, c].rearrange("p (b o z) -> p b o z", b=B, o=1).to_broadcast(
                                         [P, B, 2, S])).then_inc(xd_ready, 1)

        @block.scalar
        def _(act):
            n = [0]

            def chain(ins):
                n[0] += 1
                ins.then_inc(sca, 1)
                act.wait_ge(sca, n[0])

            act.wait_ge(consts, 2)

            def norm(k):
                act.wait_ge(ln_stat, k + 1)
                act.activation(std[:], mv[:, :, 1], ACT.Sqrt, bias=eps5[:]).then_inc(ln_std, 1)
                act.wait_ge(ln_tr, 2 * k + 1)
                act.activation(XT[:, 0], ps[:, 6], ACT.Copy).then_inc(ln_xt, 1)

            def cross(s):
                def exp(p):
                    n = NT * s + p
                    act.wait_ge(mx_ready, n + 1)
                    act.activation(prob[p % 2], prob[p % 2], ACT.Exp, bias=nmx[:, p:p + 1],
                                   accum_out=den[:, p:p + 1]).then_inc(ex_ready, 1)

                exp(0)
                for p in range(NT):
                    n = NT * s + p
                    for g in range(4):
                        act.wait_ge(pt_ready, 4 * n + g + 1)
                        w = min(4, KT - 4 * g)
                        for j in range(w):
                            k = keys_of(4 * g + j, P)
                            if j == 0 or k < P:
                                full = [i for i in range(w) if keys_of(4 * g + i, P) == P]
                                if j == 0 and full:
                                    last = act.activation(probT[p % 2][:, 4 * g:4 * g + len(full)],
                                                          ps[:, 4 + g % 2, 0:P * len(full)].rearrange(
                                                              "p (a b) -> p a b", b=P), ACT.Copy)
                                if k < P:
                                    last = act.activation(probT[p % 2][0:k, 4 * g + j],
                                                          ps[0:k, 4 + g % 2, P * j:P * (j + 1)], ACT.Copy)
                        last.then_inc(pt_taken, 1)
                    if p + 1 < NT:
                        exp(p + 1)
                    if s:
                        act.wait_ge(on_ready, p + 1)
                        q = P * PAIR[n]
                        act.activation(HQT[:, :, q:q + P], ps[:, 7, 0:D].rearrange("p (c q) -> p c q", c=DC),
                                       ACT.Copy).then_inc(on_taken, 1)

            norm(0)
            act.wait_ge(ld_w, 32)
            for k, (dst, bias, scale) in enumerate(((HA, C_B1, 1.0), (HB, C_B2, 1.0), (HA, None, 1.0), (QT, None, SCALE))):
                act.wait_ge(pj_ready, 2 * k + 1)
                if bias is None:
                    act.activation(dst[:, 0], ps[:, 2 * (k % 2)], ACT.Copy, scale=scale).then_inc(pj_a, 1)
                else:
                    act.activation(dst[:, 0], ps[:, 2 * (k % 2)], ACT.Identity,
                                   bias=cols[:, bias:bias + 1]).then_inc(pj_a, 1)
            cross(0)
            if stages > 1:
                norm(1)

                def tap(k):
                    z, m = divmod(k, 2)
                    c = C_CONV + 8 * z + 4 * m + TAPS - 1
                    act.wait_ge(ap_ready, k + 1)
                    act.activation(Y[z][m], ps[:, k].rearrange("p (b t) -> p b t", b=B), ACT.Copy,
                                   scale=cols[:, c:c + 1]).then_inc(first_tap, 1)

                def silu_of(k):
                    z, m = divmod(k, 2)
                    act.wait_ge(conv_done, k + 1)
                    act.activation(Y[z][m], Y[z][m], ACT.Silu).then_inc(silu_done, 1)

                tap(0)
                tap(1)
                act.wait_ge(b_ready, 1)
                act.activation(betaT, ps[0:H, 6], ACT.Sigmoid).then_inc(small_a, 1)
                tap(2)
                silu_of(0)
                tap(3)
                silu_of(1)
                tap(4)
                silu_of(2)
                tap(5)
                for k in range(3, 6):
                    silu_of(k)
                act.wait_ge(dl_v, 1)
                act.activation(nk, ss, ACT.Sqrt).then_inc(dl_a, 1)
                act.wait_ge(y_in[2], 16)
                act.activation(OS, raw[2], ACT.Square).then_inc(q_sq, 1)
                act.wait_ge(dl_v, 2)
                act.activation(nk, ss, ACT.Sqrt).then_inc(dl_a, 1)
                act.wait_ge(dl_v, 3)
                act.activation(nk, ss, ACT.Sqrt, bias=eps6[:], scale=1.0 / HD).then_inc(dl_a, 1)
            if stages > 2:
                norm(2)
                act.wait_ge(gt_ready, 1)
                act.activation(sg, ps[:, 4, 0:NT * E0].rearrange("p (a b) -> p a b", a=NT), ACT.Sigmoid).then_inc(gt_act, 1)

                def silu(count, m):
                    act.wait_ge(gu_ready, count)
                    act.activation(G[:, m], ps[:, 2 * m], ACT.Silu).then_inc(silu0, 1)

                with act.Fori(0, E0 + 1) as e:
                    for m in range(DC):
                        silu(2 * e + m + 1, m)
            if stages > 3:
                norm(3)
                cross(1)
                act.wait_ge(small_v, 1)
                act.activation(batt[0:NT], batt[0:NT], ACT.Exp).then_inc(small_a, 1)
            if stages > 4:
                norm(4)
                for m in range(DC):
                    act.wait_ge(qk_ready, m + 1)
                    act.activation(QTT[:, m], ps[:, m], ACT.Identity,
                                   bias=cols[:, C_BQ + m:C_BQ + m + 1]).then_inc(q_taken, 1)
                act.wait_ge(small_v, 2)
                act.wait_ge(qk_ready, DC + 1)
                for h in range(HC):
                    act.activation(KM[0][:, h], ps[:, 2], ACT.Identity, scale=headmask[:, h:h + 1],
                                   bias=bkm[:, h:h + 1]).then_inc(k_a, 1)
                for i in range(NT):
                    act.wait_ge(sub_done, i + 1)
                    act.activation(PA[i % 2], PA[i % 2], ACT.Exp, scale=HD ** -0.5).then_inc(pa_ready, 1)
                    act.wait_ge(at_ready, 2 * i + 1)
                    act.activation(PAT[i % 2][:, 0:4], ps[:, 2].rearrange("p (a b) -> p a b", b=P),
                                   ACT.Copy).then_inc(at_a, 1)
                    act.wait_ge(aot_ready, i + 1)
                    act.activation(OAT, ps[:, 5, 0:D].rearrange("p (a b) -> p a b", b=P), ACT.Copy).then_inc(aoc_ready, 1)
            if stages > 5:
                norm(5)
                act.wait_ge(route_done, 2)
                with act.Fori(0, E1) as e:
                    for f in range(0, FC, 2):
                        act.wait_ge(f_ready, FC * e + f + 1)
                        act.activation(HF[:, f], ps[:, f % 4], ACT.Relu,
                                       bias=cols[:, bass.ds(FC * e + (C_F1 + f), 1)]).then_inc(relu_a, 1)

        @block.vector
        def _(dve):
            n = [0]

            def chain(ins):
                n[0] += 1
                ins.then_inc(vec, 1)
                dve.wait_ge(vec, n[0])

            def norm(k):
                for i in range(NT):
                    dve.bn_stats(stats[:, i], X[:, i]).then_inc(vec, 1)
                    n[0] += 1
                dve.wait_ge(vec, n[0])
                for i in range(NT):
                    last = dve.bn_aggr(mv[:, i], stats[:, i])
                last.then_inc(ln_stat, 1)
                dve.wait_ge(ln_std, k + 1)
                chain(dve.reciprocal(std[:], std[:]))
                for i in range(NT):
                    dve.tensor_scalar(XN[:, i], X[:, i], mv[:, i, 0:1], std[:, i:i + 1], ALU.subtract,
                                      ALU.mult).then_inc(ln_xn, 1)
                dve.wait_ge(ln_tr, 2 * k + 2)
                dve.tensor_copy(XT[:, 1], ps[:, 7]).then_inc(ln_xt, 1)

            def cross(s):
                def scores(p):
                    k = NT * s + p
                    i = PAIR[k]
                    for j in range(KB4):
                        w = keys_of(j, BANK)
                        at = slice(BANK * j, BANK * j + w)
                        dve.wait_ge(sc_ready, KB4 * k + j + 1)
                        if s == 0:
                            dve.scalar_tensor_tensor(prob[p % 2][:, at], ps[:, j, 0:w], crow[:, i:i + 1], maskP[:, at],
                                                     ALU.add, ALU.add).then_inc(sc_taken, 1)
                        else:
                            dve.tensor_scalar(prob[p % 2][:, at], ps[:, j, 0:w], crow[:, i:i + 1], None,
                                              ALU.add).then_inc(sc_taken, 1)
                    dve.wait_ge(sc_taken, KB4 * (k + 1))
                    chain(dve.reduce_max(mx[:, i:i + 1], prob[p % 2], axis=AX.X))
                    dve.tensor_scalar(nmx[:, p:p + 1], mx[:, i:i + 1], -1.0, None, ALU.mult).then_inc(mx_ready, 1)

                def finish(p):
                    k = NT * s + p
                    i = PAIR[k]
                    dve.wait_ge(ex_ready, k + 1)
                    chain(dve.reciprocal(rec[:, p:p + 1], den[:, p:p + 1]))
                    dve.wait_ge(pv_ready, k + 1)
                    if s == 0:
                        dve.scalar_tensor_tensor(X[:, i], ps[:, 6, 0:D], rec[:, p:p + 1], X[:, i],
                                                 ALU.mult, ALU.add).then_inc(pv_taken, 1)
                    else:
                        if p:
                            dve.wait_ge(on_ready, p)
                        dve.tensor_scalar(hq, ps[:, 6, 0:D], rec[:, p:p + 1], None, ALU.mult).then_inc(pv_taken, 1)

                scores(0)
                for p in range(NT):
                    if p + 1 < NT:
                        scores(p + 1)
                    finish(p)
                if s == 0:
                    dve.wait_ge(pv_taken, NT)

            dve.wait_ge(ld_x, 16)
            norm(0)
            dve.wait_ge(ld_w, 32)
            for k, (dst, bias) in enumerate(((HA, C_B1), (HB, C_B2), (HA, None), (QT, None))):
                dve.wait_ge(pj_ready, 2 * k + 2)
                if bias is None:
                    dve.tensor_scalar(dst[:, 1], ps[:, 2 * (k % 2) + 1], SCALE if k == 3 else 1.0, None,
                                      ALU.mult).then_inc(pj_v, 1)
                else:
                    dve.tensor_scalar(dst[:, 1], ps[:, 2 * (k % 2) + 1], cols[:, bias + 1:bias + 2], None,
                                      ALU.add).then_inc(pj_v, 1)
            dve.wait_ge(cr_ready, 1)
            chain(dve.tensor_scalar(crow, ps[:, 7, 0:NT], SCALE, None, ALU.mult))
            dve.wait_ge(ld_mask, 32)
            cross(0)
            dve.sem_inc(xa_done, 1)

            if stages > 1:
                norm(1)
                dve.wait_ge(ld_rest, 48)
                for k in range(6):
                    z, m = divmod(k, 2)
                    c = C_CONV + 8 * z + 4 * m
                    dve.wait_ge(first_tap, k + 1)
                    pre = ps[:, k].rearrange("p (b t) -> p b t", b=B)
                    for back in range(1, TAPS):
                        ins = dve.scalar_tensor_tensor(Y[z][m][:, :, back:S], pre[:, :, 0:S - back],
                                                       cols[:, c + TAPS - 1 - back:c + TAPS - back],
                                                       Y[z][m][:, :, back:S], ALU.mult, ALU.add)
                        if back < TAPS - 1:
                            chain(ins)
                        else:
                            ins.then_inc(conv_done, 1)
                dve.wait_ge(y_in[0], 16)
                chain(dve.tensor_tensor(sq, raw[0], raw[0], ALU.mult))
                dve.reduce_sum(ss, sq.rearrange("p d t -> p t d"), axis=AX.X).then_inc(dl_v, 1)
                for v in (KB, VB):
                    chain(dve.memset(v[:, S:S + 1], 0.0))
                chain(dve.memset(nega[:, S:S + 1], 0.0))
                dve.wait_ge(y_in[1], 16)
                dve.wait_ge(b_in, 16)
                chain(dve.tensor_tensor(VB[:, 0:S].rearrange("p t m -> p m t"), raw[1],
                                        bcast_mid(beta, [P, HD, S]), ALU.mult))
                dve.wait_ge(dl_a, 1)
                chain(dve.tensor_scalar(nk, nk, 1e-6, None, ALU.max))
                chain(dve.reciprocal(nk, nk))
                chain(dve.tensor_tensor(KN[:, 0:S].rearrange("p t d -> p d t"), raw[0],
                                        bcast_mid(nk, [P, HD, S]), ALU.mult))
                chain(dve.tensor_tensor(KB[:, 0:S], KN[:, 0:S], bcast(beta, [P, S, HD]), ALU.mult))
                sqt = sq.rearrange("p d t -> p (d t)").rearrange("p (t d) -> p t d", d=HD)
                chain(dve.tensor_tensor(sqt[:, 0:S - 1], KB[:, 1:S], KN[:, 0:S - 1], ALU.mult))
                chain(dve.reduce_sum(nega[:, 1:S], sqt[:, 0:S - 1], axis=AX.X))
                chain(dve.tensor_scalar(nega[:, 1:S], nega[:, 1:S], -1.0, None, ALU.mult))
                dve.memset(state[UNROLL - 1], 0.0).then_inc(tok, 2)
                dve.wait_ge(tok, 2)
                dve.tensor_copy(uu[0], VB[:, 0]).then_inc(tok, 1)
                with dve.Fori(0, S // UNROLL) as g:
                    for r in range(UNROLL):
                        t = UNROLL * g + r
                        base = (STEPS * UNROLL) * g + STEPS * r + 3
                        old, new = state[(r - 1) % UNROLL], state[r]
                        u, unext = uu[r % 2], uu[(r + 1) % 2]
                        dve.wait_ge(tok, base - 1)
                        dve.tensor_tensor(kS, old, KB[:, bass.ds(t + 1, 1)].to_broadcast([P, HD, HD]),
                                          ALU.mult).then_inc(tok, 1)
                        dve.wait_ge(tok, base)
                        dve.tensor_tensor(outer, bcast(u, [P, HD, HD]),
                                          KN[:, bass.ds(t, 1)].to_broadcast([P, HD, HD]), ALU.mult).then_inc(tok, 1)
                        dve.wait_ge(tok, base + 1)
                        dve.reduce_sum(rsum, kS, axis=AX.X).then_inc(tok, 1)
                        dve.scalar_tensor_tensor(wv, u, nega[:, bass.ds(t + 1, 1)],
                                                 VB[:, bass.ds(t + 1, 1)].rearrange("p o m -> p (o m)"),
                                                 ALU.mult, ALU.add).then_inc(tok, 1)
                        if r == 0:
                            dve.wait_ge(q_read, UNROLL * g + 1)
                        dve.wait_ge(tok, base + 2)
                        dve.tensor_tensor(new, old, outer, ALU.add).then_inc(tok, 1)
                        dve.wait_ge(tok, base + 4)
                        dve.tensor_tensor(unext, wv, rsum, ALU.subtract).then_inc(tok, 1)
                dve.wait_ge(q_sq, 1)
                dve.reduce_sum(ss, OS.rearrange("p d t -> p t d"), axis=AX.X).then_inc(dl_v, 1)
                dve.wait_ge(dl_a, 2)
                chain(dve.tensor_scalar(nk, nk, 1e-6, None, ALU.max))
                chain(dve.reciprocal(nk, nk))
                chain(dve.tensor_scalar(qscale, nk, HD ** -0.5, None, ALU.mult))
                chain(dve.tensor_tensor(beta, qscale, qscale, ALU.mult))
                dve.wait_ge(o_part, 10 * (S // UNROLL) + 1)
                chain(dve.tensor_tensor(OS, O, O, ALU.mult))
                chain(dve.reduce_sum(ss, OS.rearrange("p m t -> p t m"), axis=AX.X))
                dve.tensor_tensor(ss, ss, beta, ALU.mult).then_inc(dl_v, 1)
                dve.wait_ge(dl_a, 3)
                chain(dve.reciprocal(nk, nk))
                chain(dve.tensor_tensor(nk, nk, qscale, ALU.mult))
                dve.tensor_tensor(O, O, bcast_mid(nk, [P, HD, S]), ALU.mult).then_inc(o_ready, 1)
                for m in range(DC):
                    dve.wait_ge(o_in, 32)
                    chain(dve.tensor_scalar(OTr[:, m], OTr[:, m], cols[:, C_ON:C_ON + 1], None, ALU.mult))
                dve.sem_inc(o_ready, 1)
                for i in range(NT):
                    dve.wait_ge(ap_ready, 7 + i)
                    chain(dve.tensor_tensor(X[:, i], ps[:, i, 0:D], X[:, i], ALU.add))
                dve.sem_inc(xa_done, 1)

            if stages > 2:
                norm(2)
                dve.wait_ge(gt_act, 1)
                chain(dve.tensor_tensor(sel, sg, bcast_mid(rows[:, R_EB:R_EB + E0], [P, NT, E0]), ALU.add))
                for i in range(NT):
                    chain(dve.max(top8[:, i], sel[:, i]))
                    chain(dve.match_replace(rep[:, i], top8[:, i], sel[:, i], CUT))
                chain(dve.tensor_tensor(rep, sel, rep, ALU.not_equal))
                chain(dve.tensor_tensor(cw[:, :, 0:E0], sg, rep, ALU.mult))
                chain(dve.reduce_sum(csum, cw[:, :, 0:E0], axis=AX.X))
                chain(dve.reciprocal(csum, csum))
                chain(dve.tensor_scalar(csum, csum, ROUTE, None, ALU.mult))
                chain(dve.tensor_tensor(cw[:, :, 0:E0], cw[:, :, 0:E0], bcast(csum, [P, NT, E0]), ALU.mult))
                chain(dve.memset(cw[:, :, E0:E0 + 1], 1.0))

                def gated(count, m, buf):
                    dve.wait_ge(silu0, count)
                    dve.tensor_tensor(HT[buf][:, m], ps[:, 2 * m + 1], G[:, m], ALU.mult).then_inc(h0_done, 1)

                def weigh(e, two_e):
                    for i in range(NT):
                        if i % 2 == 0:
                            dve.wait_ge(d_ready, two_e + i // 2 + 1)
                        w = cw[:, i, bass.ds(e, 1)] if not isinstance(e, int) else cw[:, i, e:e + 1]
                        dve.scalar_tensor_tensor(X[:, i], ps[:, 4 + i // 2, D * (i % 2):D * (i % 2 + 1)], w, X[:, i],
                                                 ALU.mult, ALU.add).then_inc(y0_taken, 1)

                for m in range(DC):
                    gated(m + 1, m, 0)
                dve.sem_inc(y0_taken, 1)
                with dve.Fori(0, E0 // 4) as g:
                    for r in range(4):
                        e = 4 * g + r
                        for m in range(DC):
                            gated(8 * g + 2 * r + 2 + m + 1, m, (r + 1) % 2)
                        dve.wait_ge(y0_taken, 16 * g + (4 * r + 1))
                        weigh(e, 8 * g + 2 * r)
                dve.wait_ge(y0_taken, 4 * E0 + 1)
                weigh(E0, 2 * E0)
                dve.wait_ge(y0_taken, 4 * (E0 + 1) + 1)
                dve.sem_inc(xa_done, 1)

            if stages > 3:
                norm(3)
                dve.wait_ge(ln_xt, 8)
                for c in range(DC):
                    dve.tensor_scalar(QT[:, c], XT[:, c], cols[:, C_S3 + c:C_S3 + c + 1],
                                      cols[:, C_S2 + c:C_S2 + c + 1], ALU.mult, ALU.add).then_inc(pj_v, 1)
                dve.wait_ge(cr_ready, 2)
                chain(dve.tensor_scalar(crow, ps[:, 7, 0:NT], rows[:, R_SIM:R_SIM + 1], None, ALU.add))
                cross(1)
                for i in range(NT):
                    chain(dve.tensor_tensor(X[:, i], X[:, i], rows[:, R_QV:R_QV + D], ALU.add))
                dve.wait_ge(small_pe, 1)
                pm = ps[0:NT, 7, 0:P].rearrange("p (a b) -> p a b", a=2)
                chain(dve.reduce_max(bsum[0:NT], pm, axis=AX.X))
                dve.tensor_tensor(battv[0:NT], pm, bcast(bsum[0:NT], [NT, 2, S]), ALU.subtract).then_inc(small_v, 1)
                dve.wait_ge(small_a, 2)
                chain(dve.reduce_sum(bsum[0:NT], battv[0:NT], axis=AX.X))
                chain(dve.reciprocal(bsum[0:NT], bsum[0:NT]))
                chain(dve.tensor_tensor(battv[0:NT], battv[0:NT], bcast(bsum[0:NT], [NT, 2, S]), ALU.mult))
                chain(dve.memset(bmask, 0.0))
                dve.sem_inc(bt_ready, 1)
                dve.wait_ge(small_pe, 2)
                for half in range(2):
                    q = slice(S * half, S * (half + 1))
                    chain(dve.tensor_copy(bmask[q, :, half], ps[q, 7, 128:128 + NT]))
                dve.sem_inc(bt_ready, 1)
                dve.wait_ge(small_pe, 3)
                chain(dve.tensor_copy(hcb, ps[:, 7, 256:256 + DC * B].rearrange("p (a b) -> p a b", a=DC)))
                dve.wait_ge(on_taken, NT)
                for c in range(DC):
                    chain(dve.tensor_tensor(F3[:, c], XT[:, c], HQT[:, c], ALU.mult))
                    chain(dve.tensor_tensor(F4[:, c].rearrange("p (b t) -> p b t", b=B),
                                            XT[:, c].rearrange("p (b t) -> p b t", b=B),
                                            bcast(hcb[:, c], [P, B, S]), ALU.mult))
                dve.sem_inc(bt_ready, 1)
                for i in range(NT):
                    dve.wait_ge(small_pe, 4 + i)
                    chain(dve.tensor_tensor(X[:, i], ps[:, i, 0:D], X[:, i], ALU.add))
                dve.sem_inc(xa_done, 1)

            if stages > 4:
                norm(4)
                chain(dve.tensor_scalar(bkm, headmask[:], cols[:, C_BK:C_BK + 1], None, ALU.mult))
                dve.sem_inc(small_v, 1)
                for i in range(NT):
                    chain(dve.tensor_tensor(X[:, i], X[:, i], rows[:, R_BO:R_BO + D], ALU.add))
                chain(dve.memset(VM, 0.0))
                dve.wait_ge(qk_ready, DC + 2)
                for h in range(HC):
                    dve.tensor_scalar(KM[1][:, h], ps[:, 3], cols[:, C_BK + 1:C_BK + 2],
                                      headmask[:, h:h + 1], ALU.add, ALU.mult).then_inc(k_v, 1)
                for b in range(B):
                    dve.wait_ge(v_ready, b + 1)
                    for half in range(2):
                        q = slice(S * half, S * (half + 1))
                        src = ps[q, 4 + b % 4, 0:D].rearrange("p (j h m) -> p j h m", h=2, m=HD)[:, :, half]
                        bias = rows[q, R_BV:R_BV + D].rearrange("p (j h m) -> p j h m", h=2, m=HD)[:, :, half]
                        dve.tensor_tensor(VM[q, b, :, HD * half:HD * (half + 1)], src, bias, ALU.add).then_inc(v_taken, 1)

                def scaled(i):
                    dve.wait_ge(as_ready, i + 1)
                    sc = psf[:, 0:H * S].rearrange("p (h z) -> p h z", h=H)
                    chain(dve.reduce_max(am, sc, axis=AX.X))
                    dve.tensor_tensor(PA[i % 2], sc, bcast(am, [P, H, S]), ALU.subtract).then_inc(sub_done, 1)

                def weighted(i):
                    dve.wait_ge(at_ready, 2 * i + 2)
                    dve.tensor_copy(PAT[i % 2][:, 4:8], ps[:, 3].rearrange("p (a b) -> p a b", b=P)).then_inc(at_v, 1)
                    chain(dve.reduce_sum(asum, PA[i % 2], axis=AX.X))
                    chain(dve.reciprocal(asum, asum))
                    dve.wait_ge(ao_ready, i + 1)
                    dve.tensor_tensor(ON.rearrange("p (h m) -> p h m", h=H),
                                      ps[:, 4, 0:D].rearrange("p (h m) -> p h m", h=H),
                                      bcast(asum, [P, H, HD]), ALU.mult).then_inc(aon_ready, 1)
                    dve.wait_ge(ay_ready, i + 1)
                    dve.tensor_tensor(X[:, i], ps[:, 5, D:2 * D], X[:, i], ALU.add).then_inc(ay_taken, 1)

                scaled(0)
                for i in range(NT):
                    if i + 1 < NT:
                        scaled(i + 1)
                    weighted(i)
                dve.wait_ge(ay_taken, NT)
                dve.sem_inc(xa_done, 1)

            if stages > 5:
                norm(5)
                dve.wait_ge(gt_ready, 2)
                chain(dve.tensor_tensor(lg, ps[:, 4, 0:NT * E1].rearrange("p (a b) -> p a b", a=NT),
                                        bcast_mid(rows[:, R_BR:R_BR + E1], [P, NT, E1]), ALU.add))
                chain(dve.reduce_max(lmax, lg, axis=AX.X))
                chain(dve.tensor_tensor(eq, lg, bcast(lmax, [P, NT, E1]), ALU.is_equal))
                chain(dve.tensor_tensor(eq, eq, index[:], ALU.mult))
                chain(dve.tensor_reduce(lmin, eq, op=ALU.min, axis=AX.X))
                chain(dve.tensor_tensor(oh, index[:], bcast(lmin, [P, NT, E1]), ALU.is_equal))
                dve.sem_inc(route_done, 1)
                dve.wait_ge(gt_ready, 3)
                chain(dve.tensor_copy(ohT, ps[0:E1, 5]))
                dve.sem_inc(route_done, 1)
                for i in range(NT):
                    dve.wait_ge(gt_ready, 4 + i // 2)
                    dve.tensor_tensor(X[:, i], ps[:, 6 + i // 2, D * (i % 2):D * (i % 2 + 1)], X[:, i],
                                      ALU.add).then_inc(y1_taken, 1)
                with dve.Fori(0, E1) as e:
                    for f in range(1, FC, 2):
                        dve.wait_ge(f_ready, FC * e + f + 1)
                        dve.tensor_scalar(HF[:, f], ps[:, f % 4], cols[:, bass.ds(FC * e + (C_F1 + f), 1)], 0.0,
                                          ALU.add, ALU.max).then_inc(relu_v, 1)
                    dve.wait_ge(y1_taken, NT * e + NT)
                    for i in range(NT):
                        dve.wait_ge(y1_ready, NT * e + i + 1)
                        dve.scalar_tensor_tensor(X[:, i], ps[:, 4 + i, 0:D], oh[:, i, bass.ds(e, 1)], X[:, i],
                                                 ALU.mult, ALU.add).then_inc(y1_taken, 1)
                dve.wait_ge(y1_taken, NT * (E1 + 1))
                dve.sem_inc(xa_done, 1)

        @block.tensor
        def _(pe):
            pe.wait_ge(consts, 5)

            def norm(k):
                for c in range(DC):
                    for i in range(NT):
                        if c == 0:
                            pe.wait_ge(ln_xn, NT * k + i + 1)
                        last = pe.transpose(ps[:, 6 + c, P * i:P * (i + 1)], XN[:, i, P * c:P * (c + 1)], ident[:])
                    last.then_inc(ln_tr, 1)
                pe.wait_ge(ln_xt, 2 * k + 2)

            def linear(dst, w, src, m):
                for c in range(DC):
                    last = pe.matmul(dst, w_of(w, c, m), src[:, c], start=(c == 0), stop=(c == DC - 1))
                return last

            def cross(s):
                def scores(p):
                    k = NT * s + p
                    pe.wait_ge(ld_ct[k % 2], 16 * LOADS[k])
                    for j in range(KB4):
                        w = keys_of(j, BANK)
                        if k:
                            pe.wait_ge(sc_taken, KB4 * (k - 1) + j + 1)
                        for c in range(DC):
                            for half in range(2):
                                q = P * PAIR[k] + S * half
                                last = pe.matmul(ps[S * half:S * (half + 1), j, 0:w], QT[:, c, q:q + S],
                                                 CTX_T[:, k % 2, half, c, BANK * j:BANK * j + w],
                                                 start=(c == 0), stop=(c == DC - 1))
                        last.then_inc(sc_ready, 1)

                def turn(p):
                    pe.wait_ge(pv_taken, NT * s + p + 1)
                    if p:
                        pe.wait_ge(on_taken, p)
                    for c in range(DC):
                        last = pe.transpose(ps[:, 7, P * c:P * (c + 1)], hq[:, P * c:P * (c + 1)], ident[:])
                    last.then_inc(on_ready, 1)

                scores(0)
                for p in range(NT):
                    k = NT * s + p
                    if p + 1 < NT:
                        scores(p + 1)
                    if s and p:
                        turn(p - 1)
                    pe.wait_ge(ex_ready, k + 1)
                    for g in range(4):
                        if 4 * k + g >= 2:
                            pe.wait_ge(pt_taken, 4 * k + g - 1)
                        for j in range(4 * g, min(KT, 4 * g + 4)):
                            w = keys_of(j, P)
                            last = pe.transpose(ps[0:w, 4 + g % 2, P * (j % 4):P * (j % 4 + 1)],
                                                prob[p % 2][:, P * j:P * j + w], ident[:])
                        last.then_inc(pt_ready, 1)
                    pe.wait_ge(ld_cn[k % 2], 16 * LOADS[k])
                    pe.wait_ge(pt_taken, 4 * k + 4)
                    if k:
                        pe.wait_ge(pv_taken, k)
                    for j in range(KT):
                        w = keys_of(j, P)
                        for half in range(2):
                            q = slice(S * half, S * (half + 1))
                            last = pe.matmul(ps[q, 6, 0:D], probT[p % 2][0:w, j, q], CTX_N[0:w, k % 2, half, j],
                                             start=(j == 0), stop=(j == KT - 1))
                    last.then_inc(pv_ready, 1)
                if s:
                    turn(NT - 1)

            norm(0)
            pe.wait_ge(ld_w, 32)
            for k, (w, src) in enumerate(((W1T, XT), (W2T, HA), (W2N, HB), (W1N, HA))):
                if k:
                    pe.wait_ge(pj_a, k)
                    pe.wait_ge(pj_v, k)
                for m in range(DC):
                    linear(ps[:, 2 * (k % 2) + m], w, src, m).then_inc(pj_ready, 1)
            for i in range(NT):
                q = slice(P * i, P * (i + 1))
                terms = [(HA, C_B1, c) for c in range(DC)] + [(HB, C_B2, c) for c in range(DC)]
                for k, (src, col, c) in enumerate(terms):
                    last = pe.matmul(ps[:, 7, i:i + 1], src[:, c, q], cols[:, col + c:col + c + 1],
                                     start=(k == 0), stop=(k == 3))
            last.then_inc(cr_ready, 1)
            pe.wait_ge(pj_a, 4)
            pe.wait_ge(pj_v, 4)
            cross(0)

            if stages > 1:
                norm(1)
                pe.wait_ge(ld_rest, 48)
                for z, w in enumerate((AK, AV, AQ)):
                    for m in range(DC):
                        linear(ps[:, 2 * z + m], w, XT, m).then_inc(ap_ready, 1)
                    if z == 0:
                        for c in range(DC):
                            last = pe.matmul(ps[0:H, 6], narrow[:, c, N_BETA:N_BETA + H], XT[:, c],
                                             start=(c == 0), stop=(c == DC - 1))
                        last.then_inc(b_ready, 1)
                pe.wait_ge(o_ready, 2)
                for i in range(NT):
                    for c in range(DC):
                        last = pe.matmul(ps[:, i, 0:D], OTr[:, c, P * i:P * (i + 1)], W[:, AO, c],
                                         start=(c == 0), stop=(c == DC - 1))
                    last.then_inc(ap_ready, 1)

            def gates(col, width, at):
                for i in range(NT):
                    for c in range(DC):
                        last = pe.matmul(ps[:, 4, width * i:width * (i + 1)], XT[:, c, P * i:P * (i + 1)],
                                         narrow[:, c, col:col + width], start=(c == 0), stop=(c == DC - 1))
                last.then_inc(gt_ready, 1)

            if stages > 2:
                norm(2)
                gates(N_GATE, E0, 4)
                pe.wait_ge(gt_act, 1)

                def gate_up(buf, loaded, free):
                    pe.wait_ge(ld_w0[buf], loaded)
                    for m in range(DC):
                        if free is not None:
                            pe.wait_ge(h0_done, free + m)
                        for part in range(2):
                            for c in range(DC):
                                last = pe.matmul(ps[:, 2 * m + part], W0[buf][:, part, c, P * m:P * (m + 1)],
                                                 XT[:, c], start=(c == 0), stop=(c == DC - 1))
                        last.then_inc(gu_ready, 1)

                def down(buf, done, taken):
                    pe.wait_ge(h0_done, done)
                    pe.wait_ge(y0_taken, taken)
                    for i in range(NT):
                        for c in range(DC):
                            last = pe.matmul(ps[:, 4 + i // 2, D * (i % 2):D * (i % 2 + 1)],
                                             HT[buf % 2][:, c, P * i:P * (i + 1)], W0[buf][:, 2, c],
                                             start=(c == 0), stop=(c == DC - 1))
                        if i % 2:
                            last.then_inc(d_ready, 1)

                gate_up(0, 16, None)
                with pe.Fori(0, E0 // 4) as g:
                    for r in range(4):
                        gate_up((r + 1) % 4, 16 * g + (16 if r < 3 else 32), 8 * g + 2 * r + 1)
                        down(r, 8 * g + 2 * r + 2, 16 * g + (4 * r + 1))
                down(0, 2 * (E0 + 1), 4 * E0 + 1)

            if stages > 3:
                norm(3)
                for i in range(NT):
                    for c in range(DC):
                        last = pe.matmul(ps[:, 7, i:i + 1], XT[:, c, P * i:P * (i + 1)],
                                         cols[:, C_S1 + c:C_S1 + c + 1], start=(c == 0), stop=(c == DC - 1))
                last.then_inc(cr_ready, 1)
                pe.wait_ge(pj_v, 6)
                cross(1)
                pe.wait_ge(mx_ready, 2 * NT)
                pe.wait_ge(on_taken, NT)
                pe.transpose(ps[0:NT, 7, 0:P], mx, ident[:]).then_inc(small_pe, 1)
                pe.wait_ge(bt_ready, 1)
                pe.transpose(ps[:, 7, 128:128 + NT], batt[0:NT], ident[0:NT, 0:NT]).then_inc(small_pe, 1)
                pe.wait_ge(bt_ready, 2)
                for c in range(DC):
                    for i in range(NT):
                        at = 256 + B * c + 2 * i
                        last = pe.matmul(ps[:, 7, at:at + 2], XN[:, i, P * c:P * (c + 1)], bmask[:, i],
                                         start=True, stop=True)
                last.then_inc(small_pe, 1)
                pe.wait_ge(bt_ready, 3)
                pe.wait_ge(ld_wqv, 16)
                for i in range(NT):
                    for k, f in enumerate((XT, HQT, F3, F4)):
                        for c in range(DC):
                            last = pe.matmul(ps[:, i, 0:D], f[:, c, P * i:P * (i + 1)], WQV[:, DC * k + c],
                                             start=(k == 0 and c == 0), stop=(k == 3 and c == DC - 1))
                    last.then_inc(small_pe, 1)

            if stages > 4:
                norm(4)
                for m in range(DC):
                    linear(ps[:, m], SQ, XT, m).then_inc(qk_ready, 1)
                for m in range(DC):
                    linear(ps[:, 2 + m], SK, XT, m).then_inc(qk_ready, 1)
                pe.wait_ge(xd_ready, DC)
                for b in range(B):
                    if b >= 4:
                        pe.wait_ge(v_taken, 2 * (b - 3))
                    for c in range(DC):
                        last = pe.matmul(ps[:, 4 + b % 4, 0:D], XD[:, c, b], W[:, SV, c], start=(c == 0), stop=(c == DC - 1))
                    last.then_inc(v_ready, 1)
                pe.wait_ge(q_taken, DC)
                pe.wait_ge(k_a, HC)
                pe.wait_ge(k_v, HC)
                pe.wait_ge(v_taken, 2 * B)

                def scores(i):
                    if i:
                        pe.wait_ge(sub_done, i)
                    for m in range(DC):
                        for half in range(2):
                            q = P * i + S * half
                            last = pe.matmul(ps[S * half:S * (half + 1), m], QTT[:, m, q:q + S],
                                             KM[m][:, :, q:q + S], start=True, stop=True)
                    last.then_inc(as_ready, 1)

                scores(0)
                for i in range(NT):
                    if i + 1 < NT:
                        scores(i + 1)
                    pe.wait_ge(pa_ready, i + 1)
                    if i:
                        pe.wait_ge(at_v, i)
                        pe.wait_ge(at_a, i)
                    flat = PA[i % 2].rearrange("p h z -> p (h z)")
                    for j in range(HC):
                        last = pe.transpose(ps[:, 2 + j // 4, P * (j % 4):P * (j % 4 + 1)], flat[:, P * j:P * (j + 1)],
                                            ident[:])
                        if j % 4 == 3:
                            last.then_inc(at_ready, 1)
                    pe.wait_ge(at_a, i + 1)
                    pe.wait_ge(at_v, i + 1)
                    for half in range(2):
                        for j in range(HC):
                            last = pe.matmul(ps[S * half:S * (half + 1), 4, 32 * j:32 * (j + 1)],
                                             PAT[i % 2][:, j, S * half:S * (half + 1)], VM[:, 2 * i + half, j],
                                             start=True, stop=True)
                    last.then_inc(ao_ready, 1)
                    pe.wait_ge(aon_ready, i + 1)
                    if i:
                        pe.wait_ge(ay_taken, i)
                    for c in range(DC):
                        last = pe.transpose(ps[:, 5, P * c:P * (c + 1)], ON[:, P * c:P * (c + 1)], ident[:])
                    last.then_inc(aot_ready, 1)
                    pe.wait_ge(aoc_ready, i + 1)
                    for c in range(DC):
                        last = pe.matmul(ps[:, 5, D:2 * D], OAT[:, c], W[:, SO, c], start=(c == 0), stop=(c == DC - 1))
                    last.then_inc(ay_ready, 1)

            if stages > 5:
                norm(5)
                gates(N_ROUTE, E1, 4)
                pe.wait_ge(route_done, 1)
                for i in range(NT):
                    last = pe.transpose(ps[0:E1, 5, P * i:P * (i + 1)], oh[:, i], ident[:])
                last.then_inc(gt_ready, 1)
                pe.wait_ge(route_done, 2)
                for i in range(NT):
                    last = pe.matmul(ps[:, 6 + i // 2, D * (i % 2):D * (i % 2 + 1)], ohT[:, P * i:P * (i + 1)], b2e[:],
                                     start=True, stop=True)
                    if i % 2:
                        last.then_inc(gt_ready, 1)

                def expert(e, buf, g):
                    pe.wait_ge(ld_we[buf], 32 * g + 32)
                    for f in range(FC):
                        if f >= 4:
                            if f % 2 == 0:
                                pe.wait_ge(relu_a, 4 * e + (f // 2 - 1))
                            else:
                                pe.wait_ge(relu_v, 4 * e + (f // 2 - 1))
                        for c in range(DC):
                            last = pe.matmul(ps[:, f % 4], WE1[buf][:, c, P * f:P * (f + 1)], XT[:, c],
                                             start=(c == 0), stop=(c == DC - 1))
                        last.then_inc(f_ready, 1)
                    for i in range(NT):
                        pe.wait_ge(y1_taken, NT * e + (i + 1))
                        for f in range(FC):
                            if i == 0:
                                if f % 2 == 0:
                                    pe.wait_ge(relu_a, 4 * e + (f // 2 + 1))
                                else:
                                    pe.wait_ge(relu_v, 4 * e + (f // 2 + 1))
                            last = pe.matmul(ps[:, 4 + i, 0:D], HF[:, f, P * i:P * (i + 1)], WE2[buf][:, f],
                                             start=(f == 0), stop=(f == FC - 1))
                        last.then_inc(y1_ready, 1)
                    pe.wait_ge(y1_ready, NT * e + NT)
                    pe.sem_inc(we_used, 1)

                with pe.Fori(0, E1 // 2) as g:
                    for r in range(2):
                        expert(2 * g + r, r, g)


STAGES = 6


def kernel(x, ctx_1024, fside_1xSxS2_0, L0_xattn_W1, L0_xattn_b1, L0_xattn_W2, L0_xattn_b2, L0_attn_Wq, L0_attn_Wk,
           L0_attn_Wv, L0_attn_Wb, L0_attn_Wo, L0_attn_conv_q, L0_attn_conv_k, L0_attn_conv_v, L0_attn_o_norm_w,
           L0_ffn_gate_w, L0_ffn_expert_bias, L0_ffn_w_gate, L0_ffn_w_up, L0_ffn_w_down, L0_ffn_shared_gate_w,
           L0_ffn_shared_up_w, L0_ffn_shared_down_w, L1_xattn_w_sim, L1_xattn_b_sim, L1_xattn_W_qv, L1_xattn_b_qv,
           L1_attn_Wq, L1_attn_bq, L1_attn_Wk, L1_attn_bk, L1_attn_Wv, L1_attn_bv, L1_attn_Wo, L1_attn_bo,
           L1_ffn_Wr, L1_ffn_br, L1_ffn_W1, L1_ffn_b1, L1_ffn_W2, L1_ffn_b2):
    import numpy as np
    import concourse.bacc as bacc
    from concourse.bass_utils import run_bass_kernel_spmd

    a = lambda v: np.asarray(v)

    def chunked(w):
        w = a(w)
        *lead, r, n = w.shape
        return np.moveaxis(w.reshape(*lead, r // P, P, n), -3, -2)

    def turned(w):
        return np.swapaxes(a(w), -1, -2)

    def columns(v):
        return a(v).reshape(-1, P).T

    def taps(w):
        return chunked(w).reshape(P, DC * TAPS)

    def spread(v):
        return np.broadcast_to(a(v).reshape(1, -1), (P, a(v).size))

    arrays = {
        "x": chunked(a(x).reshape(T, D)),
        "ctx_n": np.pad(a(ctx_1024), ((0, 0), (0, KT * P - KEYS), (0, 0))).reshape(NT, 2, KT, P, D).transpose(0, 3, 1, 2, 4),
        "ctx_t": a(ctx_1024).reshape(NT, 2, KEYS, DC, P).transpose(0, 4, 1, 3, 2),
        "mask": np.concatenate([a(fside_1xSxS2_0)[0]] * 2, axis=0),
        "w_small": np.stack([chunked(w) for w in (
            turned(L0_xattn_W1), turned(L0_xattn_W2), L0_xattn_W2, L0_xattn_W1,
            turned(L0_attn_Wk), turned(L0_attn_Wv), turned(L0_attn_Wq), turned(L0_attn_Wo),
            turned(L1_attn_Wq), turned(L1_attn_Wk), turned(L1_attn_Wv), turned(L1_attn_Wo))], axis=1),
        "cols": np.concatenate([
            columns(L0_xattn_b1), columns(L0_xattn_b2), taps(L0_attn_conv_k), taps(L0_attn_conv_v), taps(L0_attn_conv_q),
            np.tile(a(L0_attn_o_norm_w), HC).reshape(P, 1), np.zeros((P, 1), np.float32), columns(L1_xattn_w_sim),
            columns(L1_attn_bq), columns(L1_attn_bk), columns(a(L1_ffn_b1).reshape(-1))], axis=1),
        "rows": np.concatenate([spread(v) for v in (
            L1_xattn_b_qv, L1_attn_bv, L1_attn_bo, L0_ffn_expert_bias, L1_ffn_br, L1_xattn_b_sim)], axis=1),
        "narrow": np.concatenate([chunked(turned(w)) for w in (L0_attn_Wb, L0_ffn_gate_w, L1_ffn_Wr)], axis=2),
        "wqv": chunked(L1_xattn_W_qv),
        "w_ffn0": np.stack([
            chunked(turned(np.concatenate([a(w), a(shared)[None]], axis=0)))
            for w, shared in ((L0_ffn_w_gate, L0_ffn_shared_gate_w), (L0_ffn_w_up, L0_ffn_shared_up_w),
                              (L0_ffn_w_down, L0_ffn_shared_down_w))], axis=2),
        "w_ffn1": np.concatenate([
            chunked(turned(L1_ffn_W1)).reshape(E1, P, DC * F1), chunked(turned(L1_ffn_W2)).reshape(E1, P, FC * D)], axis=2),
        "b2": a(L1_ffn_b2),
    }
    arrays = {k: np.ascontiguousarray(v) for k, v in arrays.items()}
    nc = bacc.Bacc("TRN2", target_bir_lowering=False, num_devices=1)
    args = [nc.dram_tensor(f"in_{k}", v.shape, F32, kind="ExternalInput").ap() for k, v in arrays.items()]
    args.append(nc.dram_tensor("out", (P, NT, D), F32, kind="ExternalOutput").ap())
    perceiver(nc, *args, STAGES)
    r = run_bass_kernel_spmd(nc, [{f"in_{k}": v for k, v in arrays.items()}], core_ids=[0])
    return np.ascontiguousarray(a(r.results[0]["out"]).transpose(1, 0, 2)).reshape(B, S, D)
```

```python
from contextlib import ExitStack

import concourse.bass as bass
from concourse import mybir

F32 = mybir.dt.float32
F32R = mybir.dt.float32r
ALU = mybir.AluOpType
ACT = mybir.ActivationFunctionType
AX = mybir.AxisListType

P = 128
B, S, D = 8, 64, 256
T = B * S
NT = T // P
DC = D // P
KEYS = 1601
KT = -(-KEYS // P)
BANK = 512
KB4 = -(-KEYS // BANK)
H, HD = 16, 16
HC = H // DC
TAPS = 4
E0 = 16
E1, F1 = 8, 1024
FC = F1 // P
OVER = (T - 1) // P
NB = E1 + OVER
ROUTE = 2.826
SCALE = D ** -0.5
UNROLL = 8
GROUP = 4
STEPS = 6
CUT = -1.0e30

W1T, W2T, W2N, W1N, AK, AV, AQ, AO, SQ, SK, SV, SO = range(12)
C_B1, C_B2, C_CONV, C_ON, C_S1, C_S2, C_S3, C_BQ, C_BK, C_F1 = 0, 2, 4, 28, 30, 32, 34, 36, 38, 40
NCOLS = C_F1 + E1 * FC
XCOLS = C_F1 + NB * FC
R_QV, R_BV, R_BO, R_EB, R_BR, R_SIM = 0, 256, 512, 768, 784, 792
NROWS = 793
N_BETA, N_GATE, N_ROUTE, NNARROW = 0, 16, 32, 40


PAIR = [0, 1, 2, 3, 2, 3, 0, 1]
LOADS = [1, 1, 2, 2, 2, 2, 3, 3]


def keys_of(j, width):
    return min(KEYS, (j + 1) * width) - j * width


def perceiver(nc, x_in, ctx_n, ctx_t, mask_in, w_small, cols_in, rows_in, narrow_in, wqv_in,
              w_ffn0, w_ffn1, b2_in, out, stages):
    with ExitStack() as ctx:
        def sb(name, shape):
            return ctx.enter_context(nc.sbuf_tensor(name, shape, F32))

        def sem(name):
            return ctx.enter_context(nc.semaphore(name))

        X = sb("X", [P, NT, D])
        XN = sb("XN", [P, NT, D])
        XT = sb("XT", [P, DC, T])
        W = sb("W", [P, 12, DC, D])
        cols = sb("cols", [P, XCOLS])
        rows = sb("rows", [P, NROWS])
        narrow = sb("narrow", [P, DC, NNARROW])
        b2e = sb("b2e", [E1, D])
        ident = sb("ident", [P, P])
        eps5 = sb("eps5", [P, 1])
        eps6 = sb("eps6", [P, 1])
        headmask = sb("headmask", [P, HC])
        index = sb("index", [P, NT, E1])
        further = ctx.enter_context(nc.sbuf_tensor("further", [1, OVER], mybir.dt.int32))
        stats = sb("stats", [P, NT, 6])
        mv = sb("mv", [P, NT, 2])
        std = sb("std", [P, NT])
        warm = sb("warm", [P, 1])
        big_at = -(-nc.sbuf_base // 32) * 32
        big = sb("big", [P, 14336])
        CTX_T = sb("CTX_T", [P, 2, 2, DC, KEYS])
        CTX_N = sb("CTX_N", [P, 2, 2, KT, D])
        ps = ctx.enter_context(nc.psum_tensor("ps", [P, 8, BANK], F32))
        psf = ps[:].rearrange("p b n -> p (b n)")
        scratch = nc.dram_tensor("scratch", [4, B, D, S], F32, kind="Internal").ap()
        scratch_beta = nc.dram_tensor("scratch_beta", [B, H, S], F32, kind="Internal").ap()

        def cut(at, *shape):
            n = 1
            for m in shape:
                n *= m
            v = big[:, at:at + n]
            if len(shape) == 2:
                v = v.rearrange("p (a b) -> p a b", a=shape[0])
            elif len(shape) == 3:
                v = v.rearrange("p (a b c) -> p a b c", a=shape[0], b=shape[1])
            return v

        def parts(name, at, *shape):
            n = 1
            for m in shape:
                n *= m
            t = nc.alloc_sbuf_tensor_at(name, [P, n], F32R, offset=big_at + 4 * at)
            if len(shape) == 2:
                return t[:].rearrange("p (a b) -> p a b", a=shape[0])
            return t[:].rearrange("p (a b c) -> p a b c", a=shape[0], b=shape[1])

        maskP = cut(0, KEYS)
        prob = [cut(1601, KEYS), cut(3202, KEYS)]
        probT = [cut(4804, KT, P), cut(6468, KT, P)]
        QT = cut(8132, DC, T)
        HA, HB = cut(9156, DC, T), cut(10180, DC, T)
        F3, F4 = cut(9156, DC, T), cut(10180, DC, T)
        HQT = cut(11204, DC, T)
        crow = cut(12228, NT)
        mx = cut(12232, NT)
        nmx = cut(12236, NT)
        den = cut(12240, NT)
        rec = cut(12244, NT)
        batt = cut(12248, P)
        bsum = cut(12376, 2)
        bmask = cut(12378, NT, 2)
        hcb = cut(12386, DC, B)
        hq = cut(12402, D)
        battv = batt.rearrange("p (a b) -> p a b", a=2)
        Y = [[cut(1024 * z + 512 * m, B, S) for m in range(DC)] for z in range(3)]
        raw = [cut(3072 + 1024 * z, HD, S) for z in range(3)]
        KN = cut(6144, S + 1, HD)
        KB = cut(7184, S + 1, HD)
        VB = cut(8224, S + 1, HD)
        QN = cut(9264, S, HD)
        sq = cut(10288, HD, S)
        beta = cut(11312, S)
        ss = cut(11376, S)
        nk = cut(11440, S)
        nega = cut(11504, S + 1)
        qscale = cut(11570, S)
        state = [cut(11634 + 256 * r, HD, HD) for r in range(UNROLL)]
        betaT = big[0:H, 11634:11634 + T]
        kS, outer = cut(3072, HD, HD), cut(3328, HD, HD)
        rsum, wv = cut(3584, HD), cut(3600, HD)
        uu = [cut(3616, HD), cut(3632, HD)]
        O = cut(0, HD, S)
        OS = cut(1024, HD, S)
        OTr = cut(2048, DC, T)
        qS = cut(4096, GROUP * HD, HD)
        tr8, tr4, tr2 = cut(5120, GROUP * HD, 8), cut(5632, GROUP * HD, 4), cut(5888, GROUP * HD, 2)
        WG = [cut(1024 * r, 2, DC, D) for r in range(2)]
        WD = [cut(2048 + 512 * r, DC, D) for r in range(2)]
        WG_L = [parts(f"WG_L{r}", 1024 * r, 2, DC, D) for r in range(2)]
        WD_L = [parts(f"WD_L{r}", 2048 + 512 * r, DC, D) for r in range(2)]
        WG_H = [parts(f"WG_H{r}", 3072 + 1024 * r, 2, DC, D) for r in range(2)]
        WD_H = [parts(f"WD_H{r}", 5120 + 512 * r, DC, D) for r in range(2)]
        G = cut(6144, DC, T)
        sg, sel, rep = cut(7168, NT, E0), cut(7232, NT, E0), cut(7296, NT, E0)
        top8 = cut(7360, NT, 8)
        csum = cut(7392, NT)
        cw = cut(7396, NT, E0 + 1)
        HT_H = [parts(f"HT_H{r}", 7552 + 1024 * r, DC, T) for r in range(2)]
        HT_L = [parts(f"HT_L{r}", 9600 + 1024 * r, DC, T) for r in range(2)]
        XT_H, XT_L = parts("XT_H", 11648, DC, T), parts("XT_L", 12672, DC, T)
        KM = [cut(0, HC, T), cut(4096, HC, T)]
        QTT = cut(8192, DC, T)
        PA = [cut(9216, H, S), cut(10240, H, S)]
        PAT = [cut(11264, HC, P), cut(12288, HC, P)]
        ON = cut(13312, D)
        OAT = cut(13568, DC, P)
        am, asum = cut(13824, H), cut(13840, H)
        bkm = cut(13856, HC)
        XD = cut(11264, DC, B, 2 * S)
        VM = CTX_N[:].rearrange("p a b c k -> p (a b c k)")[:, 0:B * H * HD].rearrange(
            "p (b h m) -> p b h m", b=B, h=HC)
        HF = cut(0, FC, P)
        XG = [cut(1024, DC, P), cut(1280, DC, P)]
        YB = [cut(1536, D), cut(1792, D)]
        PG = [cut(2048, NT, P), cut(2560, NT, P)]
        PS = [cut(3072, T), cut(3584, T)]
        lg, oh, eq = cut(4096, NT, E1), cut(4128, NT, E1), cut(4160, NT, E1)
        lmax, lmin = cut(4192, NT), cut(4196, NT)
        ohT = big[0:E1, 4200:4200 + T]
        posrow = cut(4736, T)
        diag = cut(5248, NT, P)
        rank, over = cut(5760, NT, E1), cut(5792, NT, E1)
        more, ostart, oend, shift = cut(5824, E1), cut(5832, E1), cut(5840, E1), cut(5848, E1)
        gt3 = cut(5856, E1, OVER)
        low_more = cut(5888, E1, E1)
        ended = cut(5952, OVER, E1)
        oexp = cut(5976, OVER)
        pos = cut(5984, NT)
        posm = cut(6000, NB, NT)
        osel = cut(6048, OVER, E1)
        obias = cut(6080, FC, E1)
        ctx_nf = CTX_N[:].rearrange("p a b c k -> p (a b c k)")

        def room(at, *shape):
            n = 1
            for m in shape:
                n *= m
            v = ctx_nf[:, at:at + n]
            return v.rearrange("p (a b) -> p a b", a=shape[0]) if len(shape) == 2 else v

        before = room(2048, P)
        ones = room(2176, P)
        slots = room(2304, P)
        slotcol = room(2432, NB)
        first_slot = room(2448, NB, NT)
        lower = room(2496, E1, E1)
        own = room(2560, E1)
        full = room(2568, E1, OVER)
        order = room(2592, OVER, E1)
        jump = room(2616, E1)
        ctx_tf = CTX_T[:].rearrange("p a b c k -> p (a b c k)")
        WE1 = [ctx_tf[:, at:at + 2048].rearrange("p (c n) -> p c n", c=DC) for at in (0, 8192)]
        WE2 = [ctx_tf[:, at:at + 2048].rearrange("p (c n) -> p c n", c=FC) for at in (2048, 10240)]
        WQV = ctx_tf[:, 4096:6144].rearrange("p (c n) -> p c n", c=2 * NT)

        ld_x, ld_w, ld_mask, ld_rest = sem("ld_x"), sem("ld_w"), sem("ld_mask"), sem("ld_rest")
        ld_ct = [sem(f"ld_ct{r}") for r in range(2)]
        ld_cn = [sem(f"ld_cn{r}") for r in range(2)]
        ld_wg = [sem(f"ld_wg{r}") for r in range(2)]
        ld_wd = [sem(f"ld_wd{r}") for r in range(2)]
        ld_we = [sem(f"ld_we{r}") for r in range(2)]
        ld_wqv = sem("ld_wqv")
        consts = sem("consts")
        vec, sca, pol = sem("vec"), sem("sca"), sem("pol")
        ln_stat, ln_std, ln_xn, ln_tr, ln_xt = (sem(n) for n in ("ln_stat", "ln_std", "ln_xn", "ln_tr", "ln_xt"))
        pj_ready, pj_a, pj_v = sem("pj_ready"), sem("pj_a"), sem("pj_v")
        cr_ready, cr_taken = sem("cr_ready"), sem("cr_taken")
        sc_ready, sc_taken = sem("sc_ready"), sem("sc_taken")
        mx_ready, ex_ready, bt_ready = sem("mx_ready"), sem("ex_ready"), sem("bt_ready")
        pt_ready, pt_taken = sem("pt_ready"), sem("pt_taken")
        pv_ready, pv_taken, on_ready, on_taken = (sem(n) for n in ("pv_ready", "pv_taken", "on_ready", "on_taken"))
        xa_done, third_ready = sem("xa_done"), sem("third_ready")
        small_pe, small_v, small_a = sem("small_pe"), sem("small_v"), sem("small_a")
        ap_ready, conv_done, silu_done = sem("ap_ready"), sem("conv_done"), sem("silu_done")
        first_tap = sem("first_tap")
        y_out = [sem(f"y_out{z}") for z in range(3)]
        y_in = [sem(f"y_in{z}") for z in range(3)]
        b_ready = sem("b_ready")
        b_out, b_in = sem("b_out"), sem("b_in")
        q_sq = sem("q_sq")
        dl_v, dl_a, q_done = sem("dl_v"), sem("dl_a"), sem("q_done")
        tok, q_read, o_part = sem("tok"), sem("q_read"), sem("o_part")
        o_ready, o_out, o_in = sem("o_ready"), sem("o_out"), sem("o_in")
        gt_ready, gt_act, route_done = sem("gt_ready"), sem("gt_act"), sem("route_done")
        gu_ready, silu0, h0_done, d_ready, y0_taken = (
            sem(n) for n in ("gu_ready", "silu0", "h0_done", "d_ready", "y0_taken"))
        x_high, x_low, wg_high, wg_low, wd_high, wd_low, h_high, h_low = (
            sem(n) for n in ("x_high", "x_low", "wg_high", "wg_low", "wd_high", "wd_low", "h_high", "h_low"))
        f_ready, relu_a, relu_v, y1_ready, y1_taken = (
            sem(n) for n in ("f_ready", "relu_a", "relu_v", "y1_ready", "y1_taken"))
        room_made, pg_ready, xg_ready, xg_taken, ps_ready, put_done, further_ready = (
            sem(n) for n in ("room_made", "pg_ready", "xg_ready", "xg_taken", "ps_ready", "put_done", "further_ready"))
        qk_ready, q_taken, k_a, k_v = sem("qk_ready"), sem("q_taken"), sem("k_a"), sem("k_v")
        xd_ready, v_ready, v_taken = sem("xd_ready"), sem("v_ready"), sem("v_taken")
        as_ready, sub_done, pa_ready = sem("as_ready"), sem("sub_done"), sem("pa_ready")
        at_ready, at_a = sem("at_ready"), sem("at_a")
        ao_ready, aon_ready, aot_ready, aoc_ready, ay_ready, ay_taken = (
            sem(n) for n in ("ao_ready", "aon_ready", "aot_ready", "aoc_ready", "ay_ready", "ay_taken"))
        stored = sem("stored")

        block = ctx.enter_context(nc.Block())

        def w_of(n, c, m):
            return W[:, n, c, m * P:(m + 1) * P]

        def column(at):
            return cols[:, at:at + 1] if isinstance(at, int) else cols[:, bass.ds(at, 1)]

        def bcast(v, shape):
            return v.rearrange("p (n o) -> p n o", o=1).to_broadcast(shape)

        def bcast_mid(v, shape):
            return v.rearrange("p (o n) -> p o n", o=1).to_broadcast(shape)

        @block.sync
        def _(sp):
            sp.dma_start(X[:], x_in).then_inc(ld_x, 16)
            sp.dma_start(W[:, 0:4], w_small[:, 0:4]).then_inc(ld_w, 16)
            sp.dma_start(cols[:, 0:NCOLS], cols_in).then_inc(ld_w, 16)
            for r in range(2):
                sp.dma_start(CTX_T[:, r], ctx_t[r]).then_inc(ld_ct[r], 16)
                if r == 0:
                    sp.dma_start(maskP, mask_in).then_inc(ld_mask, 16)
                    sp.dma_start(rows[:], rows_in).then_inc(ld_mask, 16)
                sp.dma_start(CTX_N[:, r], ctx_n[r]).then_inc(ld_cn[r], 16)
            def context_t(n):
                sp.wait_ge(sc_ready, KB4 * (n - 1))
                sp.dma_start(CTX_T[:, n % 2], ctx_t[PAIR[n]]).then_inc(ld_ct[n % 2], 16)

            def context_n(n):
                sp.wait_ge(pv_ready, n - 1)
                sp.dma_start(CTX_N[:, n % 2], ctx_n[PAIR[n]]).then_inc(ld_cn[n % 2], 16)

            for n in range(2, NT):
                context_t(n)
                context_n(n)
            sp.dma_start(W[:, 4:12], w_small[:, 4:12]).then_inc(ld_rest, 16)
            sp.dma_start(narrow[:], narrow_in).then_inc(ld_rest, 16)
            sp.dma_start(b2e[:], b2_in).then_inc(ld_rest, 16)
            if stages > 1:
                for z in range(3):
                    if z == 1:
                        sp.wait_ge(small_a, 1)
                        sp.dma_start(scratch_beta.rearrange("b h t -> h b t"),
                                     betaT.rearrange("h (b t) -> h b t", b=B)).then_inc(b_out, 16)
                    for m in range(DC):
                        sp.wait_ge(silu_done, 2 * z + m + 1)
                        sp.dma_start(scratch[z, :, m * P:(m + 1) * P, :].rearrange("b c t -> c b t"),
                                     Y[z][m]).then_inc(y_out[z], 16)
                    sp.wait_ge(y_out[z], 32)
                    sp.dma_start(raw[z], scratch[z].rearrange("b (h d) t -> (b h) d t", d=HD)).then_inc(y_in[z], 16)
                    if z == 1:
                        sp.wait_ge(b_out, 16)
                        sp.dma_start(beta, scratch_beta.rearrange("b h t -> (b h) t")).then_inc(b_in, 16)
                sp.wait_ge(o_ready, 1)
                sp.dma_start(scratch[3].rearrange("b (h m) t -> (b h) m t", m=HD), O).then_inc(o_out, 16)
                sp.wait_ge(o_out, 16)
                for m in range(DC):
                    sp.dma_start(OTr[:, m].rearrange("p (b t) -> p b t", b=B),
                                 scratch[3, :, m * P:(m + 1) * P, :].rearrange("b c t -> c b t")).then_inc(o_in, 16)
            if stages > 2:
                sp.wait_ge(xa_done, 2)
                def weights0(e, r, src):
                    if not isinstance(e, int) or e > 1:
                        sp.wait_ge(gu_ready, 2 * e - 2)
                    sp.dma_start(WG[r], src[:, 0:2]).then_inc(ld_wg[r], 16)
                    if not isinstance(e, int) or e > 1:
                        sp.wait_ge(d_ready, 2 * e + 1)
                    sp.dma_start(WD[r], src[:, 2]).then_inc(ld_wd[r], 16)

                for r in range(2):
                    weights0(r, r, w_ffn0[r])
                with sp.Fori(1, E0 // 2) as g:
                    for r in range(2):
                        weights0(2 * g + r, r, w_ffn0[bass.ds(2 * g + r, 1)].rearrange("e p a b c -> p (e a) b c"))
                weights0(E0, 0, w_ffn0[E0])
            if stages > 3:
                sp.wait_ge(xa_done, 3)
                for n in range(NT + 2, 2 * NT):
                    context_t(n)
                for n in range(NT + 2, 2 * NT):
                    context_n(n)
                sp.wait_ge(sc_ready, KB4 * (2 * NT - 1))
                sp.dma_start(WQV, wqv_in).then_inc(ld_wqv, 16)
            if stages > 5:
                def weights(b, src):
                    r = b % 2
                    sp.dma_start(WE1[r], src[:, 0:2048].rearrange("p (c n) -> p c n", c=DC)).then_inc(ld_we[r], 16)
                    sp.dma_start(WE2[r], src[:, 2048:4096].rearrange("p (c n) -> p c n", c=FC)).then_inc(ld_we[r], 16)

                for b in range(2):
                    sp.wait_ge(sc_ready, KB4 * (2 * NT - 1 + b))
                    weights(b, w_ffn1[b])
                with sp.Fori(1, E1 // 2) as g:
                    for r in range(2):
                        sp.wait_ge(y1_ready, 2 * g + (r - 1))
                        src = w_ffn1[bass.ds(2 * g + r, 1)].rearrange("e p n -> p (e n)")
                        sp.dma_start(WE1[r], src[:, 0:2048].rearrange("p (c n) -> p c n", c=DC)).then_inc(ld_we[r], 16)
                        sp.dma_start(WE2[r], src[:, 2048:4096].rearrange("p (c n) -> p c n", c=FC)).then_inc(ld_we[r], 16)
                sp.wait_ge(further_ready, 1)
                for j in range(OVER):
                    e = sp.value_load(further[:, j:j + 1], min_val=0, max_val=E1 - 1)
                    sp.wait_ge(y1_ready, E1 + j - 1)
                    weights(E1 + j, w_ffn1[bass.ds(e, 1)].rearrange("e p n -> p (e n)"))
            sp.wait_ge(xa_done, stages)
            sp.dma_start(out, X[:]).then_inc(stored, 16)
            sp.wait_ge(stored, 16)

        @block.gpsimd
        def _(pool):
            n = [0]

            def chain(ins):
                n[0] += 1
                ins.then_inc(pol, 1)
                pool.wait_ge(pol, n[0])

            pool.memset(eps5[:], 1e-5).then_inc(consts, 1)
            pool.memset(eps6[:], 1e-6).then_inc(consts, 1)
            chain(pool.memset(ident[:], 0.0))
            pool.affine_select(out=ident[:], in_=ident[:], compare_op=ALU.not_equal, fill=1.0, base=0,
                               pattern=[[-1, P]], channel_multiplier=1).then_inc(consts, 1)
            chain(pool.memset(headmask[:], 1.0))
            chain(pool.affine_select(out=headmask[:], in_=headmask[:], compare_op=ALU.is_ge, fill=0.0, base=0,
                                     pattern=[[-HD, HC]], channel_multiplier=1))
            pool.affine_select(out=headmask[:], in_=headmask[:], compare_op=ALU.is_ge, fill=0.0, base=HD - 1,
                               pattern=[[HD, HC]], channel_multiplier=-1).then_inc(consts, 1)
            pool.iota(index[:], pattern=[[0, NT], [1, E1]], base=-E1, channel_multiplier=0,
                      allow_small_or_imprecise_dtypes=True).then_inc(consts, 1)
            if stages > 1:
                pool.wait_ge(y_in[2], 16)
                pool.tensor_copy(QN.rearrange("p t d -> p d t"), raw[2]).then_inc(q_done, 1)
                pool.wait_ge(q_done, 1)
                pool.wait_ge(q_sq, 1)
                pool.sem_inc(q_read, 1)
                pool.sem_inc(o_part, 1)
                with pool.Fori(0, S // UNROLL) as g:
                    for half in range(UNROLL // GROUP):
                        part = g * 10 + (5 * half + 1)
                        pool.wait_ge(o_part, part)
                        for r in range(GROUP):
                            t = UNROLL * g + GROUP * half + r
                            pool.wait_ge(tok, STEPS * t + 8)
                            pool.tensor_tensor(qS[:, HD * r:HD * (r + 1)], state[GROUP * half + r],
                                               QN[:, bass.ds(t, 1)].to_broadcast([P, HD, HD]),
                                               ALU.mult).then_inc(q_read, 1)
                        pool.wait_ge(q_read, UNROLL * g + (GROUP * (half + 1) + 1))
                        pool.tensor_tensor(tr8, qS[:, :, 0:8], qS[:, :, 8:16], ALU.add).then_inc(o_part, 1)
                        pool.wait_ge(o_part, part + 1)
                        pool.tensor_tensor(tr4, tr8[:, :, 0:4], tr8[:, :, 4:8], ALU.add).then_inc(o_part, 1)
                        pool.wait_ge(o_part, part + 2)
                        pool.tensor_tensor(tr2, tr4[:, :, 0:2], tr4[:, :, 2:4], ALU.add).then_inc(o_part, 1)
                        pool.wait_ge(o_part, part + 3)
                        pair = tr2.rearrange("p (t m) d -> p t m d", t=GROUP)
                        pool.tensor_tensor(O[:, :, bass.ds(UNROLL * g + GROUP * half, GROUP)].rearrange("p m t -> p t m"),
                                           pair[:, :, :, 0], pair[:, :, :, 1], ALU.add).then_inc(o_part, 2)

            if stages > 2:
                def low_gate(e, r):
                    pool.wait_ge(wg_high, e + 1)
                    pool.tensor_tensor(WG_L[r], WG[r], WG_H[r].bitcast(F32), ALU.subtract).then_inc(wg_low, 1)

                def low_down(e, r):
                    pool.wait_ge(wd_high, e + 1)
                    pool.tensor_tensor(WD_L[r], WD[r], WD_H[r].bitcast(F32), ALU.subtract).then_inc(wd_low, 1)

                low_gate(0, 0)
                low_gate(1, 1)
                with pool.Fori(0, E0 // 2 - 1) as g:
                    for r in range(2):
                        low_down(2 * g + r, r)
                        low_gate(2 * g + (r + 2), r)
                low_down(E0 - 2, 0)
                low_gate(E0, 0)
                low_down(E0 - 1, 1)
                low_down(E0, 0)

            if stages > 4:
                pool.wait_ge(ln_xt, 10)
                for c in range(DC):
                    pool.tensor_copy(XD[:, c].rearrange("p b (o z) -> p b o z", o=2),
                                     XT[:, c].rearrange("p (b o z) -> p b o z", b=B, o=1).to_broadcast(
                                         [P, B, 2, S])).then_inc(xd_ready, 1)
            if stages > 5:
                def count(v, pattern, base=0, channel_multiplier=0):
                    pool.iota(v, pattern=pattern, base=base, channel_multiplier=channel_multiplier,
                              allow_small_or_imprecise_dtypes=True).then_inc(room_made, 1)

                chain(pool.memset(before, 1.0))
                pool.affine_select(out=before, in_=before, compare_op=ALU.is_gt, fill=0.0, base=0,
                                   pattern=[[1, P]], channel_multiplier=-1).then_inc(room_made, 1)
                chain(pool.memset(lower, 1.0))
                pool.affine_select(out=lower, in_=lower, compare_op=ALU.is_gt, fill=0.0, base=0,
                                   pattern=[[1, E1], [-1, E1]], channel_multiplier=0).then_inc(room_made, 1)
                pool.memset(ones, 1.0).then_inc(room_made, 1)
                count(slots, [[1, P]])
                count(slotcol, [[P, NB]], channel_multiplier=1)
                count(first_slot, [[P, NB], [0, NT]])
                count(own, [[P, E1]])
                count(full, [[0, E1], [P, OVER]], base=P)
                count(order, [[1, OVER], [0, E1]])
                count(jump, [[-P, E1]], base=P * (E1 - 1))

        @block.scalar
        def _(act):
            n = [0]

            def chain(ins):
                n[0] += 1
                ins.then_inc(sca, 1)
                act.wait_ge(sca, n[0])

            act.wait_ge(consts, 2)

            def tables(func):
                act.activation(warm[:], eps5[:], func).then_inc(sca, 1)
                n[0] += 1
                act.wait_ge(sca, n[0])

            def norm(k, func=None):
                tables(ACT.Sqrt)
                act.wait_ge(ln_stat, k + 1)
                act.activation(std[:], mv[:, :, 1], ACT.Sqrt, bias=eps5[:]).then_inc(ln_std, 1)
                if func is not None:
                    tables(func)
                act.wait_ge(ln_tr, 2 * k + 1)
                act.activation(XT[:, 0], ps[:, 6], ACT.Copy).then_inc(ln_xt, 1)

            def cross(s):
                def exp(p):
                    n = NT * s + p
                    act.wait_ge(mx_ready, n + 1)
                    act.activation(prob[p % 2], prob[p % 2], ACT.Exp, bias=nmx[:, p:p + 1],
                                   accum_out=den[:, p:p + 1]).then_inc(ex_ready, 1)

                exp(0)
                for p in range(NT):
                    n = NT * s + p
                    for g in range(4):
                        act.wait_ge(pt_ready, 4 * n + g + 1)
                        w = min(4, KT - 4 * g)
                        for j in range(w):
                            k = keys_of(4 * g + j, P)
                            if j == 0 or k < P:
                                full = [i for i in range(w) if keys_of(4 * g + i, P) == P]
                                if j == 0 and full:
                                    last = act.activation(probT[p % 2][:, 4 * g:4 * g + len(full)],
                                                          ps[:, 4 + g % 2, 0:P * len(full)].rearrange(
                                                              "p (a b) -> p a b", b=P), ACT.Copy)
                                if k < P:
                                    last = act.activation(probT[p % 2][0:k, 4 * g + j],
                                                          ps[0:k, 4 + g % 2, P * j:P * (j + 1)], ACT.Copy)
                        last.then_inc(pt_taken, 1)
                    if p + 1 < NT:
                        exp(p + 1)
                    elif s:
                        act.wait_ge(small_v, 1)
                        act.activation(batt[0:NT], batt[0:NT], ACT.Exp).then_inc(small_a, 1)
                    if s:
                        act.wait_ge(on_ready, p + 1)
                        q = P * PAIR[n]
                        act.activation(HQT[:, :, q:q + P], ps[:, 7, 0:D].rearrange("p (c q) -> p c q", c=DC),
                                       ACT.Copy).then_inc(on_taken, 1)

            norm(0, ACT.Exp)
            act.wait_ge(ld_w, 32)
            for k, (dst, bias, scale) in enumerate(((HA, C_B1, 1.0), (HB, C_B2, 1.0), (HA, None, 1.0), (QT, None, SCALE))):
                act.wait_ge(pj_ready, 2 * k + 1)
                if bias is None:
                    act.activation(dst[:, 0], ps[:, 2 * (k % 2)], ACT.Copy, scale=scale).then_inc(pj_a, 1)
                else:
                    act.activation(dst[:, 0], ps[:, 2 * (k % 2)], ACT.Identity,
                                   bias=cols[:, bias:bias + 1]).then_inc(pj_a, 1)
            cross(0)
            if stages > 1:
                norm(1, ACT.Sigmoid)

                def tap(k):
                    z, m = divmod(k, 2)
                    c = C_CONV + 8 * z + 4 * m + TAPS - 1
                    act.wait_ge(ap_ready, k + 1)
                    act.activation(Y[z][m], ps[:, k].rearrange("p (b t) -> p b t", b=B), ACT.Copy,
                                   scale=cols[:, c:c + 1]).then_inc(first_tap, 1)

                def silu_of(k):
                    z, m = divmod(k, 2)
                    act.wait_ge(conv_done, k + 1)
                    act.activation(Y[z][m], Y[z][m], ACT.Silu).then_inc(silu_done, 1)

                tap(0)
                tap(1)
                act.wait_ge(b_ready, 1)
                act.activation(betaT, ps[0:H, 6], ACT.Sigmoid).then_inc(small_a, 1)
                tap(2)
                silu_of(0)
                tap(3)
                silu_of(1)
                tap(4)
                silu_of(2)
                tap(5)
                for k in range(3, 6):
                    silu_of(k)
                act.wait_ge(dl_v, 1)
                act.activation(nk, ss, ACT.Sqrt).then_inc(dl_a, 1)
                act.wait_ge(y_in[2], 16)
                act.activation(OS, raw[2], ACT.Square).then_inc(q_sq, 1)
                act.wait_ge(dl_v, 2)
                act.activation(nk, ss, ACT.Sqrt).then_inc(dl_a, 1)
                act.wait_ge(dl_v, 3)
                act.activation(nk, ss, ACT.Sqrt, bias=eps6[:], scale=1.0 / HD).then_inc(dl_a, 1)
            if stages > 2:
                norm(2, ACT.Sigmoid)
                act.wait_ge(ln_xt, 6)
                act.activation(XT_H, XT[:], ACT.Copy).then_inc(x_high, 1)

                def high_gate(r, loaded):
                    act.wait_ge(ld_wg[r], loaded)
                    act.activation(WG_H[r], WG[r], ACT.Copy).then_inc(wg_high, 1)

                def hidden(e, r, loaded):
                    for m in range(DC):
                        act.wait_ge(gu_ready, 2 * e + (m + 1))
                        act.wait_ge(h_low, 2 * e + (m + 1))
                        act.activation(G[:, m], ps[:, 2 * m], ACT.Silu).then_inc(silu0, 1)
                    act.wait_ge(d_ready, 2 * e + 1)
                    for m in range(DC):
                        act.wait_ge(h0_done, 2 * e + (m + 1))
                        act.activation(HT_H[r][:, m], G[:, m], ACT.Copy).then_inc(h_high, 1)
                    act.wait_ge(ld_wd[r], loaded)
                    act.activation(WD_H[r], WD[r], ACT.Copy).then_inc(wd_high, 1)

                high_gate(0, 16)
                act.wait_ge(gt_ready, 1)
                act.activation(sg, ps[:, 4, 0:NT * E0].rearrange("p (a b) -> p a b", a=NT), ACT.Sigmoid).then_inc(gt_act, 1)
                high_gate(1, 16)
                with act.Fori(0, E0 // 2 - 1) as g:
                    for r in range(2):
                        hidden(2 * g + r, r, 16 * g + 16)
                        high_gate(r, 16 * g + 32)
                hidden(E0 - 2, 0, 8 * E0)
                high_gate(0, 8 * E0 + 16)
                hidden(E0 - 1, 1, 8 * E0)
                hidden(E0, 0, 8 * E0 + 16)
            if stages > 3:
                norm(3, ACT.Exp)
                cross(1)
            if stages > 4:
                norm(4, ACT.Exp)
                for m in range(DC):
                    act.wait_ge(qk_ready, m + 1)
                    act.activation(QTT[:, m], ps[:, m], ACT.Identity,
                                   bias=cols[:, C_BQ + m:C_BQ + m + 1]).then_inc(q_taken, 1)
                act.wait_ge(small_v, 2)
                act.wait_ge(qk_ready, DC + 1)
                for h in range(HC):
                    act.activation(KM[0][:, h], ps[:, 2], ACT.Identity, scale=headmask[:, h:h + 1],
                                   bias=bkm[:, h:h + 1]).then_inc(k_a, 1)
                def weights_of(i):
                    act.wait_ge(sub_done, i + 1)
                    act.activation(PA[i % 2], PA[i % 2], ACT.Exp, scale=HD ** -0.5).then_inc(pa_ready, 1)

                def turned_result(i):
                    act.wait_ge(aot_ready, i + 1)
                    if i:
                        act.wait_ge(ay_ready, i)
                    act.activation(OAT, ps[:, 5, 0:D].rearrange("p (a b) -> p a b", b=P), ACT.Copy).then_inc(aoc_ready, 1)

                weights_of(0)
                for i in range(NT):
                    for k in range(2):
                        act.wait_ge(at_ready, 2 * i + k + 1)
                        act.activation(PAT[i % 2][:, 4 * k:4 * k + 4], ps[:, 2 + k].rearrange("p (a b) -> p a b", b=P),
                                       ACT.Copy).then_inc(at_a, 1)
                    if i:
                        turned_result(i - 1)
                    if i + 1 < NT:
                        weights_of(i + 1)
                turned_result(NT - 1)
            if stages > 5:
                norm(5)
                act.wait_ge(route_done, 2)
                def body(b, r):
                    for k in range(2):
                        act.wait_ge(f_ready, 4 * b + (2 * k + 1))
                        for i in range(2):
                            f = 4 * k + i
                            last = act.activation(HF[:, f], ps[:, 4 * k, P * i:P * (i + 1)], ACT.Relu,
                                                  bias=column(FC * b + (C_F1 + f)))
                        last.then_inc(relu_a, 1)
                    if not (isinstance(b, int) and b == NB - 1):
                        act.wait_ge(xg_ready, b + 2)
                        act.activation(XG[1 - r], ps[:, 2, 0:DC * P].rearrange("p (c q) -> p c q", c=DC),
                                       ACT.Copy).then_inc(xg_taken, 1)
                    act.wait_ge(y1_ready, b + 1)
                    act.activation(YB[r], ps[:, 3, 0:D], ACT.Copy).then_inc(y1_taken, 1)

                act.wait_ge(xg_ready, 1)
                act.activation(XG[0], ps[:, 2, 0:DC * P].rearrange("p (c q) -> p c q", c=DC),
                               ACT.Copy).then_inc(xg_taken, 1)
                body(0, 0)
                act.wait_ge(ps_ready, 3)
                with act.Fori(0, E1 // 2) as g:
                    for r in range(2):
                        body(2 * g + (r + 1), 1 - r)
                for b in range(E1 + 1, NB):
                    body(b, b % 2)

        @block.vector
        def _(dve):
            n = [0]

            def chain(ins):
                n[0] += 1
                ins.then_inc(vec, 1)
                dve.wait_ge(vec, n[0])

            def norm(k):
                for i in range(NT):
                    dve.bn_stats(stats[:, i], X[:, i]).then_inc(vec, 1)
                    n[0] += 1
                dve.wait_ge(vec, n[0])
                for i in range(NT):
                    last = dve.bn_aggr(mv[:, i], stats[:, i])
                last.then_inc(ln_stat, 1)
                dve.wait_ge(ln_std, k + 1)
                chain(dve.reciprocal(std[:], std[:]))
                for i in range(NT):
                    dve.tensor_scalar(XN[:, i], X[:, i], mv[:, i, 0:1], std[:, i:i + 1], ALU.subtract,
                                      ALU.mult).then_inc(ln_xn, 1)
                dve.wait_ge(ln_tr, 2 * k + 2)
                dve.tensor_copy(XT[:, 1], ps[:, 7]).then_inc(ln_xt, 1)

            def third(p):
                dve.wait_ge(on_taken, p + 1)
                q = slice(P * PAIR[NT + p], P * (PAIR[NT + p] + 1))
                dve.tensor_tensor(F3[:, :, q], XT[:, :, q], HQT[:, :, q], ALU.mult).then_inc(third_ready, 1)

            def cross(s, row_weights=None):
                def scores(p):
                    k = NT * s + p
                    i = PAIR[k]
                    for j in range(KB4):
                        w = keys_of(j, BANK)
                        at = slice(BANK * j, BANK * j + w)
                        dve.wait_ge(sc_ready, KB4 * k + j + 1)
                        if s == 0:
                            dve.scalar_tensor_tensor(prob[p % 2][:, at], ps[:, j, 0:w], crow[:, i:i + 1], maskP[:, at],
                                                     ALU.add, ALU.add).then_inc(sc_taken, 1)
                        else:
                            dve.tensor_scalar(prob[p % 2][:, at], ps[:, j, 0:w], crow[:, i:i + 1], None,
                                              ALU.add).then_inc(sc_taken, 1)
                    dve.wait_ge(sc_taken, KB4 * (k + 1))
                    chain(dve.reduce_max(mx[:, i:i + 1], prob[p % 2], axis=AX.X))
                    dve.tensor_scalar(nmx[:, p:p + 1], mx[:, i:i + 1], -1.0, None, ALU.mult).then_inc(mx_ready, 1)

                def finish(p):
                    k = NT * s + p
                    i = PAIR[k]
                    dve.wait_ge(ex_ready, k + 1)
                    chain(dve.reciprocal(rec[:, p:p + 1], den[:, p:p + 1]))
                    dve.wait_ge(pv_ready, k + 1)
                    if s == 0:
                        dve.scalar_tensor_tensor(X[:, i], ps[:, 6, 0:D], rec[:, p:p + 1], X[:, i],
                                                 ALU.mult, ALU.add).then_inc(pv_taken, 1)
                    else:
                        if p:
                            dve.wait_ge(on_ready, p)
                        dve.tensor_scalar(hq, ps[:, 6, 0:D], rec[:, p:p + 1], None, ALU.mult).then_inc(pv_taken, 1)

                scores(0)
                for p in range(NT):
                    if p + 1 < NT:
                        scores(p + 1)
                    elif s:
                        row_weights()
                    finish(p)
                    if s and p:
                        third(p - 1)
                if s == 0:
                    dve.wait_ge(pv_taken, NT)

            dve.wait_ge(ld_x, 16)
            norm(0)
            dve.wait_ge(ld_w, 32)
            for k, (dst, bias) in enumerate(((HA, C_B1), (HB, C_B2), (HA, None), (QT, None))):
                dve.wait_ge(pj_ready, 2 * k + 2)
                if bias is None:
                    dve.tensor_scalar(dst[:, 1], ps[:, 2 * (k % 2) + 1], SCALE if k == 3 else 1.0, None,
                                      ALU.mult).then_inc(pj_v, 1)
                else:
                    dve.tensor_scalar(dst[:, 1], ps[:, 2 * (k % 2) + 1], cols[:, bias + 1:bias + 2], None,
                                      ALU.add).then_inc(pj_v, 1)
            dve.wait_ge(cr_ready, 1)
            chain(dve.tensor_scalar(crow, ps[:, 7, 0:NT], SCALE, None, ALU.mult))
            dve.wait_ge(ld_mask, 32)
            cross(0)
            dve.sem_inc(xa_done, 1)

            if stages > 1:
                norm(1)
                dve.wait_ge(ld_rest, 48)
                for k in range(6):
                    z, m = divmod(k, 2)
                    c = C_CONV + 8 * z + 4 * m
                    dve.wait_ge(first_tap, k + 1)
                    pre = ps[:, k].rearrange("p (b t) -> p b t", b=B)
                    for back in range(1, TAPS):
                        ins = dve.scalar_tensor_tensor(Y[z][m][:, :, back:S], pre[:, :, 0:S - back],
                                                       cols[:, c + TAPS - 1 - back:c + TAPS - back],
                                                       Y[z][m][:, :, back:S], ALU.mult, ALU.add)
                        if back < TAPS - 1:
                            chain(ins)
                        else:
                            ins.then_inc(conv_done, 1)
                dve.wait_ge(y_in[0], 16)
                chain(dve.tensor_tensor(sq, raw[0], raw[0], ALU.mult))
                dve.reduce_sum(ss, sq.rearrange("p d t -> p t d"), axis=AX.X).then_inc(dl_v, 1)
                for v in (KB, VB):
                    chain(dve.memset(v[:, S:S + 1], 0.0))
                chain(dve.memset(nega[:, S:S + 1], 0.0))
                dve.wait_ge(y_in[1], 16)
                dve.wait_ge(b_in, 16)
                chain(dve.tensor_tensor(VB[:, 0:S].rearrange("p t m -> p m t"), raw[1],
                                        bcast_mid(beta, [P, HD, S]), ALU.mult))
                dve.wait_ge(dl_a, 1)
                chain(dve.tensor_scalar(nk, nk, 1e-6, None, ALU.max))
                chain(dve.reciprocal(nk, nk))
                chain(dve.tensor_tensor(KN[:, 0:S].rearrange("p t d -> p d t"), raw[0],
                                        bcast_mid(nk, [P, HD, S]), ALU.mult))
                chain(dve.tensor_tensor(KB[:, 0:S], KN[:, 0:S], bcast(beta, [P, S, HD]), ALU.mult))
                sqt = sq.rearrange("p d t -> p (d t)").rearrange("p (t d) -> p t d", d=HD)
                chain(dve.tensor_tensor(sqt[:, 0:S - 1], KB[:, 1:S], KN[:, 0:S - 1], ALU.mult))
                chain(dve.reduce_sum(nega[:, 1:S], sqt[:, 0:S - 1], axis=AX.X))
                chain(dve.tensor_scalar(nega[:, 1:S], nega[:, 1:S], -1.0, None, ALU.mult))
                dve.memset(state[UNROLL - 1], 0.0).then_inc(tok, 2)
                dve.wait_ge(tok, 2)
                dve.tensor_copy(uu[0], VB[:, 0]).then_inc(tok, 1)
                with dve.Fori(0, S // UNROLL) as g:
                    for r in range(UNROLL):
                        t = UNROLL * g + r
                        base = (STEPS * UNROLL) * g + STEPS * r + 3
                        old, new = state[(r - 1) % UNROLL], state[r]
                        u, unext = uu[r % 2], uu[(r + 1) % 2]
                        dve.wait_ge(tok, base - 1)
                        dve.tensor_tensor(kS, old, KB[:, bass.ds(t + 1, 1)].to_broadcast([P, HD, HD]),
                                          ALU.mult).then_inc(tok, 1)
                        dve.wait_ge(tok, base)
                        dve.tensor_tensor(outer, bcast(u, [P, HD, HD]),
                                          KN[:, bass.ds(t, 1)].to_broadcast([P, HD, HD]), ALU.mult).then_inc(tok, 1)
                        dve.wait_ge(tok, base + 1)
                        dve.reduce_sum(rsum, kS, axis=AX.X).then_inc(tok, 1)
                        dve.scalar_tensor_tensor(wv, u, nega[:, bass.ds(t + 1, 1)],
                                                 VB[:, bass.ds(t + 1, 1)].rearrange("p o m -> p (o m)"),
                                                 ALU.mult, ALU.add).then_inc(tok, 1)
                        if r == 0:
                            dve.wait_ge(q_read, UNROLL * g + 1)
                        dve.wait_ge(tok, base + 2)
                        dve.tensor_tensor(new, old, outer, ALU.add).then_inc(tok, 1)
                        dve.wait_ge(tok, base + 4)
                        dve.tensor_tensor(unext, wv, rsum, ALU.subtract).then_inc(tok, 1)
                dve.wait_ge(q_sq, 1)
                dve.reduce_sum(ss, OS.rearrange("p d t -> p t d"), axis=AX.X).then_inc(dl_v, 1)
                dve.wait_ge(dl_a, 2)
                chain(dve.tensor_scalar(nk, nk, 1e-6, None, ALU.max))
                chain(dve.reciprocal(nk, nk))
                chain(dve.tensor_scalar(qscale, nk, HD ** -0.5, None, ALU.mult))
                chain(dve.tensor_tensor(beta, qscale, qscale, ALU.mult))
                dve.wait_ge(o_part, 10 * (S // UNROLL) + 1)
                chain(dve.tensor_tensor(OS, O, O, ALU.mult))
                chain(dve.reduce_sum(ss, OS.rearrange("p m t -> p t m"), axis=AX.X))
                dve.tensor_tensor(ss, ss, beta, ALU.mult).then_inc(dl_v, 1)
                dve.wait_ge(dl_a, 3)
                chain(dve.reciprocal(nk, nk))
                chain(dve.tensor_tensor(nk, nk, qscale, ALU.mult))
                dve.tensor_tensor(O, O, bcast_mid(nk, [P, HD, S]), ALU.mult).then_inc(o_ready, 1)
                for m in range(DC):
                    dve.wait_ge(o_in, 32)
                    chain(dve.tensor_scalar(OTr[:, m], OTr[:, m], cols[:, C_ON:C_ON + 1], None, ALU.mult))
                dve.sem_inc(o_ready, 1)
                for i in range(NT):
                    dve.wait_ge(ap_ready, 7 + i)
                    chain(dve.tensor_tensor(X[:, i], ps[:, i, 0:D], X[:, i], ALU.add))
                dve.sem_inc(xa_done, 1)

            if stages > 2:
                norm(2)
                dve.wait_ge(x_high, 1)
                dve.tensor_tensor(XT_L, XT[:], XT_H.bitcast(F32), ALU.subtract).then_inc(x_low, 1)
                dve.wait_ge(gt_act, 1)
                chain(dve.tensor_tensor(sel, sg, bcast_mid(rows[:, R_EB:R_EB + E0], [P, NT, E0]), ALU.add))
                for i in range(NT):
                    chain(dve.max(top8[:, i], sel[:, i]))
                    chain(dve.match_replace(rep[:, i], top8[:, i], sel[:, i], CUT))
                chain(dve.tensor_tensor(rep, sel, rep, ALU.not_equal))
                chain(dve.tensor_tensor(cw[:, :, 0:E0], sg, rep, ALU.mult))
                chain(dve.reduce_sum(csum, cw[:, :, 0:E0], axis=AX.X))
                chain(dve.reciprocal(csum, csum))
                chain(dve.tensor_scalar(csum, csum, ROUTE, None, ALU.mult))
                chain(dve.tensor_tensor(cw[:, :, 0:E0], cw[:, :, 0:E0], bcast(csum, [P, NT, E0]), ALU.mult))
                chain(dve.memset(cw[:, :, E0:E0 + 1], 1.0))

                def split(e, r):
                    for m in range(DC):
                        dve.wait_ge(silu0, 2 * e + (m + 1))
                        dve.tensor_tensor(G[:, m], ps[:, 2 * m + 1], G[:, m], ALU.mult).then_inc(h0_done, 1)
                    for m in range(DC):
                        dve.wait_ge(h_high, 2 * e + (m + 1))
                        dve.tensor_tensor(HT_L[r][:, m], G[:, m], HT_H[r][:, m].bitcast(F32),
                                          ALU.subtract).then_inc(h_low, 1)

                def weigh(e, two_e):
                    for i in range(NT):
                        if i % 2 == 0:
                            dve.wait_ge(d_ready, two_e + (i // 2 + 4))
                        w = cw[:, i, bass.ds(e, 1)] if not isinstance(e, int) else cw[:, i, e:e + 1]
                        dve.scalar_tensor_tensor(X[:, i], ps[:, 4 + i // 2, D * (i % 2):D * (i % 2 + 1)], w, X[:, i],
                                                 ALU.mult, ALU.add).then_inc(y0_taken, 1)

                dve.sem_inc(h_low, 2)
                split(0, 0)
                dve.sem_inc(y0_taken, 1)
                with dve.Fori(0, E0 // 2) as g:
                    for r in range(2):
                        e = 2 * g + r
                        split(e + 1, 1 - r)
                        dve.wait_ge(y0_taken, 8 * g + (4 * r + 1))
                        weigh(e, 4 * g + 2 * r)
                dve.wait_ge(y0_taken, 4 * E0 + 1)
                weigh(E0, 2 * E0)
                dve.wait_ge(y0_taken, 4 * (E0 + 1) + 1)
                dve.sem_inc(xa_done, 1)

            if stages > 3:
                norm(3)
                dve.wait_ge(ln_xt, 8)
                for c in range(DC):
                    dve.tensor_scalar(QT[:, c], XT[:, c], cols[:, C_S3 + c:C_S3 + c + 1],
                                      cols[:, C_S2 + c:C_S2 + c + 1], ALU.mult, ALU.add).then_inc(pj_v, 1)
                dve.wait_ge(cr_ready, 2)
                chain(dve.tensor_scalar(crow, ps[:, 7, 0:NT], rows[:, R_SIM:R_SIM + 1], None, ALU.add))
                for i in range(NT):
                    chain(dve.tensor_tensor(X[:, i], X[:, i], rows[:, R_QV:R_QV + D], ALU.add))
                chain(dve.memset(bmask, 0.0))

                def row_weights():
                    dve.wait_ge(small_pe, 1)
                    pm = ps[0:NT, 0, 0:P].rearrange("p (a b) -> p a b", a=2)
                    chain(dve.reduce_max(bsum[0:NT], pm, axis=AX.X))
                    dve.tensor_tensor(battv[0:NT], pm, bcast(bsum[0:NT], [NT, 2, S]), ALU.subtract).then_inc(small_v, 1)
                    dve.wait_ge(small_a, 2)
                    chain(dve.reduce_sum(bsum[0:NT], battv[0:NT], axis=AX.X))
                    chain(dve.reciprocal(bsum[0:NT], bsum[0:NT]))
                    dve.tensor_tensor(battv[0:NT], battv[0:NT], bcast(bsum[0:NT], [NT, 2, S]),
                                      ALU.mult).then_inc(bt_ready, 1)

                cross(1, row_weights)
                dve.wait_ge(small_pe, 2)
                for half in range(2):
                    q = slice(S * half, S * (half + 1))
                    dve.tensor_copy(bmask[q, :, half], ps[q, 1, 0:NT]).then_inc(bt_ready, 1)
                third(NT - 1)
                dve.wait_ge(small_pe, 3)
                chain(dve.tensor_copy(hcb, ps[:, 2, 0:DC * B].rearrange("p (a b) -> p a b", a=DC)))
                for c in range(DC):
                    dve.tensor_tensor(F4[:, c].rearrange("p (b t) -> p b t", b=B),
                                      XT[:, c].rearrange("p (b t) -> p b t", b=B),
                                      bcast(hcb[:, c], [P, B, S]), ALU.mult).then_inc(bt_ready, 1)
                for i in range(NT):
                    dve.wait_ge(small_pe, 4 + i)
                    chain(dve.tensor_tensor(X[:, i], ps[:, 3 + i, 0:D], X[:, i], ALU.add))
                dve.sem_inc(xa_done, 1)

            if stages > 4:
                norm(4)
                chain(dve.tensor_scalar(bkm, headmask[:], cols[:, C_BK:C_BK + 1], None, ALU.mult))
                dve.sem_inc(small_v, 1)
                for i in range(NT):
                    chain(dve.tensor_tensor(X[:, i], X[:, i], rows[:, R_BO:R_BO + D], ALU.add))
                chain(dve.memset(VM, 0.0))
                dve.wait_ge(qk_ready, DC + 2)
                for h in range(HC):
                    dve.tensor_scalar(KM[1][:, h], ps[:, 3], cols[:, C_BK + 1:C_BK + 2],
                                      headmask[:, h:h + 1], ALU.add, ALU.mult).then_inc(k_v, 1)
                for b in range(B):
                    dve.wait_ge(v_ready, b + 1)
                    for half in range(2):
                        q = slice(S * half, S * (half + 1))
                        src = ps[q, 4 + b % 4, 0:D].rearrange("p (j h m) -> p j h m", h=2, m=HD)[:, :, half]
                        bias = rows[q, R_BV:R_BV + D].rearrange("p (j h m) -> p j h m", h=2, m=HD)[:, :, half]
                        dve.tensor_tensor(VM[q, b, :, HD * half:HD * (half + 1)], src, bias, ALU.add).then_inc(v_taken, 1)

                def scaled(i):
                    dve.wait_ge(as_ready, i + 1)
                    sc = psf[:, 0:H * S].rearrange("p (h z) -> p h z", h=H)
                    chain(dve.reduce_max(am, sc, axis=AX.X))
                    dve.tensor_tensor(PA[i % 2], sc, bcast(am, [P, H, S]), ALU.subtract).then_inc(sub_done, 1)

                def weighted(i):
                    if i:
                        dve.wait_ge(aon_ready, i)
                    chain(dve.reduce_sum(asum, PA[i % 2], axis=AX.X))
                    chain(dve.reciprocal(asum, asum))
                    dve.wait_ge(ao_ready, i + 1)
                    if i:
                        dve.wait_ge(aot_ready, i)
                    dve.tensor_tensor(ON.rearrange("p (h m) -> p h m", h=H),
                                      ps[:, 4, 0:D].rearrange("p (h m) -> p h m", h=H),
                                      bcast(asum, [P, H, HD]), ALU.mult).then_inc(aon_ready, 1)

                def add(i):
                    dve.wait_ge(ay_ready, i + 1)
                    dve.tensor_tensor(X[:, i], ps[:, 6, 0:D], X[:, i], ALU.add).then_inc(ay_taken, 1)

                scaled(0)
                for i in range(NT):
                    if i + 1 < NT:
                        scaled(i + 1)
                    dve.wait_ge(pa_ready, i + 1)
                    weighted(i)
                    if i:
                        add(i - 1)
                add(NT - 1)
                dve.wait_ge(ay_taken, NT)
                dve.sem_inc(xa_done, 1)

            if stages > 5:
                norm(5)
                dve.wait_ge(gt_ready, 2)
                chain(dve.tensor_tensor(lg, ps[:, 4, 0:NT * E1].rearrange("p (a b) -> p a b", a=NT),
                                        bcast_mid(rows[:, R_BR:R_BR + E1], [P, NT, E1]), ALU.add))
                chain(dve.reduce_max(lmax, lg, axis=AX.X))
                chain(dve.tensor_tensor(eq, lg, bcast(lmax, [P, NT, E1]), ALU.is_equal))
                chain(dve.tensor_tensor(eq, eq, index[:], ALU.mult))
                chain(dve.tensor_reduce(lmin, eq, op=ALU.min, axis=AX.X))
                chain(dve.tensor_tensor(oh, index[:], bcast(lmin, [P, NT, E1]), ALU.is_equal))
                dve.sem_inc(route_done, 1)
                dve.wait_ge(room_made, 10)
                dve.wait_ge(gt_ready, 3)
                ranks = ps[:, 4, 64:64 + NT * E1].rearrange("p (a b) -> p a b", a=NT)
                total = ps[:, 4, 96:96 + E1]
                chain(dve.tensor_tensor(gt3, bcast(total, [P, E1, OVER]), full, ALU.is_gt))
                chain(dve.reduce_sum(more, gt3, axis=AX.X))
                chain(dve.tensor_tensor(low_more, bcast_mid(more, [P, E1, E1]), lower, ALU.mult))
                chain(dve.reduce_sum(ostart, low_more, axis=AX.X))
                for ins in (dve.scalar_tensor_tensor(shift, ostart, float(P), jump, ALU.mult, ALU.add),
                            dve.tensor_tensor(oend, ostart, more, ALU.add),
                            dve.tensor_scalar(over, ranks, float(P), None, ALU.is_ge)):
                    ins.then_inc(vec, 1)
                    n[0] += 1
                chain(dve.tensor_tensor(rank, ranks, bcast_mid(own, [P, NT, E1]), ALU.add))
                chain(dve.tensor_tensor(over, over, bcast_mid(shift, [P, NT, E1]), ALU.mult))
                chain(dve.tensor_tensor(rank, rank, over, ALU.add))
                chain(dve.tensor_tensor(rank, rank, oh, ALU.mult))
                chain(dve.reduce_sum(pos, rank, axis=AX.X))
                chain(dve.tensor_tensor(posm, bcast_mid(pos, [P, NB, NT]), first_slot, ALU.subtract))

                def gather_map(b, r):
                    at = posm[:, b] if isinstance(b, int) else posm[:, bass.ds(b, 1)].rearrange("p o n -> p (o n)")
                    dve.tensor_tensor(PG[r], bcast_mid(slots, [P, NT, P]), bcast(at, [P, NT, P]),
                                      ALU.is_equal).then_inc(pg_ready, 1)

                gather_map(0, 0)
                for i in range(NT):
                    chain(dve.tensor_scalar(diag[:, i], ident[:], pos[:, i:i + 1], None, ALU.mult))
                dve.sem_inc(route_done, 1)
                dve.wait_ge(gt_ready, 4)
                chain(dve.tensor_copy(ohT, ps[0:E1, 5]))
                dve.sem_inc(route_done, 1)
                gather_map(1, 1)
                chain(dve.tensor_tensor(ended, bcast_mid(oend, [P, OVER, E1]), order, ALU.is_le))
                chain(dve.reduce_sum(oexp, ended, axis=AX.X))
                chain(dve.tensor_scalar(oexp, oexp, float(E1 - 1), None, ALU.min))
                dve.tensor_copy(further[:], oexp[0:1]).then_inc(further_ready, 1)
                dve.wait_ge(gt_ready, 5)
                dve.tensor_copy(posrow, ps[:, 5]).then_inc(ps_ready, 1)
                dve.wait_ge(ps_ready, 1)

                def body(b, r):
                    for k in range(2):
                        dve.wait_ge(f_ready, 4 * b + (2 * k + 2))
                        for i in range(2):
                            f = 4 * k + 2 + i
                            last = dve.tensor_scalar(HF[:, f], ps[:, 4 * k + 1, P * i:P * (i + 1)],
                                                     column(FC * b + (C_F1 + f)), 0.0, ALU.add, ALU.max)
                        last.then_inc(relu_v, 1)
                    at = slotcol[:, b:b + 1] if isinstance(b, int) else slotcol[:, bass.ds(b, 1)]
                    if not isinstance(b, int) or b > 1:
                        dve.wait_ge(put_done, b)
                    dve.tensor_scalar(PS[r], posrow, at, None, ALU.is_equal).then_inc(ps_ready, 1)
                    if not isinstance(b, int) or b + 2 < NB:
                        dve.wait_ge(xg_ready, b + 1)
                        gather_map(b + 2, r)

                body(0, 0)
                chain(dve.tensor_scalar(oexp, oexp, float(-E1), None, ALU.add))
                chain(dve.tensor_tensor(osel, bcast(oexp, [P, OVER, E1]), bcast_mid(index[:, 0], [P, OVER, E1]),
                                        ALU.is_equal))
                for j in range(OVER):
                    chain(dve.tensor_tensor(obias, cols[:, C_F1:NCOLS].rearrange("p (e f) -> p f e", e=E1),
                                            bcast_mid(osel[:, j], [P, FC, E1]), ALU.mult))
                    at = NCOLS + FC * j
                    chain(dve.reduce_sum(cols[:, at:at + FC], obias, axis=AX.X))
                dve.sem_inc(ps_ready, 1)
                with dve.Fori(0, E1 // 2) as g:
                    for r in range(2):
                        body(2 * g + (r + 1), 1 - r)
                for b in range(E1 + 1, NB):
                    body(b, b % 2)
                dve.wait_ge(put_done, NB + 1)
                for i in range(0, NT, 2):
                    chain(dve.tensor_tensor(X[:, i:i + 2].rearrange("p a b -> p (a b)"), ps[:, 6 + i // 2],
                                            X[:, i:i + 2].rearrange("p a b -> p (a b)"), ALU.add))
                dve.sem_inc(xa_done, 1)

        @block.tensor
        def _(pe):
            pe.wait_ge(consts, 5)

            def norm(k):
                for c in range(DC):
                    for i in range(NT):
                        if c == 0:
                            pe.wait_ge(ln_xn, NT * k + i + 1)
                        last = pe.transpose(ps[:, 6 + c, P * i:P * (i + 1)], XN[:, i, P * c:P * (c + 1)], ident[:])
                    last.then_inc(ln_tr, 1)
                pe.wait_ge(ln_xt, 2 * k + 2)

            def linear(dst, w, src, m):
                for c in range(DC):
                    last = pe.matmul(dst, w_of(w, c, m), src[:, c], start=(c == 0), stop=(c == DC - 1))
                return last

            def turn(s, p):
                pe.wait_ge(pv_taken, NT * s + p + 1)
                if p:
                    pe.wait_ge(on_taken, p)
                for c in range(DC):
                    last = pe.transpose(ps[:, 7, P * c:P * (c + 1)], hq[:, P * c:P * (c + 1)], ident[:])
                last.then_inc(on_ready, 1)

            def cross(s):
                def scores(p):
                    k = NT * s + p
                    pe.wait_ge(ld_ct[k % 2], 16 * LOADS[k])
                    for j in range(KB4):
                        w = keys_of(j, BANK)
                        if k:
                            pe.wait_ge(sc_taken, KB4 * (k - 1) + j + 1)
                        for c in range(DC):
                            for half in range(2):
                                q = P * PAIR[k] + S * half
                                last = pe.matmul(ps[S * half:S * (half + 1), j, 0:w], QT[:, c, q:q + S],
                                                 CTX_T[:, k % 2, half, c, BANK * j:BANK * j + w],
                                                 start=(c == 0), stop=(c == DC - 1))
                        last.then_inc(sc_ready, 1)

                scores(0)
                for p in range(NT):
                    k = NT * s + p
                    if p + 1 < NT:
                        scores(p + 1)
                    if s and p:
                        turn(s, p - 1)
                    if s and p == NT - 1:
                        pe.wait_ge(mx_ready, 2 * NT)
                        pe.transpose(ps[0:NT, 0, 0:P], mx, ident[:]).then_inc(small_pe, 1)
                    pe.wait_ge(ex_ready, k + 1)
                    for g in range(4):
                        if 4 * k + g >= 2:
                            pe.wait_ge(pt_taken, 4 * k + g - 1)
                        for j in range(4 * g, min(KT, 4 * g + 4)):
                            w = keys_of(j, P)
                            last = pe.transpose(ps[0:w, 4 + g % 2, P * (j % 4):P * (j % 4 + 1)],
                                                prob[p % 2][:, P * j:P * j + w], ident[:])
                        last.then_inc(pt_ready, 1)
                    pe.wait_ge(ld_cn[k % 2], 16 * LOADS[k])
                    pe.wait_ge(pt_taken, 4 * k + 4)
                    if k:
                        pe.wait_ge(pv_taken, k)
                    for j in range(KT):
                        w = keys_of(j, P)
                        for half in range(2):
                            q = slice(S * half, S * (half + 1))
                            last = pe.matmul(ps[q, 6, 0:D], probT[p % 2][0:w, j, q], CTX_N[0:w, k % 2, half, j],
                                             start=(j == 0), stop=(j == KT - 1))
                    last.then_inc(pv_ready, 1)

            norm(0)
            pe.wait_ge(ld_w, 32)
            for k, (w, src) in enumerate(((W1T, XT), (W2T, HA), (W2N, HB), (W1N, HA))):
                if k:
                    pe.wait_ge(pj_a, k)
                    pe.wait_ge(pj_v, k)
                for m in range(DC):
                    linear(ps[:, 2 * (k % 2) + m], w, src, m).then_inc(pj_ready, 1)
            for i in range(NT):
                q = slice(P * i, P * (i + 1))
                terms = [(HA, C_B1, c) for c in range(DC)] + [(HB, C_B2, c) for c in range(DC)]
                for k, (src, col, c) in enumerate(terms):
                    last = pe.matmul(ps[:, 7, i:i + 1], src[:, c, q], cols[:, col + c:col + c + 1],
                                     start=(k == 0), stop=(k == 3))
            last.then_inc(cr_ready, 1)
            pe.wait_ge(pj_a, 4)
            pe.wait_ge(pj_v, 4)
            cross(0)

            if stages > 1:
                norm(1)
                pe.wait_ge(ld_rest, 48)
                for z, w in enumerate((AK, AV, AQ)):
                    for m in range(DC):
                        linear(ps[:, 2 * z + m], w, XT, m).then_inc(ap_ready, 1)
                    if z == 0:
                        for c in range(DC):
                            last = pe.matmul(ps[0:H, 6], narrow[:, c, N_BETA:N_BETA + H], XT[:, c],
                                             start=(c == 0), stop=(c == DC - 1))
                        last.then_inc(b_ready, 1)
                pe.wait_ge(o_ready, 2)
                for i in range(NT):
                    for c in range(DC):
                        last = pe.matmul(ps[:, i, 0:D], OTr[:, c, P * i:P * (i + 1)], W[:, AO, c],
                                         start=(c == 0), stop=(c == DC - 1))
                    last.then_inc(ap_ready, 1)

            def gates(col, width, at):
                for i in range(NT):
                    for c in range(DC):
                        last = pe.matmul(ps[:, 4, width * i:width * (i + 1)], XT[:, c, P * i:P * (i + 1)],
                                         narrow[:, c, col:col + width], start=(c == 0), stop=(c == DC - 1))
                last.then_inc(gt_ready, 1)

            if stages > 2:
                norm(2)
                gates(N_GATE, E0, 4)
                pe.wait_ge(gt_act, 1)
                pe.wait_ge(x_low, 1)
                pe.sem_inc(d_ready, 3)

                def three(dst, high, low, x_h, x_l):
                    terms = [(w, x) for c in range(DC) for w, x in ((high(c), x_h(c)), (high(c), x_l(c)), (low(c), x_h(c)))]
                    for k, (w, x) in enumerate(terms):
                        last = pe.matmul(dst, w, x, start=(k == 0), stop=(k == len(terms) - 1))
                    return last

                def gate_up(e, r):
                    pe.wait_ge(wg_low, e + 1)
                    for m in range(DC):
                        if not isinstance(e, int) or e:
                            pe.wait_ge(h0_done, 2 * e + (m - 1))
                        f = slice(P * m, P * (m + 1))
                        for part in range(2):
                            last = three(ps[:, 2 * m + part], lambda c: WG_H[r][:, part, c, f],
                                         lambda c: WG_L[r][:, part, c, f], lambda c: XT_H[:, c], lambda c: XT_L[:, c])
                        last.then_inc(gu_ready, 1)

                def down(e, r):
                    pe.wait_ge(wd_low, e + 1)
                    pe.wait_ge(h_low, 2 * e + 4)
                    pe.wait_ge(y0_taken, 4 * e + 1)
                    for i in range(NT):
                        q = slice(P * i, P * (i + 1))
                        last = three(ps[:, 4 + i // 2, D * (i % 2):D * (i % 2 + 1)], lambda c: HT_H[r][:, c, q],
                                     lambda c: HT_L[r][:, c, q], lambda c: WD_H[r][:, c], lambda c: WD_L[r][:, c])
                        if i % 2:
                            last.then_inc(d_ready, 1)

                gate_up(0, 0)
                with pe.Fori(0, E0 // 2) as g:
                    for r in range(2):
                        e = 2 * g + r
                        gate_up(e + 1, 1 - r)
                        down(e, r)
                down(E0, 0)

            if stages > 3:
                norm(3)
                for i in range(NT):
                    for c in range(DC):
                        last = pe.matmul(ps[:, 7, i:i + 1], XT[:, c, P * i:P * (i + 1)],
                                         cols[:, C_S1 + c:C_S1 + c + 1], start=(c == 0), stop=(c == DC - 1))
                last.then_inc(cr_ready, 1)
                pe.wait_ge(pj_v, 6)
                cross(1)
                pe.wait_ge(bt_ready, 1)
                pe.transpose(ps[:, 1, 0:NT], batt[0:NT], ident[0:NT, 0:NT]).then_inc(small_pe, 1)
                turn(1, NT - 1)
                pe.wait_ge(ld_wqv, 16)

                def project(part, f):
                    for i in range(NT):
                        for c in range(DC):
                            last = pe.matmul(ps[:, 3 + i, 0:D], f[:, c, P * i:P * (i + 1)], WQV[:, DC * part + c],
                                             start=(part == 0 and c == 0), stop=(part == 3 and c == DC - 1))
                        if part == 3:
                            last.then_inc(small_pe, 1)

                project(0, XT)
                pe.wait_ge(bt_ready, 3)
                for c in range(DC):
                    for i in range(NT):
                        at = B * c + 2 * i
                        last = pe.matmul(ps[:, 2, at:at + 2], XN[:, i, P * c:P * (c + 1)], bmask[:, i],
                                         start=True, stop=True)
                last.then_inc(small_pe, 1)
                pe.wait_ge(third_ready, NT)
                project(1, HQT)
                project(2, F3)
                pe.wait_ge(bt_ready, 5)
                project(3, F4)

            if stages > 4:
                norm(4)
                for m in range(DC):
                    linear(ps[:, m], SQ, XT, m).then_inc(qk_ready, 1)
                for m in range(DC):
                    linear(ps[:, 2 + m], SK, XT, m).then_inc(qk_ready, 1)
                pe.wait_ge(xd_ready, DC)
                for b in range(B):
                    if b >= 4:
                        pe.wait_ge(v_taken, 2 * (b - 3))
                    for c in range(DC):
                        last = pe.matmul(ps[:, 4 + b % 4, 0:D], XD[:, c, b], W[:, SV, c], start=(c == 0), stop=(c == DC - 1))
                    last.then_inc(v_ready, 1)
                pe.wait_ge(q_taken, DC)
                pe.wait_ge(k_a, HC)
                pe.wait_ge(k_v, HC)
                pe.wait_ge(v_taken, 2 * B)

                def scores(i):
                    if i:
                        pe.wait_ge(sub_done, i)
                    for m in range(DC):
                        for half in range(2):
                            q = P * i + S * half
                            last = pe.matmul(ps[S * half:S * (half + 1), m], QTT[:, m, q:q + S],
                                             KM[m][:, :, q:q + S], start=True, stop=True)
                    last.then_inc(as_ready, 1)

                def turn_weights(i):
                    pe.wait_ge(pa_ready, i + 1)
                    if i:
                        pe.wait_ge(at_a, 2 * i)
                    flat = PA[i % 2].rearrange("p h z -> p (h z)")
                    for j in range(HC):
                        last = pe.transpose(ps[:, 2 + j // 4, P * (j % 4):P * (j % 4 + 1)], flat[:, P * j:P * (j + 1)],
                                            ident[:])
                        if j % 4 == 3:
                            last.then_inc(at_ready, 1)

                def turn_result(i):
                    pe.wait_ge(aon_ready, i + 1)
                    for c in range(DC):
                        last = pe.transpose(ps[:, 5, P * c:P * (c + 1)], ON[:, P * c:P * (c + 1)], ident[:])
                    last.then_inc(aot_ready, 1)

                def weigh_values(i):
                    pe.wait_ge(at_a, 2 * i + 2)
                    for j in range(HC):
                        for half in range(2):
                            last = pe.matmul(ps[S * half:S * (half + 1), 4, 32 * j:32 * (j + 1)],
                                             PAT[i % 2][:, j, S * half:S * (half + 1)], VM[:, 2 * i + half, j],
                                             start=True, stop=True)
                    last.then_inc(ao_ready, 1)

                def project(i):
                    pe.wait_ge(aoc_ready, i + 1)
                    if i:
                        pe.wait_ge(ay_taken, i)
                    for c in range(DC):
                        last = pe.matmul(ps[:, 6, 0:D], OAT[:, c], W[:, SO, c], start=(c == 0), stop=(c == DC - 1))
                    last.then_inc(ay_ready, 1)

                scores(0)
                for i in range(NT):
                    if i + 1 < NT:
                        scores(i + 1)
                    turn_weights(i)
                    if i:
                        turn_result(i - 1)
                    weigh_values(i)
                    if i:
                        project(i - 1)
                turn_result(NT - 1)
                project(NT - 1)

            if stages > 5:
                norm(5)
                gates(N_ROUTE, E1, 4)
                pe.wait_ge(route_done, 1)
                pe.wait_ge(room_made, 10)
                for i in range(NT + 1):
                    for k in range(min(i + 1, NT)):
                        at = 64 + E1 * i
                        last = pe.matmul(ps[:, 4, at:at + E1], before if k == i else ones, oh[:, k],
                                         start=(k == 0), stop=(k == min(i, NT - 1)))
                last.then_inc(gt_ready, 1)
                for i in range(NT):
                    last = pe.transpose(ps[0:E1, 5, P * i:P * (i + 1)], oh[:, i], ident[:])
                last.then_inc(gt_ready, 1)

                def gather(b, r):
                    pe.wait_ge(pg_ready, b + 1)
                    for c in range(DC):
                        for i in range(NT):
                            last = pe.matmul(ps[:, 2, P * c:P * (c + 1)], XN[:, i, P * c:P * (c + 1)], PG[r][:, i],
                                             start=(i == 0), stop=(i == NT - 1))
                    last.then_inc(xg_ready, 1)

                def put(b, r, final):
                    pe.wait_ge(y1_taken, b + 1)
                    pe.wait_ge(ps_ready, b + 2 if isinstance(b, int) and b == 0 else b + 3)
                    for i in range(NT):
                        last = pe.matmul(ps[:, 6 + i // 2, D * (i % 2):D * (i % 2 + 1)], PS[r][:, P * i:P * (i + 1)],
                                         YB[r], start=False, stop=final, skip_group_check=True)
                    last.then_inc(put_done, 1)

                def body(b, r, load):
                    pe.wait_ge(xg_taken, b + 1)
                    pe.wait_ge(ld_we[r], load)
                    for k, bank in enumerate((0, 1, 4, 5)):
                        for i in range(2):
                            f = 2 * k + i
                            for c in range(DC):
                                last = pe.matmul(ps[:, bank, P * i:P * (i + 1)], WE1[r][:, c, P * f:P * (f + 1)],
                                                 XG[r][:, c], start=(c == 0), stop=(c == DC - 1))
                        last.then_inc(f_ready, 1)
                    if not isinstance(b, int) or b + 1 < NB:
                        gather(b + 1, 1 - r)
                    if not isinstance(b, int) or b:
                        put(b - 1, 1 - r, False)
                    for f in range(FC):
                        if f % 4 == 0:
                            pe.wait_ge(relu_a, 2 * b + (f // 4 + 1))
                        elif f % 4 == 2:
                            pe.wait_ge(relu_v, 2 * b + (f // 4 + 1))
                        last = pe.matmul(ps[:, 3, 0:D], HF[:, f], WE2[r][:, f], start=(f == 0), stop=(f == FC - 1))
                    last.then_inc(y1_ready, 1)

                gather(0, 0)
                pe.wait_ge(route_done, 3)
                for i in range(NT):
                    last = pe.matmul(ps[:, 6 + i // 2, D * (i % 2):D * (i % 2 + 1)], ohT[:, P * i:P * (i + 1)], b2e[:],
                                     start=(i % 2 == 0), stop=False, skip_group_check=True)
                last.then_inc(put_done, 1)
                for i in range(NT):
                    last = pe.matmul(ps[:, 5, P * i:P * (i + 1)], ones, diag[:, i], start=True, stop=True)
                last.then_inc(gt_ready, 1)
                pe.wait_ge(ps_ready, 1)
                body(0, 0, 32)
                with pe.Fori(0, E1 // 2) as g:
                    for r in range(2):
                        body(2 * g + (r + 1), 1 - r, 32 * g + 32 * (r + 1))
                for b in range(E1 + 1, NB):
                    body(b, b % 2, 32 * (b // 2 + 1))
                put(NB - 1, (NB - 1) % 2, True)


STAGES = 6


def kernel(x, ctx_1024, fside_1xSxS2_0, L0_xattn_W1, L0_xattn_b1, L0_xattn_W2, L0_xattn_b2, L0_attn_Wq, L0_attn_Wk,
           L0_attn_Wv, L0_attn_Wb, L0_attn_Wo, L0_attn_conv_q, L0_attn_conv_k, L0_attn_conv_v, L0_attn_o_norm_w,
           L0_ffn_gate_w, L0_ffn_expert_bias, L0_ffn_w_gate, L0_ffn_w_up, L0_ffn_w_down, L0_ffn_shared_gate_w,
           L0_ffn_shared_up_w, L0_ffn_shared_down_w, L1_xattn_w_sim, L1_xattn_b_sim, L1_xattn_W_qv, L1_xattn_b_qv,
           L1_attn_Wq, L1_attn_bq, L1_attn_Wk, L1_attn_bk, L1_attn_Wv, L1_attn_bv, L1_attn_Wo, L1_attn_bo,
           L1_ffn_Wr, L1_ffn_br, L1_ffn_W1, L1_ffn_b1, L1_ffn_W2, L1_ffn_b2):
    import numpy as np
    import concourse.bacc as bacc
    from concourse.bass_utils import run_bass_kernel_spmd

    a = lambda v: np.asarray(v)

    def chunked(w):
        w = a(w)
        *lead, r, n = w.shape
        return np.moveaxis(w.reshape(*lead, r // P, P, n), -3, -2)

    def turned(w):
        return np.swapaxes(a(w), -1, -2)

    def columns(v):
        return a(v).reshape(-1, P).T

    def taps(w):
        return chunked(w).reshape(P, DC * TAPS)

    def spread(v):
        return np.broadcast_to(a(v).reshape(1, -1), (P, a(v).size))

    arrays = {
        "x": chunked(a(x).reshape(T, D)),
        "ctx_n": np.pad(a(ctx_1024), ((0, 0), (0, KT * P - KEYS), (0, 0))).reshape(NT, 2, KT, P, D).transpose(0, 3, 1, 2, 4),
        "ctx_t": a(ctx_1024).reshape(NT, 2, KEYS, DC, P).transpose(0, 4, 1, 3, 2),
        "mask": np.concatenate([a(fside_1xSxS2_0)[0]] * 2, axis=0),
        "w_small": np.stack([chunked(w) for w in (
            turned(L0_xattn_W1), turned(L0_xattn_W2), L0_xattn_W2, L0_xattn_W1,
            turned(L0_attn_Wk), turned(L0_attn_Wv), turned(L0_attn_Wq), turned(L0_attn_Wo),
            turned(L1_attn_Wq), turned(L1_attn_Wk), turned(L1_attn_Wv), turned(L1_attn_Wo))], axis=1),
        "cols": np.concatenate([
            columns(L0_xattn_b1), columns(L0_xattn_b2), taps(L0_attn_conv_k), taps(L0_attn_conv_v), taps(L0_attn_conv_q),
            np.tile(a(L0_attn_o_norm_w), HC).reshape(P, 1), np.zeros((P, 1), np.float32), columns(L1_xattn_w_sim),
            columns(L1_attn_bq), columns(L1_attn_bk), columns(a(L1_ffn_b1).reshape(-1))], axis=1),
        "rows": np.concatenate([spread(v) for v in (
            L1_xattn_b_qv, L1_attn_bv, L1_attn_bo, L0_ffn_expert_bias, L1_ffn_br, L1_xattn_b_sim)], axis=1),
        "narrow": np.concatenate([chunked(turned(w)) for w in (L0_attn_Wb, L0_ffn_gate_w, L1_ffn_Wr)], axis=2),
        "wqv": chunked(L1_xattn_W_qv),
        "w_ffn0": np.stack([
            chunked(turned(np.concatenate([a(w), a(shared)[None]], axis=0)))
            for w, shared in ((L0_ffn_w_gate, L0_ffn_shared_gate_w), (L0_ffn_w_up, L0_ffn_shared_up_w),
                              (L0_ffn_w_down, L0_ffn_shared_down_w))], axis=2),
        "w_ffn1": np.concatenate([
            chunked(turned(L1_ffn_W1)).reshape(E1, P, DC * F1), chunked(turned(L1_ffn_W2)).reshape(E1, P, FC * D)], axis=2),
        "b2": a(L1_ffn_b2),
    }
    arrays = {k: np.ascontiguousarray(v) for k, v in arrays.items()}
    nc = bacc.Bacc("TRN2", target_bir_lowering=False, num_devices=1)
    args = [nc.dram_tensor(f"in_{k}", v.shape, F32, kind="ExternalInput").ap() for k, v in arrays.items()]
    args.append(nc.dram_tensor("out", (P, NT, D), F32, kind="ExternalOutput").ap())
    perceiver(nc, *args, STAGES)
    r = run_bass_kernel_spmd(nc, [{f"in_{k}": v for k, v in arrays.items()}], core_ids=[0])
    return np.ascontiguousarray(a(r.results[0]["out"]).transpose(1, 0, 2)).reshape(B, S, D)
```

```python
from contextlib import ExitStack

import concourse.bass as bass
from concourse import mybir

F32 = mybir.dt.float32
F32R = mybir.dt.float32r
ALU = mybir.AluOpType
ACT = mybir.ActivationFunctionType
AX = mybir.AxisListType

P = 128
B, S, D = 8, 64, 256
T = B * S
NT = T // P
DC = D // P
KEYS = 1601
KT = -(-KEYS // P)
BANK = 512
KB4 = -(-KEYS // BANK)
H, HD = 16, 16
HC = H // DC
TAPS = 4
E0 = 16
E1, F1 = 8, 1024
FC = F1 // P
OVER = (T - 1) // P
NB = E1 + OVER
ROUTE = 2.826
SCALE = D ** -0.5
UNROLL = 16
STEPS_V = 3
STEPS_P = 4
TERMS = HD + 3
CUT = -1.0e30

W2T, W1N, AK, AV, AQ, AO, SQ, SK, SV, SO = range(10)
C_B1, C_B2, C_CONV, C_ON, C_S1, C_S2, C_S3, C_BQ, C_BK, C_F1 = 0, 2, 4, 28, 30, 32, 34, 36, 38, 40
NCOLS = C_F1 + E1 * FC
XCOLS = C_F1 + NB * FC
R_QV, R_BV, R_BO, R_EB, R_BR, R_SIM = 0, 256, 512, 768, 784, 792
NROWS = 793
N_BETA, N_GATE, N_ROUTE, NNARROW = 0, 16, 32, 40


PAIR = [0, 1, 2, 3, 2, 3, 0, 1]
LOADS_N = [1, 1, 2, 2, 2, 2, 3, 3]
LOADS_T = [0, 1, 1, 2, 1, 2, 2, 3]
TURN_BANKS = (4, 5, 7)
CF = 4 * (KEYS // BANK) + 1
EARLY = 8


def keys_of(j, width):
    return min(KEYS, (j + 1) * width) - j * width


def perceiver(nc, x_in, ctx_n, ctx_t, mask_in, w_small, cols_in, rows_in, narrow_in, wqv_in,
              w_ffn0, w_ffn1, b2_in, out, stages):
    with ExitStack() as ctx:
        def sb(name, shape):
            return ctx.enter_context(nc.sbuf_tensor(name, shape, F32))

        def sem(name):
            return ctx.enter_context(nc.semaphore(name))

        X = sb("X", [P, NT, D])
        XN = sb("XN", [P, NT, D])
        XT = sb("XT", [P, DC, T])
        W = sb("W", [P, 10, DC, D])
        cols = sb("cols", [P, XCOLS])
        rows = sb("rows", [P, NROWS])
        narrow = sb("narrow", [P, DC, NNARROW])
        b2e = sb("b2e", [E1, D])
        ident = sb("ident", [P, P])
        eps5 = sb("eps5", [P, 1])
        eps6 = sb("eps6", [P, 1])
        headmask = sb("headmask", [P, HC])
        index = sb("index", [P, NT, E1])
        further = ctx.enter_context(nc.sbuf_tensor("further", [1, OVER], mybir.dt.int32))
        stats = sb("stats", [P, NT, 6])
        mv = sb("mv", [P, NT, 2])
        std = sb("std", [P, NT])
        warm = sb("warm", [P, 1])
        big_at = -(-nc.sbuf_base // 32) * 32
        big = sb("big", [P, 14336])
        ctx_t_at = -(-nc.sbuf_base // 32) * 32
        CTX_T = sb("CTX_T", [P, 2, 2, DC, KEYS])
        ctx_n_at = -(-nc.sbuf_base // 32) * 32
        CTX_N = sb("CTX_N", [P, 2, 2, KT, D])
        ps = ctx.enter_context(nc.psum_tensor("ps", [P, 8, BANK], F32))
        psf = ps[:].rearrange("p b n -> p (b n)")
        scratch = nc.dram_tensor("scratch", [2, B, D, S], F32, kind="Internal").ap()
        scratch_beta = nc.dram_tensor("scratch_beta", [B, H, S], F32, kind="Internal").ap()

        def cut(at, *shape):
            n = 1
            for m in shape:
                n *= m
            v = big[:, at:at + n]
            if len(shape) == 2:
                v = v.rearrange("p (a b) -> p a b", a=shape[0])
            elif len(shape) == 3:
                v = v.rearrange("p (a b c) -> p a b c", a=shape[0], b=shape[1])
            return v

        def parts(name, at, *shape, room_at=big_at):
            n = 1
            for m in shape:
                n *= m
            t = nc.alloc_sbuf_tensor_at(name, [P, n], F32R, offset=room_at + 4 * at)
            if len(shape) == 1:
                return t[:]
            if len(shape) == 2:
                return t[:].rearrange("p (a b) -> p a b", a=shape[0])
            return t[:].rearrange("p (a b c) -> p a b c", a=shape[0], b=shape[1])

        maskP = cut(0, KEYS)
        prob = [cut(1601, KEYS), cut(3202, KEYS)]
        probT = [cut(4804, KT, P), cut(6468, KT, P)]
        QT = cut(8132, DC, T)
        W21, WFOLD = cut(9156, DC, D), cut(9668, DC, D)
        gcol, hcol, hscaled = cut(10180, DC), cut(10182, DC), cut(10440, DC)
        gwide = cut(10184, DC, P)
        F3, F4 = cut(9156, DC, T), cut(10180, DC, T)
        HQT = cut(11204, DC, T)
        crow = cut(12228, NT)
        mx = cut(12232, NT)
        nmx = cut(12236, NT)
        den = cut(12240, NT)
        rec = cut(12244, NT)
        batt = cut(12248, P)
        bsum = cut(12376, 2)
        bmask = cut(12378, NT, 2)
        hcb = cut(12386, DC, B)
        hq = cut(12402, D)
        battv = batt.rearrange("p (a b) -> p a b", a=2)
        Y = [[cut(1024 * z + 512 * m, B, S) for m in range(DC)] for z in range(3)]
        raw = [cut(3072 + 1024 * z, HD, S) for z in range(2)]
        KN = cut(5120, S + 2, HD)
        KB = cut(6176, S + 2, HD)
        VB = cut(7232, S + 2, HD)
        sq = cut(8288, HD, S)
        dot2 = cut(12808, S, HD)
        U = cut(8288, S, HD)
        beta, ss, nk = cut(9312, S), cut(9376, S), cut(9440, S)
        nega1, nega2 = cut(9504, S + 2), cut(9572, S + 2)
        state = [cut(9640 + 256 * r, HD, HD) for r in range(2)]
        terms = [cut(10152 + HD * TERMS * r, HD, TERMS) for r in range(2)]
        outer = [cut(10760 + 256 * r, HD, HD) for r in range(2)]
        uu = cut(11272, UNROLL, HD)
        qn, qscale, qs2, os = (cut(11528 + 64 * r, NT, H) for r in range(4))
        betaT = big[0:H, 11784:11784 + T]
        qsq = cut(11784, DC, T)
        QM = cut(12808, DC * HC // 2, P)
        AT = [cut(3072, H, S), cut(4096, H, S), cut(1024, H, S),
              XN[:].rearrange("p i c -> p (i c)").rearrange("p (h t) -> p h t", h=H)]
        UT = cut(11784, NT, D)
        ON1 = cut(5120, NT, D)
        OSQ = cut(7232, NT, D)
        OTr = cut(4096, DC, T)
        causal = cut(13832, S)
        WG = [cut(1024 * r, 2, DC, D) for r in range(2)]
        WD = [cut(2048 + 512 * r, DC, D) for r in range(2)]
        WG_L = [parts(f"WG_L{r}", 1024 * r, 2, DC, D) for r in range(2)]
        WD_L = [parts(f"WD_L{r}", 2048 + 512 * r, DC, D) for r in range(2)]
        WG_H = [parts(f"WG_H{r}", 3072 + 1024 * r, 2, DC, D) for r in range(2)]
        WD_H = [parts(f"WD_H{r}", 5120 + 512 * r, DC, D) for r in range(2)]
        G = cut(6144, DC, T)
        sg, sel, rep = cut(7168, NT, E0), cut(7232, NT, E0), cut(7296, NT, E0)
        top8 = cut(7360, NT, 8)
        csum = cut(7392, NT)
        cw = cut(7396, NT, E0 + 1)
        HT_H = [parts(f"HT_H{r}", 7552 + 1024 * r, DC, T) for r in range(2)]
        HT_L = [parts(f"HT_L{r}", 9600 + 1024 * r, DC, T) for r in range(2)]
        XT_H, XT_L = parts("XT_H", 11648, DC, T), parts("XT_L", 12672, DC, T)
        KM = [cut(0, HC, T), cut(4096, HC, T)]
        QTT = cut(8192, DC, T)
        PA = [cut(9216, H, S), cut(10240, H, S)]
        PAT = [cut(11264, HC, P), cut(12288, HC, P)]
        ON = cut(13312, D)
        OAT = cut(13568, DC, P)
        am, asum = cut(13824, H), cut(13840, H)
        bkm = cut(13856, HC)
        XD = cut(11264, DC, B, 2 * S)
        VM = CTX_N[:].rearrange("p a b c k -> p (a b c k)")[:, 0:B * H * HD].rearrange(
            "p (b h m) -> p b h m", b=B, h=HC)
        HF = cut(0, FC, P)
        XG = cut(1024, DC, 2 * P)
        YB = [cut(1536, D), cut(1792, D)]
        HF_H, HF_L = parts("HF_H", 2048, FC, P), parts("HF_L", 3072, FC, P)
        PG = parts("PG", 6272, NT, 2 * P)
        XN_H, XN_L = parts("XN_H", 7296, NT, D), parts("XN_L", 8320, NT, D)
        PS = [parts(f"PS{r}", 9344 + 512 * r, T) for r in range(2)]
        YB_H = [parts(f"YB_H{r}", 10368 + 256 * r, D) for r in range(2)]
        YB_L = [parts(f"YB_L{r}", 10880 + 256 * r, D) for r in range(2)]
        lg, oh, eq = cut(4096, NT, E1), cut(4128, NT, E1), cut(4160, NT, E1)
        lmax, lmin = cut(4192, NT), cut(4196, NT)
        ohT = big[0:E1, 4200:4200 + T]
        posrow = cut(4736, T)
        diag = cut(5248, NT, P)
        rank, over = cut(5760, NT, E1), cut(5792, NT, E1)
        more, ostart, oend, shift = cut(5824, E1), cut(5832, E1), cut(5840, E1), cut(5848, E1)
        gt3 = cut(5856, E1, OVER)
        low_more = cut(5888, E1, E1)
        ended = cut(5952, OVER, E1)
        oexp = cut(5976, OVER)
        pos = cut(5984, NT)
        posm = cut(6144, NB + 1, NT)
        osel = cut(6000, OVER, E1)
        obias = cut(6024, FC, E1)
        ctx_nf = CTX_N[:].rearrange("p a b c k -> p (a b c k)")

        def room(at, *shape):
            n = 1
            for m in shape:
                n *= m
            v = ctx_nf[:, at:at + n]
            return v.rearrange("p (a b) -> p a b", a=shape[0]) if len(shape) == 2 else v

        before = room(2048, P)
        ones = room(2176, P)
        slots = room(2304, P)
        slotcol = room(2432, NB)
        first_slot = room(2624, NB + 1, NT)
        lower = room(2496, E1, E1)
        own_block = room(2560, E1)
        full = room(2568, E1, OVER)
        order = room(2592, OVER, E1)
        jump = room(2616, E1)
        ctx_tf = CTX_T[:].rearrange("p a b c k -> p (a b c k)")
        WE1 = [ctx_tf[:, at:at + 2048].rearrange("p (c n) -> p c n", c=DC) for at in (0, 8192)]
        WE2 = [ctx_tf[:, at:at + 2048].rearrange("p (c n) -> p c n", c=FC) for at in (2048, 10240)]
        WE2_H = [parts(f"WE2_H{r}", 4096 + 2048 * r, FC, D, room_at=ctx_n_at) for r in range(2)]
        WE2_L = [parts(f"WE2_L{r}", at, FC, D, room_at=ctx_t_at) for r, at in ((0, 2048), (1, 10240))]
        WQV = ctx_tf[:, 4096:6144].rearrange("p (c n) -> p c n", c=2 * NT)

        ld_x, ld_w, ld_mask, ld_rest = sem("ld_x"), sem("ld_w"), sem("ld_mask"), sem("ld_rest")
        ld_ct = [sem(f"ld_ct{r}") for r in range(2)]
        ld_cn = [sem(f"ld_cn{r}") for r in range(2)]
        ld_wg = [sem(f"ld_wg{r}") for r in range(2)]
        ld_wd = [sem(f"ld_wd{r}") for r in range(2)]
        ld_we = [sem(f"ld_we{r}") for r in range(2)]
        ld_we2 = [sem(f"ld_we2{r}") for r in range(2)]
        ld_wqv = sem("ld_wqv")
        consts = sem("consts")
        vec, sca, pol = sem("vec"), sem("sca"), sem("pol")
        ln_stat, ln_std, ln_xn, ln_tr, ln_xt = (sem(n) for n in ("ln_stat", "ln_std", "ln_xn", "ln_tr", "ln_xt"))
        pj_ready, pj_a, pj_v = sem("pj_ready"), sem("pj_a"), sem("pj_v")
        cr_ready = sem("cr_ready")
        sc_ready, sc_taken = sem("sc_ready"), sem("sc_taken")
        mx_ready, ex_ready, bt_ready = sem("mx_ready"), sem("ex_ready"), sem("bt_ready")
        pt_ready, pt_taken = sem("pt_ready"), sem("pt_taken")
        ld_early, filled, emptied_a, emptied_v = (sem(n) for n in ("ld_early", "filled", "emptied_a", "emptied_v"))
        pv_ready, pv_taken, on_ready, on_taken = (sem(n) for n in ("pv_ready", "pv_taken", "on_ready", "on_taken"))
        xa_done, third_ready = sem("xa_done"), sem("third_ready")
        small_pe, small_v, small_a = sem("small_pe"), sem("small_v"), sem("small_a")
        ap_ready, conv_done, silu_done = sem("ap_ready"), sem("conv_done"), sem("silu_done")
        first_tap = sem("first_tap")
        y_out = [sem(f"y_out{z}") for z in range(2)]
        y_in = [sem(f"y_in{z}") for z in range(2)]
        b_ready = sem("b_ready")
        b_out, b_in = sem("b_out"), sem("b_in")
        q_sq, q_sum, q_norm = sem("q_sq"), sem("q_sum"), sem("q_norm")
        dl_v, dl_a = sem("dl_v"), sem("dl_a")
        ksq_done, kn_done, vb_done, dot2_done = (sem(n) for n in ("ksq_done", "kn_done", "vb_done", "dot2_done"))
        tok, tok_p, u_kept = sem("tok"), sem("tok_p"), sem("u_kept")
        causal_made, qm_ready, kq_ready, kq_taken, kq_masked = (
            sem(n) for n in ("causal_made", "qm_ready", "kq_ready", "kq_taken", "kq_masked"))
        un_ready, ut_ready, ut_taken, o_half, o_ready, os_v, os_a, on1_ready, ot_ready, ot_taken = (
            sem(n) for n in ("un_ready", "ut_ready", "ut_taken", "o_half", "o_ready", "os_v", "os_a", "on1_ready", "ot_ready",
                             "ot_taken"))
        gt_ready, gt_act, route_done = sem("gt_ready"), sem("gt_act"), sem("route_done")
        gu_ready, silu0, h0_done, d_ready, y0_taken = (
            sem(n) for n in ("gu_ready", "silu0", "h0_done", "d_ready", "y0_taken"))
        x_high, x_low, wg_high, wg_low, wd_high, wd_low, h_high, h_low = (
            sem(n) for n in ("x_high", "x_low", "wg_high", "wg_low", "wd_high", "wd_low", "h_high", "h_low"))
        f_ready, relu_a, relu_v, y1_ready = (sem(n) for n in ("f_ready", "relu_a", "relu_v", "y1_ready"))
        room_made, pg_ready, xg_ready, xg_taken, ps_ready, put_done, further_ready = (
            sem(n) for n in ("room_made", "pg_ready", "xg_ready", "xg_taken", "ps_ready", "put_done", "further_ready"))
        xn_high, xn_low, we_high, we_low, hf_high_a, hf_low, y1_high, y1_low = (
            sem(n) for n in ("xn_high", "xn_low", "we_high", "we_low", "hf_high_a", "hf_low", "y1_high", "y1_low"))
        qk_ready, q_taken, k_a, k_v = sem("qk_ready"), sem("q_taken"), sem("k_a"), sem("k_v")
        xd_ready, v_ready, v_taken = sem("xd_ready"), sem("v_ready"), sem("v_taken")
        as_ready, sub_done, pa_ready = sem("as_ready"), sem("sub_done"), sem("pa_ready")
        at_ready, at_a = sem("at_ready"), sem("at_a")
        ao_ready, aon_ready, aot_ready, aoc_ready, ay_ready, ay_taken = (
            sem(n) for n in ("ao_ready", "aon_ready", "aot_ready", "aoc_ready", "ay_ready", "ay_taken"))
        stored = sem("stored")

        block = ctx.enter_context(nc.Block())

        def w_of(n, c, m):
            return W[:, n, c, m * P:(m + 1) * P]

        def turned_context(engine, fills):
            for f in fills:
                if (f % 2 == 0) != (engine is nc.scalar):
                    continue
                engine.wait_ge(filled, f + 1)
                if f < CF - 1:
                    j, (half, c) = f // 4, divmod(f % 4, 2)
                    dst, src = CTX_T[:, 0, half, c, BANK * j:BANK * (j + 1)], ps[:, TURN_BANKS[f % 3]]
                else:
                    w = keys_of(KT - 1, P)
                    dst = CTX_T[:, 0].rearrange("p b c k -> p (b c) k")[:, :, KEYS - w:KEYS]
                    src = ps[:, TURN_BANKS[f % 3]].rearrange("p (a b) -> p a b", b=P)[:, :, 0:w]
                if engine is nc.scalar:
                    nc.scalar.activation(dst, src, ACT.Copy).then_inc(emptied_a, 1)
                else:
                    nc.vector.tensor_copy(dst, src).then_inc(emptied_v, 1)

        def column(at):
            return cols[:, at:at + 1] if isinstance(at, int) else cols[:, bass.ds(at, 1)]

        def bcast(v, shape):
            return v.rearrange("p (n o) -> p n o", o=1).to_broadcast(shape)

        def bcast_mid(v, shape):
            return v.rearrange("p (o n) -> p o n", o=1).to_broadcast(shape)

        @block.sync
        def _(sp):
            sp.dma_start(X[:], x_in).then_inc(ld_x, 16)
            sp.dma_start(W[:, 0:2], w_small[:, 0:2]).then_inc(ld_w, 16)
            sp.dma_start(cols[:, 0:NCOLS], cols_in).then_inc(ld_w, 16)
            sp.dma_start(CTX_N[:, 0, :, 0:EARLY], ctx_n[0, :, :, 0:EARLY]).then_inc(ld_early, 16)
            sp.dma_start(CTX_N[:, 0, :, EARLY:KT], ctx_n[0, :, :, EARLY:KT]).then_inc(ld_cn[0], 16)
            sp.dma_start(maskP, mask_in).then_inc(ld_mask, 16)
            sp.dma_start(CTX_T[:, 1], ctx_t[1]).then_inc(ld_ct[1], 16)
            sp.dma_start(CTX_N[:, 1], ctx_n[1]).then_inc(ld_cn[1], 16)
            def context_t(n):
                sp.wait_ge(sc_ready, KB4 * (n - 1))
                sp.dma_start(CTX_T[:, n % 2], ctx_t[PAIR[n]]).then_inc(ld_ct[n % 2], 16)

            def context_n(n):
                sp.wait_ge(pv_ready, n - 1)
                sp.dma_start(CTX_N[:, n % 2], ctx_n[PAIR[n]]).then_inc(ld_cn[n % 2], 16)

            for n in range(2, NT):
                context_t(n)
            for n in range(2, NT):
                context_n(n)
            sp.dma_start(rows[:], rows_in).then_inc(ld_rest, 16)
            sp.dma_start(W[:, 2:10], w_small[:, 2:10]).then_inc(ld_rest, 16)
            sp.dma_start(narrow[:], narrow_in).then_inc(ld_rest, 16)
            sp.dma_start(b2e[:], b2_in).then_inc(ld_rest, 16)
            if stages > 1:
                def out_of(z, m):
                    sp.wait_ge(silu_done, 2 * z + m + 1)
                    sp.dma_start(scratch[z, :, m * P:(m + 1) * P, :].rearrange("b c t -> c b t"),
                                 Y[z][m]).then_inc(y_out[z], 16)

                def back(z):
                    sp.wait_ge(y_out[z], 32)
                    sp.dma_start(raw[z], scratch[z].rearrange("b (h d) t -> (b h) d t", d=HD)).then_inc(y_in[z], 16)

                out_of(0, 0)
                out_of(0, 1)
                back(0)
                out_of(1, 0)
                out_of(1, 1)
                back(1)
                sp.wait_ge(small_a, 1)
                sp.dma_start(scratch_beta.rearrange("b h t -> h b t"),
                             betaT.rearrange("h (b t) -> h b t", b=B)).then_inc(b_out, 16)
                sp.wait_ge(b_out, 16)
                sp.dma_start(beta, scratch_beta.rearrange("b h t -> (b h) t")).then_inc(b_in, 16)
            if stages > 2:
                def weights0(e, r, src):
                    if not isinstance(e, int) or e > 1:
                        sp.wait_ge(gu_ready, 2 * e - 2)
                    sp.dma_start(WG[r], src[:, 0:2]).then_inc(ld_wg[r], 16)
                    if not isinstance(e, int) or e > 1:
                        sp.wait_ge(d_ready, 2 * e + 1)
                    sp.dma_start(WD[r], src[:, 2]).then_inc(ld_wd[r], 16)

                sp.wait_ge(kq_ready, 2 * NT)
                weights0(0, 0, w_ffn0[0])
                sp.wait_ge(o_ready, 2)
                weights0(1, 1, w_ffn0[1])
                with sp.Fori(1, E0 // 2) as g:
                    for r in range(2):
                        weights0(2 * g + r, r, w_ffn0[bass.ds(2 * g + r, 1)].rearrange("e p a b c -> p (e a) b c"))
                weights0(E0, 0, w_ffn0[E0])
            if stages > 3:
                sp.wait_ge(xa_done, 3)
                for n in range(NT + 2, 2 * NT):
                    context_t(n)
                for n in range(NT + 2, 2 * NT):
                    context_n(n)
                sp.wait_ge(sc_ready, KB4 * (2 * NT - 1))
                sp.dma_start(WQV, wqv_in).then_inc(ld_wqv, 16)
            if stages > 5:
                def first(b, src):
                    sp.dma_start(WE1[b % 2], src[:, 0:2048].rearrange("p (c n) -> p c n", c=DC)).then_inc(ld_we[b % 2], 16)

                def second(b, src):
                    sp.dma_start(WE2[b % 2], src[:, 2048:4096].rearrange("p (c n) -> p c n", c=FC)).then_inc(
                        ld_we2[b % 2], 16)

                for b in range(2):
                    sp.wait_ge(sc_ready, KB4 * (2 * NT - 1 + b))
                    first(b, w_ffn1[b])
                    second(b, w_ffn1[b])
                with sp.Fori(1, E1 // 2) as g:
                    for r in range(2):
                        src = w_ffn1[bass.ds(2 * g + r, 1)].rearrange("e p n -> p (e n)")
                        sp.wait_ge(f_ready, 8 * g + (4 * r - 4))
                        first(r, src)
                        sp.wait_ge(y1_ready, 2 * g + (r - 1))
                        second(r, src)
                sp.wait_ge(further_ready, 1)
                for b in range(E1, NB):
                    e = sp.value_load(further[:, b - E1:b - E1 + 1], min_val=0, max_val=E1 - 1)
                    src = w_ffn1[bass.ds(e, 1)].rearrange("e p n -> p (e n)")
                    sp.wait_ge(f_ready, 4 * (b - 1))
                    first(b, src)
                    sp.wait_ge(y1_ready, b - 1)
                    second(b, src)
            sp.wait_ge(xa_done, stages)
            sp.dma_start(out, X[:]).then_inc(stored, 16)
            sp.wait_ge(stored, 16)

        @block.gpsimd
        def _(pool):
            n = [0]

            def chain(ins):
                n[0] += 1
                ins.then_inc(pol, 1)
                pool.wait_ge(pol, n[0])

            pool.memset(eps5[:], 1e-5).then_inc(consts, 1)
            pool.memset(eps6[:], 1e-6).then_inc(consts, 1)
            chain(pool.memset(ident[:], 0.0))
            pool.affine_select(out=ident[:], in_=ident[:], compare_op=ALU.not_equal, fill=1.0, base=0,
                               pattern=[[-1, P]], channel_multiplier=1).then_inc(consts, 1)
            chain(pool.memset(headmask[:], 1.0))
            chain(pool.affine_select(out=headmask[:], in_=headmask[:], compare_op=ALU.is_ge, fill=0.0, base=0,
                                     pattern=[[-HD, HC]], channel_multiplier=1))
            pool.affine_select(out=headmask[:], in_=headmask[:], compare_op=ALU.is_ge, fill=0.0, base=HD - 1,
                               pattern=[[HD, HC]], channel_multiplier=-1).then_inc(consts, 1)
            pool.iota(index[:], pattern=[[0, NT], [1, E1]], base=-E1, channel_multiplier=0,
                      allow_small_or_imprecise_dtypes=True).then_inc(consts, 1)
            if stages > 1:
                chain(pool.memset(causal, 1.0))
                for half in range(2):
                    rows_of = causal[S * half:S * (half + 1)]
                    pool.affine_select(out=rows_of, in_=rows_of, compare_op=ALU.is_ge, fill=0.0, base=0,
                                       pattern=[[1, S]], channel_multiplier=-1).then_inc(causal_made, 1)
                pool.wait_ge(causal_made, 2)
                pool.wait_ge(kn_done, 1)
                pool.tensor_tensor(dot2[:, 0:S - 2], KN[:, 2:S], KN[:, 0:S - 2], ALU.mult).then_inc(dot2_done, 1)
                pool.wait_ge(y_in[1], 16)
                pool.wait_ge(b_in, 16)
                pool.wait_ge(dot2_done, 1)
                pool.tensor_tensor(VB[:, 0:S].rearrange("p t m -> p m t"), raw[1], bcast_mid(beta, [P, HD, S]),
                                   ALU.mult).then_inc(vb_done, 1)
                pool.wait_ge(vb_done, 1)
                pool.wait_ge(tok, 5)
                pool.sem_inc(tok_p, 3)
                with pool.Fori(0, S // UNROLL) as g:
                    for r in range(UNROLL):
                        t = UNROLL * g + r
                        u = uu[:, r]
                        one, two = terms[(r + 1) % 2], terms[r % 2]
                        pool.wait_ge(tok, (STEPS_V * UNROLL) * g + (STEPS_V * r + 4))
                        pool.tensor_tensor(one[:, :, HD + 1], u, nega1[:, bass.ds(t + 1, 1)].to_broadcast([P, HD]),
                                           ALU.mult).then_inc(tok_p, 1)
                        pool.tensor_tensor(outer[r % 2], bcast(u, [P, HD, HD]),
                                           KN[:, bass.ds(t, 1)].to_broadcast([P, HD, HD]), ALU.mult).then_inc(tok_p, 1)
                        pool.tensor_tensor(two[:, :, HD + 2], u, nega2[:, bass.ds(t + 2, 1)].to_broadcast([P, HD]),
                                           ALU.mult).then_inc(tok_p, 1)
                        pool.tensor_copy(two[:, :, HD], VB[:, bass.ds(t + 2, 1)].rearrange(
                            "p o m -> p (o m)")).then_inc(tok_p, 1)

            if stages > 2:
                def low_gate(e, r):
                    pool.wait_ge(wg_high, e + 1)
                    pool.tensor_tensor(WG_L[r], WG[r], WG_H[r].bitcast(F32), ALU.subtract).then_inc(wg_low, 1)

                def low_down(e, r):
                    pool.wait_ge(wd_high, e + 1)
                    pool.tensor_tensor(WD_L[r], WD[r], WD_H[r].bitcast(F32), ALU.subtract).then_inc(wd_low, 1)

                low_gate(0, 0)
                low_gate(1, 1)
                with pool.Fori(0, E0 // 2 - 1) as g:
                    for r in range(2):
                        low_down(2 * g + r, r)
                        low_gate(2 * g + (r + 2), r)
                low_down(E0 - 2, 0)
                low_gate(E0, 0)
                low_down(E0 - 1, 1)
                low_down(E0, 0)

            if stages > 4:
                pool.wait_ge(ln_xt, 10)
                for c in range(DC):
                    pool.tensor_copy(XD[:, c].rearrange("p b (o z) -> p b o z", o=2),
                                     XT[:, c].rearrange("p (b o z) -> p b o z", b=B, o=1).to_broadcast(
                                         [P, B, 2, S])).then_inc(xd_ready, 1)
            if stages > 5:
                def count(v, pattern, base=0, channel_multiplier=0):
                    pool.iota(v, pattern=pattern, base=base, channel_multiplier=channel_multiplier,
                              allow_small_or_imprecise_dtypes=True).then_inc(room_made, 1)

                chain(pool.memset(before, 1.0))
                pool.affine_select(out=before, in_=before, compare_op=ALU.is_gt, fill=0.0, base=0,
                                   pattern=[[1, P]], channel_multiplier=-1).then_inc(room_made, 1)
                chain(pool.memset(lower, 1.0))
                pool.affine_select(out=lower, in_=lower, compare_op=ALU.is_gt, fill=0.0, base=0,
                                   pattern=[[1, E1], [-1, E1]], channel_multiplier=0).then_inc(room_made, 1)
                pool.memset(ones, 1.0).then_inc(room_made, 1)
                count(slots, [[1, P]])
                count(slotcol, [[P, NB]], channel_multiplier=1)
                count(first_slot, [[P, NB + 1], [0, NT]])
                count(own_block, [[P, E1]])
                count(full, [[0, E1], [P, OVER]], base=P)
                count(order, [[1, OVER], [0, E1]])
                count(jump, [[-P, E1]], base=P * (E1 - 1))

                def low_part(b, r):
                    pool.wait_ge(we_high, b + 1)
                    pool.tensor_tensor(WE2_L[r], WE2[r], WE2_H[r].bitcast(F32), ALU.subtract).then_inc(we_low, 1)

                low_part(0, 0)
                with pool.Fori(0, NB // 2) as g:
                    for r in range(2):
                        low_part(2 * g + (r + 1), 1 - r)

        @block.scalar
        def _(act):
            n = [0]

            def chain(ins):
                n[0] += 1
                ins.then_inc(sca, 1)
                act.wait_ge(sca, n[0])

            act.wait_ge(consts, 2)

            def tables(func):
                act.activation(warm[:], eps5[:], func).then_inc(sca, 1)
                n[0] += 1
                act.wait_ge(sca, n[0])

            def deviation(k, func=None):
                tables(ACT.Sqrt)
                act.wait_ge(ln_stat, k + 1)
                act.activation(std[:], mv[:, :, 1], ACT.Sqrt, bias=eps5[:]).then_inc(ln_std, 1)
                if func is not None:
                    tables(func)

            def norm(k, func=None):
                deviation(k, func)
                turned_norm(k)

            def turned_norm(k):
                act.wait_ge(ln_tr, 2 * k + 1)
                act.activation(XT[:, 0], ps[:, 6], ACT.Copy).then_inc(ln_xt, 1)

            def cross(s):
                def exp(p):
                    n = NT * s + p
                    act.wait_ge(mx_ready, n + 1)
                    act.activation(prob[p % 2], prob[p % 2], ACT.Exp, bias=nmx[:, p:p + 1],
                                   accum_out=den[:, p:p + 1]).then_inc(ex_ready, 1)

                if s == 0:
                    turned_context(act, range(CF))
                exp(0)
                for p in range(NT):
                    n = NT * s + p
                    for g in range(4):
                        act.wait_ge(pt_ready, 4 * n + g + 1)
                        w = min(4, KT - 4 * g)
                        for j in range(w):
                            k = keys_of(4 * g + j, P)
                            if j == 0 or k < P:
                                full = [i for i in range(w) if keys_of(4 * g + i, P) == P]
                                if j == 0 and full:
                                    last = act.activation(probT[p % 2][:, 4 * g:4 * g + len(full)],
                                                          ps[:, 4 + g % 2, 0:P * len(full)].rearrange(
                                                              "p (a b) -> p a b", b=P), ACT.Copy)
                                if k < P:
                                    last = act.activation(probT[p % 2][0:k, 4 * g + j],
                                                          ps[0:k, 4 + g % 2, P * j:P * (j + 1)], ACT.Copy)
                        last.then_inc(pt_taken, 1)
                    if p + 1 < NT:
                        exp(p + 1)
                    elif s:
                        act.wait_ge(small_v, 1)
                        act.activation(batt[0:NT], batt[0:NT], ACT.Exp).then_inc(small_a, 1)
                    if s:
                        act.wait_ge(on_ready, p + 1)
                        q = P * PAIR[n]
                        act.activation(HQT[:, :, q:q + P], ps[:, 7, 0:D].rearrange("p (c q) -> p c q", c=DC),
                                       ACT.Copy).then_inc(on_taken, 1)

            deviation(0, ACT.Exp)
            act.wait_ge(pj_ready, 1)
            act.activation(W21[:, 0], ps[:, 0, 0:D], ACT.Copy).then_inc(pj_a, 1)
            turned_norm(0)
            act.wait_ge(pj_ready, 2)
            act.activation(WFOLD[:, 0], ps[:, 2, 0:D], ACT.Copy).then_inc(pj_a, 1)
            act.wait_ge(pj_v, 4)
            act.wait_ge(pj_ready, 4)
            act.activation(QT[:, 0], ps[:, 0], ACT.Identity, scale=SCALE, bias=hscaled[:, 0:1]).then_inc(pj_a, 1)
            cross(0)
            if stages > 1:
                norm(1, ACT.Silu)

                def tap(k):
                    z, m = divmod(k, 2)
                    c = C_CONV + 8 * z + 4 * m + TAPS - 1
                    act.wait_ge(ap_ready, k + 1)
                    act.activation(Y[z][m], ps[:, k].rearrange("p (b t) -> p b t", b=B), ACT.Copy,
                                   scale=cols[:, c:c + 1]).then_inc(first_tap, 1)

                def silu_of(k):
                    z, m = divmod(k, 2)
                    act.wait_ge(conv_done, k + 1)
                    act.activation(Y[z][m], Y[z][m], ACT.Silu).then_inc(silu_done, 1)

                tap(0)
                tap(1)
                for k in range(3):
                    silu_of(k)
                    tap(k + 2)
                silu_of(3)
                act.wait_ge(b_ready, 1)
                act.activation(betaT, ps[0:H, 6], ACT.Sigmoid).then_inc(small_a, 1)
                tap(5)
                act.wait_ge(y_in[0], 16)
                act.activation(sq, raw[0], ACT.Square).then_inc(ksq_done, 1)
                tables(ACT.Sqrt)
                act.wait_ge(dl_v, 1)
                act.activation(nk, ss, ACT.Sqrt).then_inc(dl_a, 1)
                silu_of(4)
                silu_of(5)
                act.wait_ge(silu_done, 6)
                act.wait_ge(b_out, 16)
                for m in range(DC):
                    act.activation(qsq[:, m].rearrange("p (b t) -> p b t", b=B), Y[2][m], ACT.Square).then_inc(q_sq, 1)
                act.wait_ge(q_sum, 1)
                act.activation(qn, ps[:, 6, 0:NT * H].rearrange("p (a b) -> p a b", a=NT), ACT.Sqrt).then_inc(q_norm, 1)
                act.wait_ge(tok, 5)
                act.sem_inc(u_kept, 1)

                def keep(g):
                    for half in range(2):
                        n8 = UNROLL // 2 * half
                        act.wait_ge(tok, STEPS_V * (UNROLL * g + n8 + UNROLL // 2 - 1) + 4)
                        act.activation(U[:, UNROLL * g + n8:UNROLL * g + n8 + UNROLL // 2],
                                       uu[:, n8:n8 + UNROLL // 2], ACT.Copy).then_inc(u_kept, 1)

                def keys_queries(k):
                    i, part = divmod(k, 2)
                    if k:
                        act.wait_ge(kq_ready, k)
                    for m in range(DC):
                        for j in range(HC // 2):
                            h = HC // 2 * part + j
                            act.activation(QM[:, HC // 2 * m + j].rearrange("p (b t) -> p b t", b=2),
                                           Y[2][m][:, 2 * i:2 * i + 2], ACT.Copy,
                                           scale=headmask[:, h:h + 1]).then_inc(qm_ready, 1)
                    act.wait_ge(kq_ready, k + 1)
                    for m in range(DC):
                        h = HC * m + HC // 2 * part
                        act.activation(AT[i][:, h:h + HC // 2],
                                       ps[:, 7, 256 * m:256 * (m + 1)].rearrange("p (h t) -> p h t", t=S),
                                       ACT.Copy).then_inc(kq_taken, 1)

                def turned_u(rows_of, k):
                    act.activation(UT[rows_of].rearrange("p i (h m) -> p m i h", m=HD)[:, 8 * k:8 * (k + 1)],
                                   ps[rows_of, k].rearrange("p (m i h) -> p m i h", m=8, i=NT),
                                   ACT.Copy).then_inc(ut_taken, 1)

                for k in range(4):
                    keys_queries(k)
                keep(0)
                for k in range(4, 2 * NT):
                    keys_queries(k)
                keep(1)
                for k in range(2):
                    act.wait_ge(ut_ready, k + 1)
                    for half in range(2):
                        turned_u(slice(S * half, S * half + S // 2), k)
                keep(2)
                keep(3)
                act.wait_ge(o_half, 1)
                for k in range(2):
                    act.wait_ge(ut_ready, k + 3)
                    turned_u(slice(0, P), k)
                for k in range(2):
                    act.wait_ge(os_v, k + 1)
                    act.activation(os[:, 2 * k:2 * k + 2], os[:, 2 * k:2 * k + 2], ACT.Sqrt, bias=eps6[:],
                                   scale=1.0 / HD).then_inc(os_a, 1)
                act.wait_ge(ot_ready, 1)
                act.activation(OTr[:, 0], ps[:, 4], ACT.Copy, scale=cols[:, C_ON:C_ON + 1]).then_inc(ot_taken, 1)
            if stages > 2:
                def high_gate(r, loaded):
                    act.wait_ge(ld_wg[r], loaded)
                    act.activation(WG_H[r], WG[r], ACT.Copy).then_inc(wg_high, 1)

                act.wait_ge(o_ready, 2)
                high_gate(0, 16)
                norm(2, ACT.Sigmoid)
                act.wait_ge(ln_xt, 6)
                act.activation(XT_H, XT[:], ACT.Copy).then_inc(x_high, 1)

                def hidden(e, r, loaded):
                    for m in range(DC):
                        act.wait_ge(gu_ready, 2 * e + (m + 1))
                        act.wait_ge(h_low, 2 * e + (m + 1))
                        act.activation(G[:, m], ps[:, 2 * m], ACT.Silu).then_inc(silu0, 1)
                    act.wait_ge(d_ready, 2 * e + 1)
                    for m in range(DC):
                        act.wait_ge(h0_done, 2 * e + (m + 1))
                        act.activation(HT_H[r][:, m], G[:, m], ACT.Copy).then_inc(h_high, 1)
                    act.wait_ge(ld_wd[r], loaded)
                    act.activation(WD_H[r], WD[r], ACT.Copy).then_inc(wd_high, 1)

                act.wait_ge(gt_ready, 1)
                act.activation(sg, ps[:, 4, 0:NT * E0].rearrange("p (a b) -> p a b", a=NT), ACT.Sigmoid).then_inc(gt_act, 1)
                high_gate(1, 16)
                with act.Fori(0, E0 // 2 - 1) as g:
                    for r in range(2):
                        hidden(2 * g + r, r, 16 * g + 16)
                        high_gate(r, 16 * g + 32)
                hidden(E0 - 2, 0, 8 * E0)
                high_gate(0, 8 * E0 + 16)
                hidden(E0 - 1, 1, 8 * E0)
                hidden(E0, 0, 8 * E0 + 16)
            if stages > 3:
                norm(3, ACT.Exp)
                cross(1)
            if stages > 4:
                norm(4, ACT.Exp)
                for m in range(DC):
                    act.wait_ge(qk_ready, m + 1)
                    act.activation(QTT[:, m], ps[:, m], ACT.Identity,
                                   bias=cols[:, C_BQ + m:C_BQ + m + 1]).then_inc(q_taken, 1)
                act.wait_ge(small_v, 2)
                act.wait_ge(qk_ready, DC + 1)
                for h in range(HC):
                    act.activation(KM[0][:, h], ps[:, 2], ACT.Identity, scale=headmask[:, h:h + 1],
                                   bias=bkm[:, h:h + 1]).then_inc(k_a, 1)
                def weights_of(i):
                    act.wait_ge(sub_done, i + 1)
                    act.activation(PA[i % 2], PA[i % 2], ACT.Exp, scale=HD ** -0.5).then_inc(pa_ready, 1)

                def turned_result(i):
                    act.wait_ge(aot_ready, i + 1)
                    if i:
                        act.wait_ge(ay_ready, i)
                    act.activation(OAT, ps[:, 5, 0:D].rearrange("p (a b) -> p a b", b=P), ACT.Copy).then_inc(aoc_ready, 1)

                weights_of(0)
                for i in range(NT):
                    for k in range(2):
                        act.wait_ge(at_ready, 2 * i + k + 1)
                        act.activation(PAT[i % 2][:, 4 * k:4 * k + 4], ps[:, 2 + k].rearrange("p (a b) -> p a b", b=P),
                                       ACT.Copy).then_inc(at_a, 1)
                    if i:
                        turned_result(i - 1)
                    if i + 1 < NT:
                        weights_of(i + 1)
                turned_result(NT - 1)
            if stages > 5:
                norm(5)
                def high_part(r, loaded):
                    act.wait_ge(ld_we2[r], loaded)
                    act.activation(WE2_H[r], WE2[r], ACT.Copy).then_inc(we_high, 1)

                def gathered(pair):
                    act.wait_ge(xg_ready, pair + 1)
                    act.activation(XG, ps[:, 2].rearrange("p (c q) -> p c q", c=DC), ACT.Copy).then_inc(xg_taken, 1)

                def body(b, r, pair, loaded):
                    for k in range(2):
                        act.wait_ge(f_ready, 4 * b + (2 * k + 1))
                        for i in range(2):
                            f = 4 * k + i
                            last = act.activation(HF[:, f], ps[:, 4 * k, P * i:P * (i + 1)], ACT.Relu,
                                                  bias=column(FC * b + (C_F1 + f)))
                        last.then_inc(relu_a, 1)
                        act.wait_ge(relu_a, 2 * b + (k + 1))
                        act.activation(HF_H[:, 4 * k:4 * k + 2], HF[:, 4 * k:4 * k + 2], ACT.Copy).then_inc(hf_high_a, 1)
                    if r == 1:
                        gathered(pair + 1)
                    if loaded is not None:
                        high_part(1 - r, loaded)
                    act.wait_ge(y1_ready, b + 1)
                    act.activation(YB[r], ps[:, 3, 0:D], ACT.Copy)
                    act.activation(YB_H[r], ps[:, 3, 0:D], ACT.Copy).then_inc(y1_high, 1)

                act.wait_ge(ln_xn, 6 * NT)
                act.activation(XN_H, XN[:], ACT.Copy).then_inc(xn_high, 1)
                high_part(0, 16)
                gathered(0)
                body(0, 0, 0, 16)
                act.wait_ge(ps_ready, 3)
                with act.Fori(0, E1 // 2) as g:
                    body(2 * g + 1, 1, g, 16 * g + 32)
                    body(2 * g + 2, 0, g + 1, 16 * g + 32)
                body(E1 + 1, 1, E1 // 2, 16 * (NB // 2 + 1))
                body(E1 + 2, 0, E1 // 2 + 1, None)

        @block.vector
        def _(dve):
            n = [0]

            def chain(ins):
                n[0] += 1
                ins.then_inc(vec, 1)
                dve.wait_ge(vec, n[0])

            def statistics(i):
                dve.bn_stats(stats[:, i], X[:, i]).then_inc(vec, 1)
                n[0] += 1

            def norm(k):
                normalize(k)
                turned_norm(k)

            def turned_norm(k):
                dve.wait_ge(ln_tr, 2 * k + 2)
                dve.tensor_copy(XT[:, 1], ps[:, 7]).then_inc(ln_xt, 1)

            def normalize(k):
                if k == 0:
                    for i in range(NT):
                        statistics(i)
                dve.wait_ge(vec, n[0])
                for i in range(NT):
                    last = dve.bn_aggr(mv[:, i], stats[:, i])
                last.then_inc(ln_stat, 1)
                dve.wait_ge(ln_std, k + 1)
                chain(dve.reciprocal(std[:], std[:]))
                for i in range(NT):
                    dve.tensor_scalar(XN[:, i], X[:, i], mv[:, i, 0:1], std[:, i:i + 1], ALU.subtract,
                                      ALU.mult).then_inc(ln_xn, 1)

            def third(p):
                dve.wait_ge(on_taken, p + 1)
                q = slice(P * PAIR[NT + p], P * (PAIR[NT + p] + 1))
                dve.tensor_tensor(F3[:, :, q], XT[:, :, q], HQT[:, :, q], ALU.mult).then_inc(third_ready, 1)

            def cross(s, row_weights=None):
                def scores(p):
                    k = NT * s + p
                    i = PAIR[k]
                    if k == 0:
                        turned_context(dve, range(4))
                    for j in range(KB4):
                        if k == 0:
                            turned_context(dve, range(4 * j + 4, min(4 * j + 8, CF)))
                        w = keys_of(j, BANK)
                        at = slice(BANK * j, BANK * j + w)
                        dve.wait_ge(sc_ready, KB4 * k + j + 1)
                        if s == 0:
                            dve.scalar_tensor_tensor(prob[p % 2][:, at], ps[:, j, 0:w], crow[:, i:i + 1], maskP[:, at],
                                                     ALU.add, ALU.add).then_inc(sc_taken, 1)
                        else:
                            dve.tensor_scalar(prob[p % 2][:, at], ps[:, j, 0:w], crow[:, i:i + 1], None,
                                              ALU.add).then_inc(sc_taken, 1)
                    dve.wait_ge(sc_taken, KB4 * (k + 1))
                    chain(dve.reduce_max(mx[:, i:i + 1], prob[p % 2], axis=AX.X))
                    dve.tensor_scalar(nmx[:, p:p + 1], mx[:, i:i + 1], -1.0, None, ALU.mult).then_inc(mx_ready, 1)

                def finish(p):
                    k = NT * s + p
                    i = PAIR[k]
                    dve.wait_ge(ex_ready, k + 1)
                    chain(dve.reciprocal(rec[:, p:p + 1], den[:, p:p + 1]))
                    dve.wait_ge(pv_ready, k + 1)
                    if s == 0:
                        dve.scalar_tensor_tensor(X[:, i], ps[:, 6, 0:D], rec[:, p:p + 1], X[:, i],
                                                 ALU.mult, ALU.add).then_inc(pv_taken, 1)
                        dve.wait_ge(pv_taken, k + 1)
                        statistics(i)
                    else:
                        if p:
                            dve.wait_ge(on_ready, p)
                        dve.tensor_scalar(hq, ps[:, 6, 0:D], rec[:, p:p + 1], None, ALU.mult).then_inc(pv_taken, 1)

                scores(0)
                for p in range(NT):
                    if p + 1 < NT:
                        scores(p + 1)
                    elif s:
                        row_weights()
                    finish(p)
                    if s and p:
                        third(p - 1)
                if s == 0:
                    dve.wait_ge(pv_taken, NT)

            dve.wait_ge(ld_x, 16)
            normalize(0)
            dve.wait_ge(ld_w, 32)
            dve.wait_ge(pj_ready, 1)
            dve.tensor_copy(W21[:, 1], ps[:, 1, 0:D]).then_inc(pj_v, 1)
            chain(dve.tensor_tensor(gcol, ps[:, 4, 0:DC], cols[:, C_B2:C_B2 + DC], ALU.add))
            for c in range(DC):
                chain(dve.tensor_copy(gwide[:, c], gcol[:, c:c + 1].to_broadcast([P, P])))
            dve.sem_inc(pj_v, 1)
            turned_norm(0)
            dve.wait_ge(pj_ready, 2)
            dve.tensor_copy(WFOLD[:, 1], ps[:, 3, 0:D]).then_inc(pj_v, 1)
            dve.wait_ge(pj_ready, 3)
            chain(dve.tensor_copy(hcol, ps[:, 5, 0:DC]))
            dve.tensor_scalar(hscaled, hcol, SCALE, None, ALU.mult).then_inc(pj_v, 1)
            dve.wait_ge(pj_ready, 5)
            dve.tensor_scalar(QT[:, 1], ps[:, 1], SCALE, hscaled[:, 1:2], ALU.mult, ALU.add).then_inc(pj_v, 1)
            dve.wait_ge(cr_ready, 1)
            chain(dve.tensor_scalar(crow, ps[:, 6, 0:NT], SCALE, None, ALU.mult))
            dve.wait_ge(ld_mask, 16)
            cross(0)
            dve.sem_inc(xa_done, 1)

            if stages > 1:
                norm(1)
                dve.wait_ge(ld_rest, 64)
                for k in range(6):
                    z, m = divmod(k, 2)
                    c = C_CONV + 8 * z + 4 * m
                    dve.wait_ge(first_tap, k + 1)
                    pre = ps[:, k].rearrange("p (b t) -> p b t", b=B)
                    for back in range(1, TAPS):
                        ins = dve.scalar_tensor_tensor(Y[z][m][:, :, back:S], pre[:, :, 0:S - back],
                                                       cols[:, c + TAPS - 1 - back:c + TAPS - back],
                                                       Y[z][m][:, :, back:S], ALU.mult, ALU.add)
                        if back < TAPS - 1:
                            chain(ins)
                        else:
                            ins.then_inc(conv_done, 1)
                dve.wait_ge(ksq_done, 1)
                dve.reduce_sum(ss, sq.rearrange("p d t -> p t d"), axis=AX.X).then_inc(dl_v, 1)
                for v in (KB, VB):
                    chain(dve.memset(v[:, S:S + 2], 0.0))
                for v in (nega1, nega2):
                    chain(dve.memset(v[:, S:S + 2], 0.0))
                for v in (state[0], outer[1], terms[1]):
                    dve.memset(v, 0.0).then_inc(tok, 1)
                dve.wait_ge(dl_a, 1)
                chain(dve.tensor_scalar(nk, nk, 1e-6, None, ALU.max))
                chain(dve.reciprocal(nk, nk))
                chain(dve.tensor_tensor(KN[:, 0:S].rearrange("p t d -> p d t"), raw[0],
                                        bcast_mid(nk, [P, HD, S]), ALU.mult))
                dve.sem_inc(kn_done, 1)
                sqt = sq.rearrange("p d t -> p (d t)").rearrange("p (t d) -> p t d", d=HD)
                chain(dve.tensor_tensor(sqt[:, 0:S - 1], KN[:, 1:S], KN[:, 0:S - 1], ALU.mult))
                chain(dve.reduce_sum(nega1[:, 1:S], sqt[:, 0:S - 1], axis=AX.X))
                dve.wait_ge(b_in, 16)
                chain(dve.scalar_tensor_tensor(KB[:, 0:S], KN[:, 0:S], -1.0, bcast(beta, [P, S, HD]),
                                               ALU.mult, ALU.mult))
                dve.wait_ge(dot2_done, 1)
                chain(dve.reduce_sum(nega2[:, 2:S], dot2[:, 0:S - 2], axis=AX.X))
                for back, dots in ((1, nega1), (2, nega2)):
                    chain(dve.scalar_tensor_tensor(dots[:, back:S], dots[:, back:S], -1.0, beta[:, back:S],
                                                   ALU.mult, ALU.mult))
                dve.wait_ge(vb_done, 1)
                dve.wait_ge(tok, 3)
                dve.tensor_copy(terms[1][:, :, HD], VB[:, 1]).then_inc(tok, 1)
                dve.tensor_copy(uu[:, 0], VB[:, 0]).then_inc(tok, 1)
                dve.wait_ge(tok, 5)
                def recur(first, end):
                    with dve.Fori(first, end) as g:
                        for r in range(UNROLL):
                            t = UNROLL * g + r
                            base = (STEPS_V * UNROLL) * g + (STEPS_V * r + 5)
                            own = (STEPS_P * UNROLL) * g + (STEPS_P * r + 3)
                            dve.wait_ge(tok_p, own - 2)
                            dve.wait_ge(tok, base - 2)
                            dve.tensor_tensor(state[(r + 1) % 2], state[r % 2], outer[(r + 1) % 2],
                                              ALU.add).then_inc(tok, 1)
                            if r % (UNROLL // 2) == UNROLL // 2 - 1:
                                dve.wait_ge(u_kept, 2 * g + (2 if r == UNROLL - 1 else 1))
                            dve.wait_ge(tok_p, own + 1)
                            dve.wait_ge(tok, base)
                            dve.reduce_sum(uu[:, (r + 1) % UNROLL], terms[(r + 1) % 2], axis=AX.X).then_inc(tok, 1)
                            dve.wait_ge(tok, base + 1)
                            dve.tensor_tensor(terms[r % 2][:, :, 0:HD], state[(r + 1) % 2],
                                              KB[:, bass.ds(t + 2, 1)].to_broadcast([P, HD, HD]),
                                              ALU.mult).then_inc(tok, 1)

                def scale_u(part):
                    t = slice(S // 2 * part, S // 2 * (part + 1))
                    dve.wait_ge(u_kept, S // UNROLL * (part + 1) + 1)
                    dve.tensor_tensor(U[:, t], U[:, t], bcast(nk[:, t], [P, S // 2, HD]), ALU.mult).then_inc(un_ready, 1)

                def mask(part):
                    t = slice(S // 2 * part, S // 2 * (part + 1))
                    for i in range(NT):
                        dve.wait_ge(kq_taken, 4 * i + 4)
                        dve.tensor_tensor(AT[i][:, :, t], AT[i][:, :, t], bcast_mid(causal[:, t], [P, H, S // 2]),
                                          ALU.mult).then_inc(kq_masked, 1)

                recur(0, S // UNROLL // 2)
                scale_u(0)
                dve.wait_ge(causal_made, 2)
                mask(0)
                recur(S // UNROLL // 2, S // UNROLL)
                scale_u(1)
                dve.wait_ge(o_half, 1)
                mask(1)
                dve.wait_ge(tok_p, STEPS_P * S + 3)
                dve.wait_ge(q_norm, 1)
                chain(dve.tensor_scalar(qscale, qn, 1e-6, None, ALU.max))
                chain(dve.reciprocal(qscale, qscale))
                chain(dve.tensor_scalar(qscale, qscale, HD ** -0.5, None, ALU.mult))
                chain(dve.tensor_tensor(qs2, qscale, qscale, ALU.mult))
                def by_head(v, k):
                    return v[:, 2 * k:2 * k + 2].rearrange("p i (h m) -> p (i h) m", m=HD)

                def flat(v, k):
                    return v[:, 2 * k:2 * k + 2].rearrange("p i h -> p (i h)")

                for k in range(2):
                    dve.wait_ge(o_ready, k + 1)
                    raw_o = ps[:, 2 + k].rearrange("p (h m) -> p h m", m=HD)
                    chain(dve.tensor_copy(by_head(ON1, k), raw_o))
                    chain(dve.tensor_tensor(by_head(OSQ, k), by_head(ON1, k), by_head(ON1, k), ALU.mult))
                    chain(dve.reduce_sum(flat(os, k), by_head(OSQ, k), axis=AX.X))
                    dve.tensor_tensor(flat(os, k), flat(os, k), flat(qs2, k), ALU.mult).then_inc(os_v, 1)
                for k in range(2):
                    dve.wait_ge(os_a, k + 1)
                    chain(dve.reciprocal(flat(os, k), flat(os, k)))
                    chain(dve.tensor_tensor(flat(os, k), flat(os, k), flat(qscale, k), ALU.mult))
                    dve.tensor_tensor(by_head(ON1, k), by_head(ON1, k), bcast(flat(os, k), [P, 2 * H, HD]),
                                      ALU.mult).then_inc(on1_ready, 1)
                dve.wait_ge(ot_ready, 2)
                dve.tensor_scalar(OTr[:, 1], ps[:, 5], cols[:, C_ON:C_ON + 1], None, ALU.mult).then_inc(ot_taken, 1)
                for i in range(NT):
                    dve.wait_ge(ap_ready, 7 + i)
                    chain(dve.tensor_tensor(X[:, i], ps[:, i, 0:D], X[:, i], ALU.add))
                    statistics(i)
                dve.sem_inc(xa_done, 1)

            if stages > 2:
                norm(2)
                dve.wait_ge(x_high, 1)
                dve.tensor_tensor(XT_L, XT[:], XT_H.bitcast(F32), ALU.subtract).then_inc(x_low, 1)
                dve.wait_ge(gt_act, 1)
                chain(dve.tensor_tensor(sel, sg, bcast_mid(rows[:, R_EB:R_EB + E0], [P, NT, E0]), ALU.add))
                for i in range(NT):
                    chain(dve.max(top8[:, i], sel[:, i]))
                    chain(dve.match_replace(rep[:, i], top8[:, i], sel[:, i], CUT))
                chain(dve.tensor_tensor(rep, sel, rep, ALU.not_equal))
                chain(dve.tensor_tensor(cw[:, :, 0:E0], sg, rep, ALU.mult))
                chain(dve.reduce_sum(csum, cw[:, :, 0:E0], axis=AX.X))
                chain(dve.reciprocal(csum, csum))
                chain(dve.tensor_scalar(csum, csum, ROUTE, None, ALU.mult))
                chain(dve.tensor_tensor(cw[:, :, 0:E0], cw[:, :, 0:E0], bcast(csum, [P, NT, E0]), ALU.mult))
                chain(dve.memset(cw[:, :, E0:E0 + 1], 1.0))

                def split(e, r):
                    for m in range(DC):
                        dve.wait_ge(silu0, 2 * e + (m + 1))
                        dve.tensor_tensor(G[:, m], ps[:, 2 * m + 1], G[:, m], ALU.mult).then_inc(h0_done, 1)
                    for m in range(DC):
                        dve.wait_ge(h_high, 2 * e + (m + 1))
                        dve.tensor_tensor(HT_L[r][:, m], G[:, m], HT_H[r][:, m].bitcast(F32),
                                          ALU.subtract).then_inc(h_low, 1)

                def weigh(e, two_e):
                    for i in range(NT):
                        if i % 2 == 0:
                            dve.wait_ge(d_ready, two_e + (i // 2 + 4))
                        w = cw[:, i, bass.ds(e, 1)] if not isinstance(e, int) else cw[:, i, e:e + 1]
                        dve.scalar_tensor_tensor(X[:, i], ps[:, 4 + i // 2, D * (i % 2):D * (i % 2 + 1)], w, X[:, i],
                                                 ALU.mult, ALU.add).then_inc(y0_taken, 1)

                dve.sem_inc(h_low, 2)
                split(0, 0)
                dve.sem_inc(y0_taken, 1)
                with dve.Fori(0, E0 // 2) as g:
                    for r in range(2):
                        e = 2 * g + r
                        split(e + 1, 1 - r)
                        dve.wait_ge(y0_taken, 8 * g + (4 * r + 1))
                        weigh(e, 4 * g + 2 * r)
                dve.wait_ge(y0_taken, 4 * E0 + 1)
                weigh(E0, 2 * E0)
                for i in range(NT):
                    dve.wait_ge(y0_taken, 4 * E0 + 1 + i + 1)
                    statistics(i)
                dve.sem_inc(xa_done, 1)

            if stages > 3:
                norm(3)
                dve.wait_ge(ln_xt, 8)
                for c in range(DC):
                    dve.tensor_scalar(QT[:, c], XT[:, c], cols[:, C_S3 + c:C_S3 + c + 1],
                                      cols[:, C_S2 + c:C_S2 + c + 1], ALU.mult, ALU.add).then_inc(pj_v, 1)
                dve.wait_ge(cr_ready, 2)
                chain(dve.tensor_scalar(crow, ps[:, 6, 0:NT], rows[:, R_SIM:R_SIM + 1], None, ALU.add))
                for i in range(NT):
                    chain(dve.tensor_tensor(X[:, i], X[:, i], rows[:, R_QV:R_QV + D], ALU.add))
                chain(dve.memset(bmask, 0.0))

                def row_weights():
                    dve.wait_ge(small_pe, 1)
                    pm = ps[0:NT, 0, 0:P].rearrange("p (a b) -> p a b", a=2)
                    chain(dve.reduce_max(bsum[0:NT], pm, axis=AX.X))
                    dve.tensor_tensor(battv[0:NT], pm, bcast(bsum[0:NT], [NT, 2, S]), ALU.subtract).then_inc(small_v, 1)
                    dve.wait_ge(small_a, 2)
                    chain(dve.reduce_sum(bsum[0:NT], battv[0:NT], axis=AX.X))
                    chain(dve.reciprocal(bsum[0:NT], bsum[0:NT]))
                    dve.tensor_tensor(battv[0:NT], battv[0:NT], bcast(bsum[0:NT], [NT, 2, S]),
                                      ALU.mult).then_inc(bt_ready, 1)

                cross(1, row_weights)
                dve.wait_ge(small_pe, 2)
                for half in range(2):
                    q = slice(S * half, S * (half + 1))
                    dve.tensor_copy(bmask[q, :, half], ps[q, 1, 0:NT]).then_inc(bt_ready, 1)
                third(NT - 1)
                dve.wait_ge(small_pe, 3)
                chain(dve.tensor_copy(hcb, ps[:, 2, 0:DC * B].rearrange("p (a b) -> p a b", a=DC)))
                for c in range(DC):
                    dve.tensor_tensor(F4[:, c].rearrange("p (b t) -> p b t", b=B),
                                      XT[:, c].rearrange("p (b t) -> p b t", b=B),
                                      bcast(hcb[:, c], [P, B, S]), ALU.mult).then_inc(bt_ready, 1)
                for i in range(NT):
                    dve.wait_ge(small_pe, 4 + i)
                    chain(dve.tensor_tensor(X[:, i], ps[:, 3 + i, 0:D], X[:, i], ALU.add))
                    statistics(i)
                dve.sem_inc(xa_done, 1)

            if stages > 4:
                norm(4)
                chain(dve.tensor_scalar(bkm, headmask[:], cols[:, C_BK:C_BK + 1], None, ALU.mult))
                dve.sem_inc(small_v, 1)
                for i in range(NT):
                    chain(dve.tensor_tensor(X[:, i], X[:, i], rows[:, R_BO:R_BO + D], ALU.add))
                chain(dve.memset(VM, 0.0))
                dve.wait_ge(qk_ready, DC + 2)
                for h in range(HC):
                    dve.tensor_scalar(KM[1][:, h], ps[:, 3], cols[:, C_BK + 1:C_BK + 2],
                                      headmask[:, h:h + 1], ALU.add, ALU.mult).then_inc(k_v, 1)
                def values(first, end):
                    for b in range(first, end):
                        dve.wait_ge(v_ready, b + 1)
                        for half in range(2):
                            q = slice(S * half, S * (half + 1))
                            src = ps[q, 4 + b % 4, 0:D].rearrange("p (j h m) -> p j h m", h=2, m=HD)[:, :, half]
                            bias = rows[q, R_BV:R_BV + D].rearrange("p (j h m) -> p j h m", h=2, m=HD)[:, :, half]
                            dve.tensor_tensor(VM[q, b, :, HD * half:HD * (half + 1)], src, bias,
                                              ALU.add).then_inc(v_taken, 1)

                def scaled(i):
                    dve.wait_ge(as_ready, i + 1)
                    sc = psf[:, 0:H * S].rearrange("p (h z) -> p h z", h=H)
                    chain(dve.reduce_max(am, sc, axis=AX.X))
                    dve.tensor_tensor(PA[i % 2], sc, bcast(am, [P, H, S]), ALU.subtract).then_inc(sub_done, 1)

                def weighted(i):
                    if i:
                        dve.wait_ge(aon_ready, i)
                    chain(dve.reduce_sum(asum, PA[i % 2], axis=AX.X))
                    chain(dve.reciprocal(asum, asum))
                    dve.wait_ge(ao_ready, i + 1)
                    if i:
                        dve.wait_ge(aot_ready, i)
                    dve.tensor_tensor(ON.rearrange("p (h m) -> p h m", h=H),
                                      ps[:, 4, 0:D].rearrange("p (h m) -> p h m", h=H),
                                      bcast(asum, [P, H, HD]), ALU.mult).then_inc(aon_ready, 1)

                def add(i):
                    dve.wait_ge(ay_ready, i + 1)
                    dve.tensor_tensor(X[:, i], ps[:, 6, 0:D], X[:, i], ALU.add).then_inc(ay_taken, 1)
                    dve.wait_ge(ay_taken, i + 1)
                    statistics(i)

                values(0, 4)
                scaled(0)
                values(4, B)
                for i in range(NT):
                    if i + 1 < NT:
                        scaled(i + 1)
                    dve.wait_ge(pa_ready, i + 1)
                    weighted(i)
                    if i:
                        add(i - 1)
                add(NT - 1)
                dve.wait_ge(ay_taken, NT)
                dve.sem_inc(xa_done, 1)

            if stages > 5:
                norm(5)
                dve.wait_ge(gt_ready, 2)
                chain(dve.tensor_tensor(lg, ps[:, 4, 0:NT * E1].rearrange("p (a b) -> p a b", a=NT),
                                        bcast_mid(rows[:, R_BR:R_BR + E1], [P, NT, E1]), ALU.add))
                chain(dve.reduce_max(lmax, lg, axis=AX.X))
                chain(dve.tensor_tensor(eq, lg, bcast(lmax, [P, NT, E1]), ALU.is_equal))
                chain(dve.tensor_tensor(eq, eq, index[:], ALU.mult))
                chain(dve.tensor_reduce(lmin, eq, op=ALU.min, axis=AX.X))
                chain(dve.tensor_tensor(oh, index[:], bcast(lmin, [P, NT, E1]), ALU.is_equal))
                dve.sem_inc(route_done, 1)
                dve.wait_ge(xn_high, 1)
                dve.tensor_tensor(XN_L, XN[:], XN_H.bitcast(F32), ALU.subtract).then_inc(xn_low, 1)
                dve.wait_ge(room_made, 10)
                dve.wait_ge(gt_ready, 3)
                ranks = ps[:, 4, 64:64 + NT * E1].rearrange("p (a b) -> p a b", a=NT)
                total = ps[:, 4, 96:96 + E1]
                chain(dve.tensor_tensor(gt3, bcast(total, [P, E1, OVER]), full, ALU.is_gt))
                chain(dve.reduce_sum(more, gt3, axis=AX.X))
                chain(dve.tensor_tensor(low_more, bcast_mid(more, [P, E1, E1]), lower, ALU.mult))
                chain(dve.reduce_sum(ostart, low_more, axis=AX.X))
                for ins in (dve.scalar_tensor_tensor(shift, ostart, float(P), jump, ALU.mult, ALU.add),
                            dve.tensor_tensor(oend, ostart, more, ALU.add),
                            dve.tensor_scalar(over, ranks, float(P), None, ALU.is_ge)):
                    ins.then_inc(vec, 1)
                    n[0] += 1
                chain(dve.tensor_tensor(rank, ranks, bcast_mid(own_block, [P, NT, E1]), ALU.add))
                chain(dve.tensor_tensor(over, over, bcast_mid(shift, [P, NT, E1]), ALU.mult))
                chain(dve.tensor_tensor(rank, rank, over, ALU.add))
                chain(dve.tensor_tensor(rank, rank, oh, ALU.mult))
                chain(dve.reduce_sum(pos, rank, axis=AX.X))
                chain(dve.tensor_tensor(posm, bcast_mid(pos, [P, NB + 1, NT]), first_slot, ALU.subtract))

                def gather_map(pair):
                    for half in range(2):
                        at = (posm[:, 2 * pair + half] if isinstance(pair, int)
                              else posm[:, bass.ds(2 * pair + half, 1)].rearrange("p o n -> p (o n)"))
                        dve.tensor_tensor(PG[:, :, P * half:P * (half + 1)], bcast_mid(slots, [P, NT, P]),
                                          bcast(at, [P, NT, P]), ALU.is_equal).then_inc(pg_ready, 1)

                gather_map(0)
                for i in range(NT):
                    chain(dve.tensor_scalar(diag[:, i], ident[:], pos[:, i:i + 1], None, ALU.mult))
                dve.sem_inc(route_done, 1)
                dve.wait_ge(gt_ready, 4)
                chain(dve.tensor_copy(ohT, ps[0:E1, 5]))
                dve.sem_inc(route_done, 1)
                chain(dve.tensor_tensor(ended, bcast_mid(oend, [P, OVER, E1]), order, ALU.is_le))
                chain(dve.reduce_sum(oexp, ended, axis=AX.X))
                chain(dve.tensor_scalar(oexp, oexp, float(E1 - 1), None, ALU.min))
                dve.tensor_copy(further[:], oexp[0:1]).then_inc(further_ready, 1)
                dve.wait_ge(gt_ready, 5)
                dve.tensor_copy(posrow, ps[:, 5]).then_inc(ps_ready, 1)
                dve.wait_ge(ps_ready, 1)

                def low_of(f):
                    dve.tensor_tensor(HF_L[:, f:f + 2], HF[:, f:f + 2], HF_H[:, f:f + 2].bitcast(F32),
                                      ALU.subtract).then_inc(hf_low, 1)

                def body(b, r, pair):
                    for k in range(2):
                        f0 = 4 * k + 2
                        dve.wait_ge(f_ready, 4 * b + (2 * k + 2))
                        for i in range(2):
                            last = dve.tensor_scalar(HF[:, f0 + i], ps[:, 4 * k + 1, P * i:P * (i + 1)],
                                                     column(FC * b + (C_F1 + f0 + i)), 0.0, ALU.add, ALU.max)
                        last.then_inc(relu_v, 1)
                        dve.wait_ge(hf_high_a, 2 * b + (k + 1))
                        low_of(f0 - 2)
                        dve.wait_ge(relu_v, 4 * b + (2 * k + 1))
                        dve.tensor_copy(HF_H[:, f0:f0 + 2], HF[:, f0:f0 + 2]).then_inc(relu_v, 1)
                        dve.wait_ge(relu_v, 4 * b + (2 * k + 2))
                        low_of(f0)
                    at = slotcol[:, b:b + 1] if isinstance(b, int) else slotcol[:, bass.ds(b, 1)]
                    if not isinstance(b, int) or b > 1:
                        dve.wait_ge(put_done, b)
                    dve.tensor_scalar(PS[r], posrow, at, None, ALU.is_equal).then_inc(ps_ready, 1)
                    if r == 0 and not (isinstance(b, int) and b == NB - 1):
                        dve.wait_ge(xg_ready, pair + 1)
                        gather_map(pair + 1)
                    dve.wait_ge(y1_high, b + 1)
                    dve.tensor_tensor(YB_L[r], YB[r], YB_H[r].bitcast(F32), ALU.subtract).then_inc(y1_low, 1)

                body(0, 0, 0)
                chain(dve.tensor_scalar(oexp, oexp, float(-E1), None, ALU.add))
                chain(dve.tensor_tensor(osel, bcast(oexp, [P, OVER, E1]), bcast_mid(index[:, 0], [P, OVER, E1]),
                                        ALU.is_equal))
                for j in range(OVER):
                    chain(dve.tensor_tensor(obias, cols[:, C_F1:NCOLS].rearrange("p (e f) -> p f e", e=E1),
                                            bcast_mid(osel[:, j], [P, FC, E1]), ALU.mult))
                    at = NCOLS + FC * j
                    chain(dve.reduce_sum(cols[:, at:at + FC], obias, axis=AX.X))
                dve.sem_inc(ps_ready, 1)
                with dve.Fori(0, E1 // 2) as g:
                    body(2 * g + 1, 1, g)
                    body(2 * g + 2, 0, g + 1)
                body(E1 + 1, 1, E1 // 2)
                body(E1 + 2, 0, E1 // 2 + 1)
                dve.wait_ge(put_done, NB + 1)
                for i in range(0, NT, 2):
                    chain(dve.tensor_tensor(X[:, i:i + 2].rearrange("p a b -> p (a b)"), ps[:, 6 + i // 2],
                                            X[:, i:i + 2].rearrange("p a b -> p (a b)"), ALU.add))
                dve.sem_inc(xa_done, 1)

        @block.tensor
        def _(pe):
            pe.wait_ge(consts, 5)

            def norm(k, wait=True):
                for i in range(NT):
                    pe.wait_ge(ln_xn, NT * k + i + 1)
                    for c in range(DC):
                        last = pe.transpose(ps[:, 6 + c, P * i:P * (i + 1)], XN[:, i, P * c:P * (c + 1)], ident[:])
                        if i == NT - 1:
                            last.then_inc(ln_tr, 1)
                if wait:
                    pe.wait_ge(ln_xt, 2 * k + 2)

            def linear(dst, w, src, m):
                for c in range(DC):
                    last = pe.matmul(dst, w_of(w, c, m), src[:, c], start=(c == 0), stop=(c == DC - 1))
                return last

            def turn(s, p):
                pe.wait_ge(pv_taken, NT * s + p + 1)
                if p:
                    pe.wait_ge(on_taken, p)
                for c in range(DC):
                    last = pe.transpose(ps[:, 7, P * c:P * (c + 1)], hq[:, P * c:P * (c + 1)], ident[:])
                last.then_inc(on_ready, 1)

            def fill_context(f):
                pe.wait_ge(*((ld_early, 16) if f < 2 * 4 else (ld_cn[0], 16)))
                if f >= len(TURN_BANKS):
                    emptied(f - len(TURN_BANKS))
                for i in range(4):
                    if f < CF - 1:
                        (half, c), tile = divmod(f % 4, 2), 4 * (f // 4) + i
                    else:
                        (half, c), tile = divmod(i, 2), KT - 1
                    w = keys_of(tile, P)
                    last = pe.transpose(ps[:, TURN_BANKS[f % 3], P * i:P * i + w],
                                        CTX_N[0:w, 0, half, tile, P * c:P * (c + 1)], ident[0:w, 0:w])
                last.then_inc(filled, 1)

            def emptied(f):
                pe.wait_ge(emptied_v if f % 2 else emptied_a, f // 2 + 1)

            def cross(s):
                def scores(p):
                    k = NT * s + p
                    if k:
                        pe.wait_ge(ld_ct[k % 2], 16 * LOADS_T[k])
                    else:
                        for f in range(4):
                            fill_context(f)
                    for j in range(KB4):
                        w = keys_of(j, BANK)
                        ahead = list(range(4 * j + 4, min(4 * j + 8, CF))) if k == 0 else []
                        if k:
                            pe.wait_ge(sc_taken, KB4 * (k - 1) + j + 1)
                        for c in range(DC):
                            for f in ahead[2 * c:2 * c + 2]:
                                fill_context(f)
                            if k == 0 and c == 0:
                                for f in range(4 * j, min(4 * j + 4, CF)):
                                    emptied(f)
                            for half in range(2):
                                q = P * PAIR[k] + S * half
                                last = pe.matmul(ps[S * half:S * (half + 1), j, 0:w], QT[:, c, q:q + S],
                                                 CTX_T[:, k % 2, half, c, BANK * j:BANK * j + w],
                                                 start=(c == 0), stop=(c == DC - 1))
                        last.then_inc(sc_ready, 1)

                scores(0)
                for p in range(NT):
                    k = NT * s + p
                    if p + 1 < NT:
                        scores(p + 1)
                    if s and p:
                        turn(s, p - 1)
                    if s and p == NT - 1:
                        pe.wait_ge(mx_ready, 2 * NT)
                        pe.transpose(ps[0:NT, 0, 0:P], mx, ident[:]).then_inc(small_pe, 1)
                    pe.wait_ge(ex_ready, k + 1)
                    for g in range(4):
                        if 4 * k + g >= 2:
                            pe.wait_ge(pt_taken, 4 * k + g - 1)
                        for j in range(4 * g, min(KT, 4 * g + 4)):
                            w = keys_of(j, P)
                            last = pe.transpose(ps[0:w, 4 + g % 2, P * (j % 4):P * (j % 4 + 1)],
                                                prob[p % 2][:, P * j:P * j + w], ident[:])
                        last.then_inc(pt_ready, 1)
                    pe.wait_ge(ld_cn[k % 2], 16 * LOADS_N[k])
                    pe.wait_ge(pt_taken, 4 * k + 4)
                    if k:
                        pe.wait_ge(pv_taken, k)
                    for j in range(KT):
                        w = keys_of(j, P)
                        for half in range(2):
                            q = slice(S * half, S * (half + 1))
                            last = pe.matmul(ps[q, 6, 0:D], probT[p % 2][0:w, j, q], CTX_N[0:w, k % 2, half, j],
                                             start=(j == 0), stop=(j == KT - 1))
                    last.then_inc(pv_ready, 1)

            pe.wait_ge(ld_w, 32)
            for m in range(DC):
                for c in range(DC):
                    pe.matmul(ps[:, m, 0:D], w_of(W2T, c, m), W[:, W1N, c], start=(c == 0), stop=(c == DC - 1))
            for m in range(DC):
                for c in range(DC):
                    last = pe.matmul(ps[:, 4, m:m + 1], w_of(W2T, c, m), cols[:, C_B1 + c:C_B1 + c + 1],
                                     start=(c == 0), stop=(c == DC - 1))
            last.then_inc(pj_ready, 1)
            norm(0, wait=False)
            pe.wait_ge(pj_a, 1)
            pe.wait_ge(pj_v, 1)
            for m in range(DC):
                for c in range(DC):
                    last = pe.matmul(ps[:, 2 + m, 0:D], W21[:, c, P * m:P * (m + 1)], W21[:, c],
                                     start=(c == 0), stop=(c == DC - 1))
            last.then_inc(pj_ready, 1)
            pe.wait_ge(pj_v, 2)
            for m in range(DC):
                for c in range(DC):
                    last = pe.matmul(ps[:, 5, m:m + 1], W21[:, c, P * m:P * (m + 1)], gcol[:, c:c + 1],
                                     start=(c == 0), stop=(c == DC - 1))
            last.then_inc(pj_ready, 1)
            pe.wait_ge(ln_xt, 2)
            pe.wait_ge(pj_a, 2)
            pe.wait_ge(pj_v, 4)
            for m in range(DC):
                for c in range(DC):
                    last = pe.matmul(ps[:, m], WFOLD[:, c, P * m:P * (m + 1)], XT[:, c], start=(c == 0), stop=(c == DC - 1))
                last.then_inc(pj_ready, 1)
            for i in range(NT):
                terms_of = [(XT[:, c, P * i:P * (i + 1)], hcol[:, c:c + 1]) for c in range(DC)]
                terms_of += [(gwide[:, c], gcol[:, c:c + 1]) for c in range(DC)]
                for k, (a, b) in enumerate(terms_of):
                    last = pe.matmul(ps[:, 6, i:i + 1], a, b, start=(k == 0), stop=(k == 3))
            last.then_inc(cr_ready, 1)
            pe.wait_ge(pj_a, 3)
            pe.wait_ge(pj_v, 5)
            cross(0)

            if stages > 1:
                norm(1)
                pe.wait_ge(ld_rest, 64)
                for z, w in enumerate((AK, AV, AQ)):
                    for m in range(DC):
                        linear(ps[:, 2 * z + m], w, XT, m).then_inc(ap_ready, 1)
                    if z == 0:
                        for c in range(DC):
                            last = pe.matmul(ps[0:H, 6], narrow[:, c, N_BETA:N_BETA + H], XT[:, c],
                                             start=(c == 0), stop=(c == DC - 1))
                        last.then_inc(b_ready, 1)
                pe.wait_ge(q_sq, 2)
                for i in range(NT):
                    for m in range(DC):
                        at = H * i + HC * m
                        last = pe.matmul(ps[:, 6, at:at + HC], qsq[:, m, P * i:P * (i + 1)], headmask[:],
                                         start=True, stop=True)
                last.then_inc(q_sum, 1)
                for k in range(2 * NT):
                    i, part = divmod(k, 2)
                    pe.wait_ge(qm_ready, HC * (k + 1))
                    if k:
                        pe.wait_ge(kq_taken, 2 * k)
                    for m in range(DC):
                        for half in range(2):
                            last = pe.matmul(ps[S * half:S * (half + 1), 7, 256 * m:256 * (m + 1)],
                                             Y[0][m][:, 2 * i + half],
                                             QM[:, HC // 2 * m:HC // 2 * (m + 1), S * half:S * (half + 1)],
                                             start=True, stop=True)
                    last.then_inc(kq_ready, 1)
                one = ident[:].rearrange("p (i b h) -> p i b h", b=2, h=H)

                def turn_u(part):
                    pe.wait_ge(un_ready, part + 1)
                    if part:
                        pe.wait_ge(ut_taken, 4)
                    for m in range(HD):
                        for half in range(2):
                            at = S * half + S // 2 * part
                            last = pe.matmul(ps[at:at + S // 2, m // 8, S * (m % 8):S * (m % 8 + 1)],
                                             U[:, S // 2 * part:S // 2 * (part + 1), m], one[:, :, half],
                                             start=True, stop=True)
                        if m % 8 == 7:
                            last.then_inc(ut_ready, 1)

                def outputs(part):
                    pe.wait_ge(ut_taken, 4 + 2 * part)
                    for i in range(NT):
                        pe.wait_ge(kq_masked, NT * part + i + 1)
                        for h in range(H):
                            for half in range(2):
                                at = S * half + S // 2 * part
                                q = slice(at, S * (half + 1))
                                col = D * (i % 2) + HD * h
                                keys = slice(at, at + S // 2)
                                last = pe.matmul(ps[q, 2 + i // 2, col:col + HD], AT[i][keys, h, S // 2 * part:],
                                                 UT[keys, i, HD * h:HD * (h + 1)],
                                                 start=(part == 0 and i % 2 == 0 and h == 0), stop=(part == 1),
                                                 skip_group_check=True)
                        if part and i % 2:
                            last.then_inc(o_ready, 1)
                    if not part:
                        last.then_inc(o_half, 1)

                turn_u(0)
                outputs(0)
                turn_u(1)
                outputs(1)
                for i in range(NT):
                    pe.wait_ge(on1_ready, i // 2 + 1)
                    for c in range(DC):
                        last = pe.transpose(ps[:, 4 + c, P * i:P * (i + 1)], ON1[:, i, P * c:P * (c + 1)], ident[:])
                        if i == NT - 1:
                            last.then_inc(ot_ready, 1)
                pe.wait_ge(ot_taken, 2)
                for i in range(NT):
                    for c in range(DC):
                        last = pe.matmul(ps[:, i, 0:D], OTr[:, c, P * i:P * (i + 1)], W[:, AO, c],
                                         start=(c == 0), stop=(c == DC - 1))
                    last.then_inc(ap_ready, 1)

            def gates(col, width):
                for i in range(NT):
                    for c in range(DC):
                        last = pe.matmul(ps[:, 4, width * i:width * (i + 1)], XT[:, c, P * i:P * (i + 1)],
                                         narrow[:, c, col:col + width], start=(c == 0), stop=(c == DC - 1))
                last.then_inc(gt_ready, 1)

            if stages > 2:
                norm(2)
                gates(N_GATE, E0)
                pe.wait_ge(gt_act, 1)
                pe.wait_ge(x_low, 1)
                pe.sem_inc(d_ready, 3)

                def three(dst, high, low, x_h, x_l):
                    terms = [(w, x) for c in range(DC) for w, x in ((high(c), x_h(c)), (high(c), x_l(c)), (low(c), x_h(c)))]
                    for k, (w, x) in enumerate(terms):
                        last = pe.matmul(dst, w, x, start=(k == 0), stop=(k == len(terms) - 1))
                    return last

                def gate_up(e, r):
                    pe.wait_ge(wg_low, e + 1)
                    for m in range(DC):
                        if not isinstance(e, int) or e:
                            pe.wait_ge(h0_done, 2 * e + (m - 1))
                        f = slice(P * m, P * (m + 1))
                        for part in range(2):
                            last = three(ps[:, 2 * m + part], lambda c: WG_H[r][:, part, c, f],
                                         lambda c: WG_L[r][:, part, c, f], lambda c: XT_H[:, c], lambda c: XT_L[:, c])
                        last.then_inc(gu_ready, 1)

                def down(e, r):
                    pe.wait_ge(wd_low, e + 1)
                    pe.wait_ge(h_low, 2 * e + 4)
                    pe.wait_ge(y0_taken, 4 * e + 1)
                    for i in range(NT):
                        q = slice(P * i, P * (i + 1))
                        last = three(ps[:, 4 + i // 2, D * (i % 2):D * (i % 2 + 1)], lambda c: HT_H[r][:, c, q],
                                     lambda c: HT_L[r][:, c, q], lambda c: WD_H[r][:, c], lambda c: WD_L[r][:, c])
                        if i % 2:
                            last.then_inc(d_ready, 1)

                gate_up(0, 0)
                with pe.Fori(0, E0 // 2) as g:
                    for r in range(2):
                        e = 2 * g + r
                        gate_up(e + 1, 1 - r)
                        down(e, r)
                down(E0, 0)

            if stages > 3:
                norm(3)
                for i in range(NT):
                    for c in range(DC):
                        last = pe.matmul(ps[:, 6, i:i + 1], XT[:, c, P * i:P * (i + 1)],
                                         cols[:, C_S1 + c:C_S1 + c + 1], start=(c == 0), stop=(c == DC - 1))
                last.then_inc(cr_ready, 1)
                pe.wait_ge(pj_v, 7)
                cross(1)
                pe.wait_ge(bt_ready, 1)
                pe.transpose(ps[:, 1, 0:NT], batt[0:NT], ident[0:NT, 0:NT]).then_inc(small_pe, 1)
                turn(1, NT - 1)
                pe.wait_ge(ld_wqv, 16)

                def project(part, f):
                    for i in range(NT):
                        for c in range(DC):
                            last = pe.matmul(ps[:, 3 + i, 0:D], f[:, c, P * i:P * (i + 1)], WQV[:, DC * part + c],
                                             start=(part == 0 and c == 0), stop=(part == 3 and c == DC - 1))
                        if part == 3:
                            last.then_inc(small_pe, 1)

                project(0, XT)
                pe.wait_ge(bt_ready, 3)
                for c in range(DC):
                    for i in range(NT):
                        at = B * c + 2 * i
                        last = pe.matmul(ps[:, 2, at:at + 2], XN[:, i, P * c:P * (c + 1)], bmask[:, i],
                                         start=True, stop=True)
                last.then_inc(small_pe, 1)
                pe.wait_ge(third_ready, NT)
                project(1, HQT)
                project(2, F3)
                pe.wait_ge(bt_ready, 5)
                project(3, F4)

            if stages > 4:
                norm(4)
                for m in range(DC):
                    linear(ps[:, m], SQ, XT, m).then_inc(qk_ready, 1)
                for m in range(DC):
                    linear(ps[:, 2 + m], SK, XT, m).then_inc(qk_ready, 1)
                def scores(i):
                    if i:
                        pe.wait_ge(sub_done, i)
                    for m in range(DC):
                        for half in range(2):
                            q = P * i + S * half
                            last = pe.matmul(ps[S * half:S * (half + 1), m], QTT[:, m, q:q + S],
                                             KM[m][:, :, q:q + S], start=True, stop=True)
                    last.then_inc(as_ready, 1)

                def values(first, end):
                    for b in range(first, end):
                        if b >= 4:
                            pe.wait_ge(v_taken, 2 * (b - 3))
                        for c in range(DC):
                            last = pe.matmul(ps[:, 4 + b % 4, 0:D], XD[:, c, b], W[:, SV, c],
                                             start=(c == 0), stop=(c == DC - 1))
                        last.then_inc(v_ready, 1)

                def turn_weights(i):
                    pe.wait_ge(pa_ready, i + 1)
                    if i:
                        pe.wait_ge(at_a, 2 * i)
                    flat = PA[i % 2].rearrange("p h z -> p (h z)")
                    for j in range(HC):
                        last = pe.transpose(ps[:, 2 + j // 4, P * (j % 4):P * (j % 4 + 1)], flat[:, P * j:P * (j + 1)],
                                            ident[:])
                        if j % 4 == 3:
                            last.then_inc(at_ready, 1)

                def turn_result(i):
                    pe.wait_ge(aon_ready, i + 1)
                    for c in range(DC):
                        last = pe.transpose(ps[:, 5, P * c:P * (c + 1)], ON[:, P * c:P * (c + 1)], ident[:])
                    last.then_inc(aot_ready, 1)

                def weigh_values(i):
                    pe.wait_ge(at_a, 2 * i + 2)
                    for j in range(HC):
                        for half in range(2):
                            last = pe.matmul(ps[S * half:S * (half + 1), 4, 32 * j:32 * (j + 1)],
                                             PAT[i % 2][:, j, S * half:S * (half + 1)], VM[:, 2 * i + half, j],
                                             start=True, stop=True)
                    last.then_inc(ao_ready, 1)

                def project(i):
                    pe.wait_ge(aoc_ready, i + 1)
                    if i:
                        pe.wait_ge(ay_taken, i)
                    for c in range(DC):
                        last = pe.matmul(ps[:, 6, 0:D], OAT[:, c], W[:, SO, c], start=(c == 0), stop=(c == DC - 1))
                    last.then_inc(ay_ready, 1)

                pe.wait_ge(xd_ready, DC)
                values(0, 4)
                pe.wait_ge(q_taken, DC)
                pe.wait_ge(k_a, HC)
                pe.wait_ge(k_v, HC)
                scores(0)
                values(4, B)
                pe.wait_ge(v_taken, 2 * B)
                for i in range(NT):
                    if i + 1 < NT:
                        scores(i + 1)
                    turn_weights(i)
                    if i:
                        turn_result(i - 1)
                    weigh_values(i)
                    if i:
                        project(i - 1)
                turn_result(NT - 1)
                project(NT - 1)

            if stages > 5:
                norm(5)
                gates(N_ROUTE, E1)
                pe.wait_ge(route_done, 1)
                pe.wait_ge(room_made, 10)
                sums = ps[:, 4, 64:64 + E1 * (NT + 1)]
                last = pe.matmul(sums[:, 0:E1 * NT], before, oh.rearrange("p a b -> p (a b)"), start=True, stop=False,
                                 skip_group_check=True)
                for k in range(NT):
                    last = pe.matmul(sums[:, E1 * (k + 1):], ones, bcast_mid(oh[:, k], [P, NT - k, E1]), start=False,
                                     stop=(k == NT - 1), skip_group_check=True)
                last.then_inc(gt_ready, 1)
                for i in range(NT):
                    last = pe.transpose(ps[0:E1, 5, P * i:P * (i + 1)], oh[:, i], ident[:])
                last.then_inc(gt_ready, 1)

                def gather(pair):
                    pe.wait_ge(pg_ready, 2 * pair + 2)
                    for c in range(DC):
                        terms_of = [(x, i) for i in range(NT) for x in (XN_H, XN_L)]
                        for k, (x, i) in enumerate(terms_of):
                            last = pe.matmul(ps[:, 2, 2 * P * c:2 * P * (c + 1)], x[:, i, P * c:P * (c + 1)], PG[:, i],
                                             start=(k == 0), stop=(k == 2 * NT - 1))
                    last.then_inc(xg_ready, 1)

                def put(b, r, final):
                    pe.wait_ge(y1_low, b + 1)
                    pe.wait_ge(ps_ready, b + 2 if isinstance(b, int) and b == 0 else b + 3)
                    for i in range(NT):
                        for y in (YB_H, YB_L):
                            last = pe.matmul(ps[:, 6 + i // 2, D * (i % 2):D * (i % 2 + 1)],
                                             PS[r][:, P * i:P * (i + 1)], y[r],
                                             start=False, stop=(final and y is YB_L), skip_group_check=True)
                    last.then_inc(put_done, 1)

                def body(b, r, pair, load):
                    pe.wait_ge(xg_taken, pair + 1)
                    pe.wait_ge(ld_we[r], load)
                    for k, bank in enumerate((0, 1, 4, 5)):
                        for i in range(2):
                            f = 2 * k + i
                            for c in range(DC):
                                last = pe.matmul(ps[:, bank, P * i:P * (i + 1)], WE1[r][:, c, P * f:P * (f + 1)],
                                                 XG[:, c, P * r:P * (r + 1)], start=(c == 0), stop=(c == DC - 1))
                        last.then_inc(f_ready, 1)
                    if r == 1:
                        gather(pair + 1)
                    if not isinstance(b, int) or b:
                        put(b - 1, 1 - r, False)
                    pe.wait_ge(we_low, b + 1)
                    for f in range(FC):
                        if f % 2 == 0:
                            pe.wait_ge(hf_low, 4 * b + (f // 2 + 1))
                        for k, (h, w) in enumerate(((HF_H, WE2_H), (HF_H, WE2_L), (HF_L, WE2_H))):
                            last = pe.matmul(ps[:, 3, 0:D], h[:, f], w[r][:, f], start=(f == 0 and k == 0),
                                             stop=(f == FC - 1 and k == 2))
                    last.then_inc(y1_ready, 1)

                pe.wait_ge(xn_low, 1)
                gather(0)
                pe.wait_ge(route_done, 3)
                for i in range(NT):
                    last = pe.matmul(ps[:, 6 + i // 2, D * (i % 2):D * (i % 2 + 1)], ohT[:, P * i:P * (i + 1)], b2e[:],
                                     start=(i % 2 == 0), stop=False, skip_group_check=True)
                last.then_inc(put_done, 1)
                for i in range(NT):
                    last = pe.matmul(ps[:, 5, P * i:P * (i + 1)], ones, diag[:, i], start=True, stop=True)
                last.then_inc(gt_ready, 1)
                pe.wait_ge(ps_ready, 1)
                body(0, 0, 0, 16)
                with pe.Fori(0, E1 // 2) as g:
                    body(2 * g + 1, 1, g, 16 * g + 16)
                    body(2 * g + 2, 0, g + 1, 16 * g + 32)
                body(E1 + 1, 1, E1 // 2, 16 * (E1 // 2 + 1))
                body(E1 + 2, 0, E1 // 2 + 1, 16 * (E1 // 2 + 2))
                put(NB - 1, (NB - 1) % 2, True)


STAGES = 6


def kernel(x, ctx_1024, fside_1xSxS2_0, L0_xattn_W1, L0_xattn_b1, L0_xattn_W2, L0_xattn_b2, L0_attn_Wq, L0_attn_Wk,
           L0_attn_Wv, L0_attn_Wb, L0_attn_Wo, L0_attn_conv_q, L0_attn_conv_k, L0_attn_conv_v, L0_attn_o_norm_w,
           L0_ffn_gate_w, L0_ffn_expert_bias, L0_ffn_w_gate, L0_ffn_w_up, L0_ffn_w_down, L0_ffn_shared_gate_w,
           L0_ffn_shared_up_w, L0_ffn_shared_down_w, L1_xattn_w_sim, L1_xattn_b_sim, L1_xattn_W_qv, L1_xattn_b_qv,
           L1_attn_Wq, L1_attn_bq, L1_attn_Wk, L1_attn_bk, L1_attn_Wv, L1_attn_bv, L1_attn_Wo, L1_attn_bo,
           L1_ffn_Wr, L1_ffn_br, L1_ffn_W1, L1_ffn_b1, L1_ffn_W2, L1_ffn_b2):
    import numpy as np
    import concourse.bacc as bacc
    from concourse.bass_utils import run_bass_kernel_spmd

    a = lambda v: np.asarray(v)

    def chunked(w):
        w = a(w)
        *lead, r, n = w.shape
        return np.moveaxis(w.reshape(*lead, r // P, P, n), -3, -2)

    def turned(w):
        return np.swapaxes(a(w), -1, -2)

    def columns(v):
        return a(v).reshape(-1, P).T

    def taps(w):
        return chunked(w).reshape(P, DC * TAPS)

    def spread(v):
        return np.broadcast_to(a(v).reshape(1, -1), (P, a(v).size))

    arrays = {
        "x": chunked(a(x).reshape(T, D)),
        "ctx_n": np.pad(a(ctx_1024), ((0, 0), (0, KT * P - KEYS), (0, 0))).reshape(NT, 2, KT, P, D).transpose(0, 3, 1, 2, 4),
        "ctx_t": a(ctx_1024).reshape(NT, 2, KEYS, DC, P).transpose(0, 4, 1, 3, 2),
        "mask": np.concatenate([a(fside_1xSxS2_0)[0]] * 2, axis=0),
        "w_small": np.stack([chunked(w) for w in (
            turned(L0_xattn_W2), L0_xattn_W1,
            turned(L0_attn_Wk), turned(L0_attn_Wv), turned(L0_attn_Wq), turned(L0_attn_Wo),
            turned(L1_attn_Wq), turned(L1_attn_Wk), turned(L1_attn_Wv), turned(L1_attn_Wo))], axis=1),
        "cols": np.concatenate([
            columns(L0_xattn_b1), columns(L0_xattn_b2), taps(L0_attn_conv_k), taps(L0_attn_conv_v), taps(L0_attn_conv_q),
            np.tile(a(L0_attn_o_norm_w), HC).reshape(P, 1), np.zeros((P, 1), np.float32), columns(L1_xattn_w_sim),
            columns(L1_attn_bq), columns(L1_attn_bk), columns(a(L1_ffn_b1).reshape(-1))], axis=1),
        "rows": np.concatenate([spread(v) for v in (
            L1_xattn_b_qv, L1_attn_bv, L1_attn_bo, L0_ffn_expert_bias, L1_ffn_br, L1_xattn_b_sim)], axis=1),
        "narrow": np.concatenate([chunked(turned(w)) for w in (L0_attn_Wb, L0_ffn_gate_w, L1_ffn_Wr)], axis=2),
        "wqv": chunked(L1_xattn_W_qv),
        "w_ffn0": np.stack([
            chunked(turned(np.concatenate([a(w), a(shared)[None]], axis=0)))
            for w, shared in ((L0_ffn_w_gate, L0_ffn_shared_gate_w), (L0_ffn_w_up, L0_ffn_shared_up_w),
                              (L0_ffn_w_down, L0_ffn_shared_down_w))], axis=2),
        "w_ffn1": np.concatenate([
            chunked(turned(L1_ffn_W1)).reshape(E1, P, DC * F1), chunked(turned(L1_ffn_W2)).reshape(E1, P, FC * D)], axis=2),
        "b2": a(L1_ffn_b2),
    }
    arrays = {k: np.ascontiguousarray(v) for k, v in arrays.items()}
    nc = bacc.Bacc("TRN2", target_bir_lowering=False, num_devices=1)
    args = [nc.dram_tensor(f"in_{k}", v.shape, F32, kind="ExternalInput").ap() for k, v in arrays.items()]
    args.append(nc.dram_tensor("out", (P, NT, D), F32, kind="ExternalOutput").ap())
    perceiver(nc, *args, STAGES)
    r = run_bass_kernel_spmd(nc, [{f"in_{k}": v for k, v in arrays.items()}], core_ids=[0])
    return np.ascontiguousarray(a(r.results[0]["out"]).transpose(1, 0, 2)).reshape(B, S, D)
```
